# Optimizing a Trainium2 kernel written in Bass

```python
import numpy as np
import jax
import jax.numpy as jnp

def _softmax(x, axis=-1):
    return jax.nn.softmax(x, axis=axis)

def _gelu(x):
    return jax.nn.gelu(x, approximate=True)

def _silu(x):
    return jax.nn.silu(x)

def _sigmoid(x):
    return jax.nn.sigmoid(x)

def _layernorm(x, axis=-1, eps=1e-05):
    m = jnp.mean(x, axis=axis, keepdims=True)
    v = jnp.var(x, axis=axis, keepdims=True)
    return (x - m) / jnp.sqrt(v + eps)

def _scatter_add(tgt, idx, src, axis=0):
    return tgt.at[idx].add(src)

def _segment_sum(src, seg, n):
    return jax.ops.segment_sum(src, seg, n)
kernel_name = 'mk_pixart_seq_d2_seqx_r8_31ef20'

def setup_inputs(seed: int=0):
    np.random.seed(seed)
    _w = jnp.asarray

    def _rec_inputs():
        import jax
        import jax.numpy as jnp
        _rk = jax.random.key(seed)
        x = -0.0003929 + 0.9999 * jax.random.normal(jax.random.fold_in(_rk, 1), (16, 128, 128), jnp.float32)
        _lenS = 128 - jax.random.randint(jax.random.fold_in(_rk, 7), (16,), 0, max(1, 128 // 4) + 1, jnp.int32)
        _lenS2 = 120 - jax.random.randint(jax.random.fold_in(_rk, 8), (16,), 0, max(1, 120 // 4) + 1, jnp.int32)
        cond_1024 = 0.00782532 + 1.00527 * jax.random.normal(jax.random.fold_in(_rk, 11), (16, 128), jnp.float32)
        _ctx_1024P = jax.random.normal(jax.random.fold_in(_rk, 12), (16, 16, 128), jnp.float32)
        _ctx_1024c = jax.random.dirichlet(jax.random.fold_in(_rk, 512), 0.3 * jnp.ones((16,), jnp.float32), (16, 120))
        _ctx_1024t = jnp.einsum('bsk,bkd->bsd', _ctx_1024c, _ctx_1024P)
        _ctx_1024t = _ctx_1024t * jax.lax.rsqrt(jnp.mean(jnp.square(_ctx_1024t)) + 1e-12) * 0.953939
        ctx_1024 = -0.000761806 + 0.999296 * (_ctx_1024t + 0.3 * jax.random.normal(jax.random.fold_in(_rk, 612), (16, 120, 128), jnp.float32))
        return (x, cond_1024, ctx_1024)
    x, cond_1024, ctx_1024 = _rec_inputs()

    def _L0_xcond_setup():
        import jax, jax.numpy as jnp
        import numpy as np
        H = 128
        RH = 2 * H
        E = 3
        B, T, P = (8, 256, 64)
        LN_EPS = 1e-05

        def _layer_norm(x, gamma, beta):
            mu = jnp.mean(x, axis=-1, keepdims=True)
            var = jnp.mean(jnp.square(x - mu), axis=-1, keepdims=True)
            return (x - mu) * jax.lax.rsqrt(var + LN_EPS) * gamma + beta
        key = jax.random.key(seed)
        ks = jax.random.split(key, 24)
        s = lambda fan_in: 1.0 / np.sqrt(fan_in)
        inp = {'mix_hidden_states': jax.random.normal(ks[0], (B, T, H), jnp.float32), 'global_anchor': jax.random.normal(ks[1], (B, H), jnp.float32), 'prototype_bank': jax.random.normal(ks[2], (B, P, H), jnp.float32), 'ln_gamma': jnp.ones((H,), jnp.float32), 'ln_beta': jnp.zeros((H,), jnp.float32), 'Wq': jax.random.normal(ks[3], (H, H), jnp.float32) * s(H), 'Wk': jax.random.normal(ks[4], (H, H), jnp.float32) * s(H), 'Wv': jax.random.normal(ks[5], (H, H), jnp.float32) * s(H), 'router_W': jax.random.normal(ks[6], (3 * H, E), jnp.float32) * s(3 * H), 'router_b': jnp.zeros((E,), jnp.float32), 'e_w1': jax.random.normal(ks[7], (E, 3 * H, RH), jnp.float32) * s(3 * H), 'e_b1': jnp.zeros((E, RH), jnp.float32), 'e_w2': jax.random.normal(ks[8], (E, RH, H), jnp.float32) * s(RH), 'e_b2': jnp.zeros((E, H), jnp.float32), 'gate_w1': jax.random.normal(ks[9], (3 * H, H), jnp.float32) * s(3 * H), 'gate_b1': jnp.zeros((H,), jnp.float32), 'gate_w2': jax.random.normal(ks[10], (H, H), jnp.float32) * s(H), 'gate_b2': jnp.zeros((H,), jnp.float32), 'out_w': jax.random.normal(ks[11], (H, H), jnp.float32) * s(H), 'out_b': jnp.zeros((H,), jnp.float32)}
        return inp
    _L0_xcond_all = _L0_xcond_setup()
    _L0_xcond_in = {k: v for k, v in _L0_xcond_all.items() if k in ('ln_gamma', 'ln_beta', 'Wq', 'Wk', 'Wv', 'router_W', 'router_b', 'e_w1', 'e_b1', 'e_w2', 'e_b2', 'gate_w1', 'gate_b1', 'gate_w2', 'gate_b2', 'out_w', 'out_b')}
    del _L0_xcond_all

    def _L1_xcond_setup():
        import jax, jax.numpy as jnp
        import numpy as np
        C = 128
        H = 16
        D = C // H
        WIN = 64
        SHIFT = 32
        TOPK = 16
        HID = 512
        EPS = 1e-06

        def _ln(x):
            x32 = x.astype(jnp.float32)
            m = x32.mean(-1, keepdims=True)
            v = jnp.mean((x32 - m) ** 2, axis=-1, keepdims=True)
            return ((x32 - m) * jax.lax.rsqrt(v + EPS)).astype(x.dtype)

        def _self_attn(h, w_qkv, b_qkv, w_so, b_so):
            B, L, _ = h.shape
            qkv = h @ w_qkv + b_qkv
            qkv = jnp.roll(qkv, -SHIFT, axis=1)
            nw = L // WIN
            qkv = qkv.reshape(B, nw, WIN, 3, H, D)
            q, k, v = (qkv[:, :, :, 0], qkv[:, :, :, 1], qkv[:, :, :, 2])
            scores = jnp.einsum('bnqhd,bnkhd->bnhqk', q, k) / jnp.sqrt(jnp.float32(D)).astype(h.dtype)
            attn = jax.nn.softmax(scores, axis=-1)
            o = jnp.einsum('bnhqk,bnkhd->bnqhd', attn, v).reshape(B, L, C)
            o = jnp.roll(o, SHIFT, axis=1)
            return o @ w_so + b_so

        def _topk_cross_attn(h, ctx, w_q, b_q, w_kv, b_kv, w_co, b_co):
            B, L, _ = h.shape
            Lc = ctx.shape[1]
            q = (h @ w_q + b_q).reshape(B, L, H, D)
            kv = (ctx @ w_kv + b_kv).reshape(B, Lc, 2, H, D)
            k, v = (kv[:, :, 0], kv[:, :, 1])
            scores = jnp.einsum('bqhd,bkhd->bhqk', q, k) / jnp.sqrt(jnp.float32(D)).astype(h.dtype)
            top_s, top_i = jax.lax.top_k(scores, TOPK)
            attn = jax.nn.softmax(top_s, axis=-1)
            v_bh = jnp.transpose(v, (0, 2, 1, 3))
            vg = jnp.take_along_axis(v_bh[:, :, None, :, :], top_i[..., None], axis=3)
            o = jnp.einsum('bhqk,bhqkd->bqhd', attn, vg).reshape(B, L, C)
            return o @ w_co + b_co

        def _swiglu(h, w_m1, b_m1, w_m2, b_m2):
            u = h @ w_m1 + b_m1
            a, b = (u[..., :HID], u[..., HID:])
            return jax.nn.silu(a) * b @ w_m2 + b_m2
        key = jax.random.key(seed)
        ks = jax.random.split(key, 24)
        s = 0.02
        inp = {'x': jax.random.normal(ks[0], (2, 512, C), jnp.float32), 'mod': jax.random.normal(ks[1], (2, C), jnp.float32), 'context': jax.random.normal(ks[2], (2, 128, C), jnp.float32), 'w_ada': jax.random.normal(ks[3], (C, 9 * C), jnp.float32) * s, 'b_ada': jnp.zeros((9 * C,), jnp.float32), 'w_qkv': jax.random.normal(ks[4], (C, 3 * C), jnp.float32) * s, 'b_qkv': jnp.zeros((3 * C,), jnp.float32), 'w_so': jax.random.normal(ks[5], (C, C), jnp.float32) * s, 'b_so': jnp.zeros((C,), jnp.float32), 'w_q': jax.random.normal(ks[6], (C, C), jnp.float32) * s, 'b_q': jnp.zeros((C,), jnp.float32), 'w_kv': jax.random.normal(ks[7], (C, 2 * C), jnp.float32) * s, 'b_kv': jnp.zeros((2 * C,), jnp.float32), 'w_co': jax.random.normal(ks[8], (C, C), jnp.float32) * s, 'b_co': jnp.zeros((C,), jnp.float32), 'w_m1': jax.random.normal(ks[9], (C, 2 * HID), jnp.float32) * s, 'b_m1': jnp.zeros((2 * HID,), jnp.float32), 'w_m2': jax.random.normal(ks[10], (HID, C), jnp.float32) * s, 'b_m2': jnp.zeros((C,), jnp.float32)}
        return inp
    _L1_xcond_all = _L1_xcond_setup()
    _L1_xcond_in = {k: v for k, v in _L1_xcond_all.items() if k in ('w_ada', 'b_ada', 'w_qkv', 'b_qkv', 'w_so', 'b_so', 'w_q', 'b_q', 'w_kv', 'b_kv', 'w_co', 'b_co', 'w_m1', 'b_m1', 'w_m2', 'b_m2')}
    del _L1_xcond_all
    return {'x': x, 'cond_1024': cond_1024, 'ctx_1024': ctx_1024, 'L0_xcond_ln_gamma': _L0_xcond_in['ln_gamma'], 'L0_xcond_ln_beta': _L0_xcond_in['ln_beta'], 'L0_xcond_Wq': _L0_xcond_in['Wq'], 'L0_xcond_Wk': _L0_xcond_in['Wk'], 'L0_xcond_Wv': _L0_xcond_in['Wv'], 'L0_xcond_router_W': _L0_xcond_in['router_W'], 'L0_xcond_router_b': _L0_xcond_in['router_b'], 'L0_xcond_e_w1': _L0_xcond_in['e_w1'], 'L0_xcond_e_b1': _L0_xcond_in['e_b1'], 'L0_xcond_e_w2': _L0_xcond_in['e_w2'], 'L0_xcond_e_b2': _L0_xcond_in['e_b2'], 'L0_xcond_gate_w1': _L0_xcond_in['gate_w1'], 'L0_xcond_gate_b1': _L0_xcond_in['gate_b1'], 'L0_xcond_gate_w2': _L0_xcond_in['gate_w2'], 'L0_xcond_gate_b2': _L0_xcond_in['gate_b2'], 'L0_xcond_out_w': _L0_xcond_in['out_w'], 'L0_xcond_out_b': _L0_xcond_in['out_b'], 'L1_xcond_w_ada': _L1_xcond_in['w_ada'], 'L1_xcond_b_ada': _L1_xcond_in['b_ada'], 'L1_xcond_w_qkv': _L1_xcond_in['w_qkv'], 'L1_xcond_b_qkv': _L1_xcond_in['b_qkv'], 'L1_xcond_w_so': _L1_xcond_in['w_so'], 'L1_xcond_b_so': _L1_xcond_in['b_so'], 'L1_xcond_w_q': _L1_xcond_in['w_q'], 'L1_xcond_b_q': _L1_xcond_in['b_q'], 'L1_xcond_w_kv': _L1_xcond_in['w_kv'], 'L1_xcond_b_kv': _L1_xcond_in['b_kv'], 'L1_xcond_w_co': _L1_xcond_in['w_co'], 'L1_xcond_b_co': _L1_xcond_in['b_co'], 'L1_xcond_w_m1': _L1_xcond_in['w_m1'], 'L1_xcond_b_m1': _L1_xcond_in['b_m1'], 'L1_xcond_w_m2': _L1_xcond_in['w_m2'], 'L1_xcond_b_m2': _L1_xcond_in['b_m2']}

def reference(x, cond_1024, ctx_1024, L0_xcond_ln_gamma, L0_xcond_ln_beta, L0_xcond_Wq, L0_xcond_Wk, L0_xcond_Wv, L0_xcond_router_W, L0_xcond_router_b, L0_xcond_e_w1, L0_xcond_e_b1, L0_xcond_e_w2, L0_xcond_e_b2, L0_xcond_gate_w1, L0_xcond_gate_b1, L0_xcond_gate_w2, L0_xcond_gate_b2, L0_xcond_out_w, L0_xcond_out_b, L1_xcond_w_ada, L1_xcond_b_ada, L1_xcond_w_qkv, L1_xcond_b_qkv, L1_xcond_w_so, L1_xcond_b_so, L1_xcond_w_q, L1_xcond_b_q, L1_xcond_w_kv, L1_xcond_b_kv, L1_xcond_w_co, L1_xcond_b_co, L1_xcond_w_m1, L1_xcond_b_m1, L1_xcond_w_m2, L1_xcond_b_m2):
    import jax
    import jax.numpy as jnp

    def _L0_xcond_ref(mix_hidden_states, global_anchor, prototype_bank, ln_gamma, ln_beta, Wq, Wk, Wv, router_W, router_b, e_w1, e_b1, e_w2, e_b2, gate_w1, gate_b1, gate_w2, gate_b2, out_w, out_b):
        import jax, jax.numpy as jnp
        import numpy as np
        H = 128
        RH = 2 * H
        E = 3
        B, T, P = (8, 256, 64)
        LN_EPS = 1e-05

        def _layer_norm(x, gamma, beta):
            mu = jnp.mean(x, axis=-1, keepdims=True)
            var = jnp.mean(jnp.square(x - mu), axis=-1, keepdims=True)
            return (x - mu) * jax.lax.rsqrt(var + LN_EPS) * gamma + beta
        x = mix_hidden_states
        nx = _layer_norm(x, ln_gamma, ln_beta)
        q = nx @ Wq
        k = prototype_bank @ Wk
        v = prototype_bank @ Wv
        scores = jnp.einsum('bth,bph->btp', q, k) * H ** (-0.5)
        weights = jax.nn.softmax(scores, axis=-1)
        evidence = jnp.einsum('btp,bph->bth', weights, v)
        anchor = jnp.broadcast_to(global_anchor[:, None, :], nx.shape)
        combined = jnp.concatenate([nx, evidence, anchor], axis=-1)
        router_logits = combined @ router_W + router_b
        router_probs = jax.nn.softmax(router_logits, axis=-1)
        h = jax.nn.silu(jnp.einsum('btc,ecr->bter', combined, e_w1) + e_b1)
        expert_out = jnp.einsum('bter,erh->bteh', h, e_w2) + e_b2
        routed = jnp.sum(expert_out * router_probs[..., None], axis=-2)
        g = jax.nn.sigmoid(jax.nn.silu(combined @ gate_w1 + gate_b1) @ gate_w2 + gate_b2)
        refined_delta = g * (routed @ out_w + out_b)
        return x + refined_delta

    def _L1_xcond_ref(x, mod, context, w_ada, b_ada, w_qkv, b_qkv, w_so, b_so, w_q, b_q, w_kv, b_kv, w_co, b_co, w_m1, b_m1, w_m2, b_m2):
        import jax, jax.numpy as jnp
        import numpy as np
        C = 128
        H = 16
        D = C // H
        WIN = 64
        SHIFT = 32
        TOPK = 16
        HID = 512
        EPS = 1e-06

        def _ln(x):
            x32 = x.astype(jnp.float32)
            m = x32.mean(-1, keepdims=True)
            v = jnp.mean((x32 - m) ** 2, axis=-1, keepdims=True)
            return ((x32 - m) * jax.lax.rsqrt(v + EPS)).astype(x.dtype)

        def _self_attn(h, w_qkv, b_qkv, w_so, b_so):
            B, L, _ = h.shape
            qkv = h @ w_qkv + b_qkv
            qkv = jnp.roll(qkv, -SHIFT, axis=1)
            nw = L // WIN
            qkv = qkv.reshape(B, nw, WIN, 3, H, D)
            q, k, v = (qkv[:, :, :, 0], qkv[:, :, :, 1], qkv[:, :, :, 2])
            scores = jnp.einsum('bnqhd,bnkhd->bnhqk', q, k) / jnp.sqrt(jnp.float32(D)).astype(h.dtype)
            attn = jax.nn.softmax(scores, axis=-1)
            o = jnp.einsum('bnhqk,bnkhd->bnqhd', attn, v).reshape(B, L, C)
            o = jnp.roll(o, SHIFT, axis=1)
            return o @ w_so + b_so

        def _topk_cross_attn(h, ctx, w_q, b_q, w_kv, b_kv, w_co, b_co):
            B, L, _ = h.shape
            Lc = ctx.shape[1]
            q = (h @ w_q + b_q).reshape(B, L, H, D)
            kv = (ctx @ w_kv + b_kv).reshape(B, Lc, 2, H, D)
            k, v = (kv[:, :, 0], kv[:, :, 1])
            scores = jnp.einsum('bqhd,bkhd->bhqk', q, k) / jnp.sqrt(jnp.float32(D)).astype(h.dtype)
            top_s, top_i = jax.lax.top_k(scores, TOPK)
            attn = jax.nn.softmax(top_s, axis=-1)
            v_bh = jnp.transpose(v, (0, 2, 1, 3))
            vg = jnp.take_along_axis(v_bh[:, :, None, :, :], top_i[..., None], axis=3)
            o = jnp.einsum('bhqk,bhqkd->bqhd', attn, vg).reshape(B, L, C)
            return o @ w_co + b_co

        def _swiglu(h, w_m1, b_m1, w_m2, b_m2):
            u = h @ w_m1 + b_m1
            a, b = (u[..., :HID], u[..., HID:])
            return jax.nn.silu(a) * b @ w_m2 + b_m2
        m = jax.nn.silu(mod) @ w_ada + b_ada
        sh_msa, sc_msa, g_msa, sh_mca, sc_mca, g_mca, sh_mlp, sc_mlp, g_mlp = [m[:, i * C:(i + 1) * C][:, None, :] for i in range(9)]
        h = _ln(x) * (1 + sc_msa) + sh_msa
        h = _self_attn(h, w_qkv, b_qkv, w_so, b_so)
        x = x + h * g_msa
        h = _ln(x) * (1 + sc_mca) + sh_mca
        h = _topk_cross_attn(h, context, w_q, b_q, w_kv, b_kv, w_co, b_co)
        x = x + h * g_mca
        h = _ln(x) * (1 + sc_mlp) + sh_mlp
        h = _swiglu(h, w_m1, b_m1, w_m2, b_m2)
        x = x + h * g_mlp
        return x
    x = _L0_xcond_ref(x, cond_1024, ctx_1024, L0_xcond_ln_gamma, L0_xcond_ln_beta, L0_xcond_Wq, L0_xcond_Wk, L0_xcond_Wv, L0_xcond_router_W, L0_xcond_router_b, L0_xcond_e_w1, L0_xcond_e_b1, L0_xcond_e_w2, L0_xcond_e_b2, L0_xcond_gate_w1, L0_xcond_gate_b1, L0_xcond_gate_w2, L0_xcond_gate_b2, L0_xcond_out_w, L0_xcond_out_b)
    x = _L1_xcond_ref(x, cond_1024, ctx_1024, L1_xcond_w_ada, L1_xcond_b_ada, L1_xcond_w_qkv, L1_xcond_b_qkv, L1_xcond_w_so, L1_xcond_b_so, L1_xcond_w_q, L1_xcond_b_q, L1_xcond_w_kv, L1_xcond_b_kv, L1_xcond_w_co, L1_xcond_b_co, L1_xcond_w_m1, L1_xcond_b_m1, L1_xcond_w_m2, L1_xcond_b_m2)
    return x

_drawn_inputs = setup_inputs


def setup_inputs(seed=0):
    import zlib

    import numpy as np

    out = dict(_drawn_inputs(seed))
    spreads = {'L0_xcond_ln_gamma': (1.0, 0.2),
     'L0_xcond_ln_beta': (0.0, 0.609),
     'L0_xcond_router_b': (0.0, 0.8),
     'L0_xcond_e_b1': (0.0, 0.376),
     'L0_xcond_e_b2': (0.0, 0.1),
     'L0_xcond_gate_b1': (0.0, 0.8),
     'L0_xcond_gate_b2': (0.0, 0.8),
     'L0_xcond_out_b': (0.0, 0.1),
     'L1_xcond_b_ada': (0.0, 0.576),
     'L1_xcond_b_qkv': (0.0, 0.8),
     'L1_xcond_b_so': (0.0, 0.535),
     'L1_xcond_b_q': (0.0, 0.8),
     'L1_xcond_b_kv': (0.0, 0.8),
     'L1_xcond_b_co': (0.0, 0.543),
     'L1_xcond_b_m1': (0.0, 0.8),
     'L1_xcond_b_m2': (0.0, 1.605)}
    factors = {'L1_xcond_w_qkv': 8.0,
     'L1_xcond_w_so': 8.0,
     'L1_xcond_w_q': 8.0,
     'L1_xcond_w_kv': 8.0,
     'L1_xcond_w_co': 8.0,
     'L1_xcond_w_m1': 8.0,
     'L1_xcond_w_m2': 8.0}
    for name, (base, spread) in spreads.items():
        noise = np.random.default_rng([zlib.crc32(name.encode()), seed]).standard_normal(out[name].shape)
        drawn = base * np.exp(spread * noise) if base else spread * noise
        out[name] = jnp.asarray(drawn.astype(out[name].dtype))
    for name, factor in factors.items():
        out[name] = (out[name] * factor).astype(out[name].dtype)
    return out
```

```python
from contextlib import ExitStack

import concourse.bass as bass
from concourse import mybir


def pixart_layers_kernel(nc: bass.Bass, I, out: bass.AP):
    f32 = mybir.dt.float32
    ALU = mybir.AluOpType
    ACT = mybir.ActivationFunctionType
    AX = mybir.AxisListType

    NB, L, C = I["x"].shape
    LC = I["ctx_1024"].shape[1]
    PAIRS = NB // 2
    TP = 2 * L
    NE, _, RH = I["L0_xcond_e_w1"].shape
    NH = 16
    D = C // NH
    WIN, SHIFT, TOPK = 64, 32, 16
    HID = I["L1_xcond_w_m2"].shape[0]
    NG = C // 32
    EPS0, EPS1 = 1e-5, 1e-6
    SC0, SC1 = float(C) ** -0.5, float(D) ** -0.5
    GONE = -1.0e30

    rows = {}
    n_rows = 0
    for name, n in (("ln_gamma", 1), ("ln_beta", 1), ("e_b1", NE * RH // C), ("gate_b1", 1), ("gate_b2", 1),
                    ("b_ada", 9), ("b_qkv", 3), ("b_so", 1), ("b_q", 1), ("b_kv", 2), ("b_co", 1),
                    ("b_m1", 2 * HID // C), ("b_m2", 1), ("cond", NB), ("e_b2", NE)):
        rows[name] = n_rows
        n_rows += n

    MODS = ["EB0", "EB1", "EB2", "EB3", "EB4", "EB5", "GB", "RL", "SC1", "SH1", "G1", "BG1", "SC2", "SH2",
            "G2", "BG2", "SC3", "SH3", "G3", "BG3"]
    MOD = {m: n for n, m in enumerate(MODS)}
    NM, NF = len(MODS), MOD["G2"]

    ctx = ExitStack()
    with ctx:
        def sb(name, *shape):
            return ctx.enter_context(nc.sbuf_tensor(name, list(shape), f32))

        rowt = sb("rowt", n_rows, C)
        cols = sb("cols", C, n_rows)
        ident = sb("ident", 128, 128)
        Wq0, Wk0, Wv0 = sb("Wq0", C, C), sb("Wk0", C, C), sb("Wv0", C, C)
        rw = sb("rw", C, 3, NE)
        rb = sb("rb", NE, 1)
        ew1 = sb("ew1", C, NE, 3, RH)
        ew2o = sb("ew2o", C, NE * 2, C)
        outw = sb("outw", C, C)
        gw1 = sb("gw1", C, 3, C)
        gw2 = sb("gw2", C, C)
        mixb = sb("mixb", NE + 1, C)
        mixh = sb("mixh", C, C)
        wqkv = sb("wqkv", C, 3, C)
        wso, wq, wkv, wco = sb("wso", C, C), sb("wq", C, C), sb("wkv", C, 2, C), sb("wco", C, C)
        wm1 = sb("wm1", C, 2 * HID)
        wm2 = sb("wm2", C, HID // C, C)
        scond = sb("scond", C, NB)
        modT = sb("modT", C, 9, NB)
        modall = sb("modall", C, PAIRS, NM, 2)
        gb2h = sb("gb2h", C, 1)
        mhalf = sb("mhalf", 128, 2)
        modf = sb("modf", C, NF, 2)
        modb = sb("modb", C, NM - NF, 2)

        x0 = sb("x0", L, 2, C)
        c0 = sb("c0", LC, 2, C)
        st0, mv0, ve0, rs0 = sb("st0", L, 2, 6), sb("mv0", L, 2, 2), sb("ve0", L, 2), sb("rs0", L, 2)
        z0 = sb("z0", L, 2, C)
        nxT = sb("nxT", C, 2, L)
        cT = sb("cT", C, 2, LC)
        q0T = sb("q0T", C, 2, L)
        k0T = sb("k0T", C, 2, LC)
        kcT = sb("kcT", C, 2, LC)
        v0 = sb("v0", LC, 2, C)
        vcA, vcM, vcB = sb("vcA", LC, 2, C), sb("vcM", LC, 2, C), sb("vcB", LC, 2, C)
        m0, nm0, l0, r0 = sb("m0", L, 2), sb("nm0", L, 2), sb("l0", L, 2), sb("r0", L, 2)
        P0 = sb("P0", L, 2, LC)
        P0n = sb("P0n", L, 2, LC)
        P0T = sb("P0T", LC, 2, L)
        evT = sb("evT", C, 2, L)
        rlT = sb("rlT", NE, 2, L)
        rm, re, rx = sb("rm", L, 2), sb("re", L, 2, NE), sb("rx", L, 2, NE)
        rs, rr = sb("rs", L, 2), sb("rr", L, 2)
        pr = sb("pr", L, 2, NE + 1)
        prT = sb("prT", C, 2, L)
        hT = sb("hT", C, NE * 2, 2, L)
        gs = sb("gs", C, 2, L)
        th = sb("th", C, 2, L)
        zb = sb("zb", L, 2, C)
        t0, t1, t2, dl = sb("t0", L, 2, C), sb("t1", L, 2, C), sb("t2", L, 2, C), sb("dl", L, 2, C)
        x1 = sb("x1", L, 2, C)
        st1, mv1, ve1, rs1 = sb("st1", L, 2, 6), sb("mv1", L, 2, 2), sb("ve1", L, 2), sb("rs1", L, 2)
        z1 = sb("z1", L, 2, C)
        h1T = sb("h1T", C, 2, L)
        q1T = sb("q1T", C, 2, L)
        k1T = sb("k1T", C, 2, L)
        kbd1 = sb("kbd1", C, 2, NH, L)
        vbd1 = sb("vbd1", 128, 2 * 2 * NG, 2, 32)
        m1 = sb("m1", L, 2, NH)
        d1 = sb("d1", L, 2, NH, WIN)
        l1, r1 = sb("l1", L, 2, NH), sb("r1", L, 2, NH)
        p1T = sb("p1T", 128, 2, NH // 2, L)
        o1T = sb("o1T", C, 2, L)
        y1T = sb("y1T", C, 2, L)
        xA, xM, xB = sb("xA", L, 2, C), sb("xM", L, 2, C), sb("xB", L, 2, C)
        st2, mv2, ve2, rs2 = sb("st2", L, 2, 6), sb("mv2", L, 2, 2), sb("ve2", L, 2), sb("rs2", L, 2)
        z2 = sb("z2", L, 2, C)
        h2T = sb("h2T", C, 2, L)
        qcT = sb("qcT", C, 2, L)
        kbdc = sb("kbdc", C, 2, NH, LC)
        S = sb("S", L, 2, NH, LC)
        Sb = sb("Sb", L, NH, LC)
        S1 = sb("S1", L, 4, LC)
        top = sb("top", L, 2, NH, TOPK)
        tops = sb("tops", L, NH, TOPK)
        lc, rc = sb("lc", L, NH), sb("rc", L, NH)
        E_ = sb("E_", L, NH, LC)
        P = sb("P", L, 2, NH, LC)
        ew2 = E_[:, 0:7, :].rearrange("p h k -> p (h k)")[:, 0:6 * C].rearrange("p (k n) -> p k n", n=C)
        ew2T = E_[:, 8:15, :].rearrange("p h k -> p (h k)")[:, 0:6 * C].rearrange("p (k n) -> p k n", n=C)
        wada = P[:, 0, 0:10, :].rearrange("p h k -> p (h k)")[:, 0:9 * C].rearrange("p (k n) -> p k n", n=C)
        vbdc = sb("vbdc", LC, 2 * NG, 4, 32)
        pcT = sb("pcT", LC, NH, L)
        ocT = sb("ocT", C, 2, L)
        y2T = sb("y2T", C, 2, L)
        x3 = sb("x3", L, 2, C)
        st3, mv3, ve3, rs3 = sb("st3", L, 2, 6), sb("mv3", L, 2, 2), sb("ve3", L, 2), sb("rs3", L, 2)
        z3 = sb("z3", L, 2, C)
        h3T = sb("h3T", C, 2, L)
        sa = sb("sa", C, HID // C, TP)
        u = sb("u", C, HID // C, TP)
        y3T = sb("y3T", C, 2, L)
        x4 = sb("x4", L, 2, C)

        ps = ctx.enter_context(nc.psum_tensor("ps", [128, 8 * 512], f32))

        def bank(n, parts=128, a=0, b=512):
            return ps[0:parts, 512 * n + a:512 * n + b]

        def two(ap):
            return ap.rearrange("p (b t) -> p b t", b=2)

        def one(name):
            return ctx.enter_context(nc.semaphore(name))

        PER, SEM = {}, {}

        def signals(per, names):
            for n in names.split():
                PER[n] = per
                SEM[n] = ctx.enter_context(nc.semaphore(n))

        signals(32, "x0_in")
        signals(16, "c0_in v_b v_m x_b x_m")
        signals(32, "x4_out")
        signals(16 * NH, "kbd1_in kbdc_in")
        signals(1, "pe_z0 pe_q0 pe_c2 pe_vc pe_S0 pe_P0T pe_ev pe_rl pe_rlt pe_e0 pe_e1 pe_e2 pe_g1 pe_prT pe_g2 "
                   "pe_thT pe_z1 pe_qk1 pe_v1 pe_o1 pe_y1 pe_y1t pe_z2 pe_qc pe_y2 pe_y2t pe_z3 pe_y3 pe_y3t")
        signals(2, "pe_y pe_S1 pe_p1T pe_o2")
        signals(8, "pe_Sc pe_pcT")
        signals(4, "pe_m1")
        signals(1, "nxT_ok cT_ok q0T_ok k0T_ok kcT_ok v0_ok vcA_ok P0T_ok evT_ok rx_ok th_ok prT_ok "
                   "q1T_ok k1T_ok o1T_ok qcT_ok")
        signals(2, "P0_ok rlT_ok gs_ok zb_ok h1T_ok v1_ok E1_ok p1T_ok y1T_ok h2T_ok tops_ok ocT_ok y2T_ok h3T_ok y3T_ok")
        signals(4, "h0_ok h1_ok h2_ok sa_ok")
        signals(8, "S_ok E_ok pcT_ok")
        signals(1, "mv0_ok m0_ok nm0_ok r0_ok rm_ok re_ok rs_ok rr_ok pr_ok dl_ok x1_ok mv1_ok xA_ok mv2_ok vbdc_ok "
                   "x3_ok mv3_ok x4_ok")
        signals(2, "st0_ok st1_ok st2_ok st3_ok z0_ok z1_ok z2_ok z3_ok P0n_ok t0_ok t1_ok t2_ok m1_ok d1_ok l1_ok r1_ok "
                   "lc_ok rc_ok")
        signals(4, "u_ok")
        signals(8, "sel_ok")
        signals(2 * NH, "max1_ok rep1_ok max2_ok rep2_ok")
        signals(1, "ve0_ok ve1_ok ve2_ok ve3_ok rs0_ok rs1_ok rs2_ok rs3_ok modf_ok modb_ok")
        signals(2, "p1_ok tsub_ok")
        signals(8, "sub_ok P_ok")

        id0, id_ok, zero_ok = one("id0"), one("id_ok"), one("zero_ok")

        passed = one("passed")

        def need(eng, what, pair, part=None, alone=False):
            value = PER[what] * pair + (PER[what] if part is None else part)
            if isinstance(value, int) and value <= 0:
                return
            eng.wait_ge(SEM[what], value)
            if alone:
                eng.sem_inc(passed, 1)

        w_rows, w_small, w_big = one("w_rows"), one("w_small"), one("w_big")
        mixb_in = one("mixb_in")
        su_pe, su_act, su_dve = one("su_pe"), one("su_act"), one("su_dve")
        mods_ok = one("mods_ok")

        LOOP = (3, PAIRS)

        def iterations(eng, body):
            body(0, True, False, False)
            body(1, True, True, False)
            body(2, True, True, True)
            with eng.Fori(*LOOP) as i:
                body(i, True, True, True)
            body(PAIRS, False, True, True)
            body(PAIRS + 1, False, False, True)

        PCT_BANK = [4 + t % 3 for t in range(8)]
        M1_BANK = [7, 4, 5, 6]
        SC_BANK = [3, 0, 1, 2]
        N_MODS = NE * 2 + 2 + 12
        N_ZERO = 8
        N_ROW_LOADS, N_SMALL, N_BIG = 15, 11, 7

        def col(name, n=0):
            return cols[:, rows[name] + n:rows[name] + n + 1]

        def diagonal(t, part, parts, off, dims):
            pitch = t[:, :].ap[0][0] if len(t.shape) == 2 else t[:, :, :, :].ap[0][0]
            return bass.AP(t, part * pitch + off, [[pitch, parts]] + dims)

        block = ctx.enter_context(nc.Block())

        @block.sync
        def _(sp):
            def row(name, src):
                n = src.shape[0]
                sp.dma_start(rowt[rows[name]:rows[name] + n, :], src).then_inc(w_rows, 16)

            def vec(name, key):
                row(name, I[key].rearrange("(r c) -> r c", c=C))

            def load(i):
                xs = I["x"][bass.ds(2 * i, 2), :, :].rearrange("b t d -> t b d")
                need(sp, "x1_ok", i - 1)
                need(sp, "pe_z0", i - 1)
                sp.dma_start(x0[0:L - SHIFT, :, :], xs[SHIFT:L, :, :]).then_inc(SEM["x0_in"], 16)
                sp.dma_start(x0[L - SHIFT:L, :, :], xs[0:SHIFT, :, :]).then_inc(SEM["x0_in"], 16)
                cs = I["ctx_1024"][bass.ds(2 * i, 2), :, :].rearrange("b t d -> t b d")
                sp.dma_start(c0[:, :, :], cs).then_inc(SEM["c0_in"], 16)

            vec("ln_gamma", "L0_xcond_ln_gamma")
            vec("ln_beta", "L0_xcond_ln_beta")
            row("e_b1", I["L0_xcond_e_b1"].rearrange("e (r c) -> (e r) c", c=C))
            vec("gate_b1", "L0_xcond_gate_b1")
            vec("gate_b2", "L0_xcond_gate_b2")
            vec("b_ada", "L1_xcond_b_ada")
            vec("b_qkv", "L1_xcond_b_qkv")
            vec("b_so", "L1_xcond_b_so")
            vec("b_q", "L1_xcond_b_q")
            vec("b_kv", "L1_xcond_b_kv")
            vec("b_co", "L1_xcond_b_co")
            vec("b_m1", "L1_xcond_b_m1")
            vec("b_m2", "L1_xcond_b_m2")
            row("cond", I["cond_1024"])
            row("e_b2", I["L0_xcond_e_b2"])
            load(0)

            def body(i, front, topk, back, more=True):
                if front:
                    need(sp, "kcT_ok", i)
                    need(sp, "pe_Sc", i - 1)
                    for h in range(NH):
                        sp.dma_start(kbdc[D * h:D * h + D, :, h, :], kcT[D * h:D * h + D, :, :]) \
                            .then_inc(SEM["kbdc_in"], 16)
                if back:
                    need(sp, "vbdc_ok", i - 2)
                if topk:
                    need(sp, "v_m", i - 1)
                    sp.dma_start(vcB[:, :, :], vcM[:, :, :]).then_inc(SEM["v_b"], 16)
                if front:
                    need(sp, "vcA_ok", i)
                    need(sp, "v_b", i - 1)
                    sp.dma_start(vcM[:, :, :], vcA[:, :, :]).then_inc(SEM["v_m"], 16)
                    if more:
                        load(i + 1)
                    need(sp, "k1T_ok", i)
                    need(sp, "pe_S1", i - 1)
                    for h in range(NH):
                        sp.dma_start(kbd1[D * h:D * h + D, :, h, :], k1T[D * h:D * h + D, :, :]) \
                            .then_inc(SEM["kbd1_in"], 16)
                if back:
                    need(sp, "x3_ok", i - 2)
                if topk:
                    need(sp, "x_m", i - 1)
                    sp.dma_start(xB[:, :, :], xM[:, :, :]).then_inc(SEM["x_b"], 16)
                if front:
                    need(sp, "xA_ok", i)
                    need(sp, "x_b", i - 1)
                    sp.dma_start(xM[:, :, :], xA[:, :, :]).then_inc(SEM["x_m"], 16)
                if back:
                    need(sp, "x4_ok", i - 2)
                    os = out[bass.ds(2 * (i - 2), 2), :, :].rearrange("b t d -> t b d")
                    sp.dma_start(os[SHIFT:L, :, :], x4[0:L - SHIFT, :, :]).then_inc(SEM["x4_out"], 16)
                    sp.dma_start(os[0:SHIFT, :, :], x4[L - SHIFT:L, :, :]).then_inc(SEM["x4_out"], 16)

            body(0, True, False, False)
            body(1, True, True, False)
            body(2, True, True, True)
            with sp.Fori(LOOP[0], PAIRS - 1) as i:
                body(i, True, True, True)
            body(PAIRS - 1, True, True, True, more=False)
            body(PAIRS, False, True, True)
            body(PAIRS + 1, False, False, True)
            need(sp, "x4_out", PAIRS - 1)

        @block.gpsimd
        def _(pool):
            g = nc.gpsimd
            g.memset(ident[:, :], 0.0).then_inc(id0, 1)
            pool.wait_ge(id0, 1)
            g.affine_select(out=ident[:, :], in_=ident[:, :], compare_op=ALU.not_equal, fill=1.0, base=0,
                            pattern=[[-1, 128]], channel_multiplier=1).then_inc(id_ok, 1)
            for dst, src in ((ew2[:, :, :], I["L0_xcond_e_w2"].rearrange("e (k p) n -> p (e k) n", p=C)),
                             (outw[:, :], I["L0_xcond_out_w"]),
                             (gw1[:, :, :], I["L0_xcond_gate_w1"].rearrange("(k p) n -> p k n", p=C)),
                             (gw2[:, :], I["L0_xcond_gate_w2"]),
                             (wada[:, :, :], I["L1_xcond_w_ada"].rearrange("p (k n) -> p k n", n=C)),
                             (wqkv[:, :, :], I["L1_xcond_w_qkv"].rearrange("p (k n) -> p k n", n=C)),
                             (wm1[:, :], I["L1_xcond_w_m1"])):
                pool.dma_start(dst, src).then_inc(w_big, 16)
            g.memset(mhalf[:, :], -0.5).then_inc(zero_ok, 1)
            g.memset(mixh[:, :], 0.0).then_inc(zero_ok, 1)
            g.memset(prT[:, :, :], 0.0).then_inc(zero_ok, 1)
            g.memset(vbd1[:, :, :, :], 0.0).then_inc(zero_ok, 1)
            g.memset(vbdc[:, :, :, :], 0.0).then_inc(zero_ok, 1)
            g.memset(kbdc[:, :, :, :], 0.0).then_inc(zero_ok, 1)
            pool.wait_ge(mods_ok, N_MODS)

            def rstd(n, ve, mv, rs, eps, pair):
                need(pool, f"mv{n}_ok", pair, alone=True)
                g.tensor_scalar(ve[:, :], mv[:, :, 1], eps, None, ALU.add).then_inc(SEM[f"ve{n}_ok"], 1)
                need(pool, f"ve{n}_ok", pair)
                g.tensor_tensor(rs[:, :], ve[:, :], mhalf[0:L, :], ALU.pow).then_inc(SEM[f"rs{n}_ok"], 1)

            def shift(pair, b, c):
                h = 4 * c
                need(pool, "max1_ok", pair, b * NH + h + 4)
                if b == 0:
                    need(pool, "P_ok", pair - 1)
                else:
                    need(pool, "P_ok", pair, 4)
                g.tensor_tensor(E_[:, h:h + 4, :], S[:, b, h:h + 4, :],
                                top[:, b, h:h + 4, 0:1].to_broadcast([L, 4, LC]), ALU.subtract) \
                    .then_inc(SEM["sub_ok"], 1)

            def shift_top(pair, b):
                need(pool, "max2_ok", pair, b * NH + NH)
                if b == 0:
                    need(pool, "lc_ok", pair - 1)
                else:
                    need(pool, "lc_ok", pair, 1)
                g.tensor_tensor(tops[:, :, :], top[:, b, :, :], top[:, b, :, 0:1].to_broadcast([L, NH, TOPK]),
                                ALU.subtract).then_inc(SEM["tsub_ok"], 1)

            def norm_top(pair, b):
                need(pool, "rc_ok", pair, b + 1)
                for c in range(4):
                    h = 4 * c
                    need(pool, "sel_ok", pair, 4 * b + c + 1)
                    need(pool, "pe_pcT", pair - 1, 4 * b + c + 1)
                    g.tensor_tensor(P[:, b, h:h + 4, :], E_[:, h:h + 4, :],
                                    rc[:, h:h + 4, None].to_broadcast([L, 4, LC]), ALU.mult) \
                        .then_inc(SEM["P_ok"], 1)

            def body(i, front, topk, back):
                k, j = i - 1, i - 2
                if front:
                    need(pool, "h2T_ok", i - 1)
                    g.tensor_copy(modf[:, :, :], modall[:, bass.ds(i, 1), 0:NF, :].rearrange("p o m b -> p (o m) b")) \
                        .then_inc(SEM["modf_ok"], 1)
                if back:
                    need(pool, "y3T_ok", j - 1)
                    g.tensor_copy(modb[:, :, :], modall[:, bass.ds(j, 1), NF:NM, :].rearrange("p o m b -> p (o m) b")) \
                        .then_inc(SEM["modb_ok"], 1)
                if front:
                    rstd(0, ve0, mv0, rs0, EPS0, i)
                if topk:
                    for c in range(4):
                        shift(k, 0, c)
                    shift_top(k, 0)
                if front:
                    rstd(1, ve1, mv1, rs1, EPS1, i)
                if back:
                    rstd(3, ve3, mv3, rs3, EPS1, j)
                if topk:
                    norm_top(k, 0)
                if front:
                    for b in range(2):
                        need(pool, "r1_ok", i, b + 1)
                        g.tensor_tensor(d1[:, b, :, :], d1[:, b, :, :], r1[:, b, :, None].to_broadcast([L, NH, WIN]),
                                        ALU.mult).then_inc(SEM["p1_ok"], 1)
                if topk:
                    for c in range(3):
                        shift(k, 1, c)
                if front:
                    rstd(2, ve2, mv2, rs2, EPS1, i)
                if topk:
                    shift(k, 1, 3)
                    shift_top(k, 1)
                    norm_top(k, 1)

            iterations(pool, body)

        @block.vector
        def _(dve):
            v = nc.vector
            v.memset(modall[:, :, :, :], 0.0).then_inc(zero_ok, 1)
            v.memset(kbd1[:, :, :, :], 0.0).then_inc(zero_ok, 1)
            dve.wait_ge(su_pe, 1)
            v.tensor_copy(cols[:, :], bank(0, C, 0, n_rows)).then_inc(su_dve, 1)
            dve.wait_ge(su_pe, 2)
            v.tensor_copy(ew2T[:, 0:4, :], bank(1).rearrange("p (k n) -> p k n", n=C)).then_inc(su_dve, 1)
            v.tensor_copy(ew2T[:, 4:6, :], bank(2, 128, 0, 256).rearrange("p (k n) -> p k n", n=C)).then_inc(su_dve, 1)
            dve.wait_ge(su_pe, 4)
            dve.wait_ge(su_dve, 1)
            dve.wait_ge(zero_ok, N_ZERO)
            pairs = lambda ap: ap.rearrange("p (i b) -> p i b", b=2)

            def put(name, src, *a, parts=C):
                v.tensor_scalar(modall[0:parts, :, MOD[name], :], pairs(src), *a).then_inc(mods_ok, 1)

            for n in range(NE * 2):
                put(f"EB{n}", bank(6, C, NB * n, NB * n + NB), col("e_b1", n), None, ALU.add)
            put("GB", bank(6, C, NB * 6, NB * 7), col("gate_b1"), None, ALU.add)
            dve.wait_ge(w_small, 16 * N_SMALL)
            put("RL", bank(6, NE, NB * 7, NB * 8), rb[:, 0:1], None, ALU.add, parts=NE)
            dve.wait_ge(su_pe, 5)
            v.tensor_tensor(modT[:, :, :], bank(7, C, 0, 9 * NB).rearrange("p (k b) -> p k b", b=NB),
                            cols[:, rows["b_ada"]:rows["b_ada"] + 9, None].to_broadcast([C, 9, NB]), ALU.add) \
                .then_inc(su_dve, 1)
            dve.wait_ge(su_dve, 4)
            for n, b in ((1, "b_so"), (2, "b_co"), (3, "b_m2")):
                t = 3 * (n - 1)
                put(f"SH{n}", modT[:, t, :], 0.0, None, ALU.add)
                put(f"SC{n}", modT[:, t + 1, :], 1.0, None, ALU.add)
                put(f"G{n}", modT[:, t + 2, :], 0.0, None, ALU.add)
                put(f"BG{n}", modT[:, t + 2, :], col(b), None, ALU.mult)

            def stats(n, x, st, mv, pair, ready):
                for b in range(2):
                    if ready:
                        need(dve, ready, pair)
                    v.bn_stats(st[:, b, :], x[:, b, :]).then_inc(SEM[f"st{n}_ok"], 1)
                need(dve, f"st{n}_ok", pair, alone=True)
                for b in range(2):
                    r = v.bn_aggr(mv[:, b, :], st[:, b, :])
                r.then_inc(SEM[f"mv{n}_ok"], 1)

            def normalise(n, x, mv, rs, z, pair):
                need(dve, f"rs{n}_ok", pair)
                for b in range(2):
                    v.tensor_scalar(z[:, b, :], x[:, b, :], mv[:, b, 0:1], rs[:, b:b + 1], ALU.subtract, ALU.mult) \
                        .then_inc(SEM[f"z{n}_ok"], 1)

            def top16(pair, b, c):
                hs = range(4 * c, 4 * c + 4)
                need(dve, "S_ok", pair, 4 * b + c + 1, alone=True)
                for h in hs:
                    v.max(top[:, b, h, 0:8], S[:, b, h, :]).then_inc(SEM["max1_ok"], 1)
                for h in hs:
                    need(dve, "max1_ok", pair, b * NH + h + 1, alone=True)
                    v.match_replace(S1[:, h % 4, :], top[:, b, h, 0:8], S[:, b, h, :], GONE).then_inc(SEM["rep1_ok"], 1)
                for h in hs:
                    need(dve, "rep1_ok", pair, b * NH + h + 1, alone=True)
                    v.max(top[:, b, h, 8:16], S1[:, h % 4, :]).then_inc(SEM["max2_ok"], 1)
                for h in hs:
                    need(dve, "max2_ok", pair, b * NH + h + 1, alone=True)
                    v.match_replace(Sb[:, h, :], top[:, b, h, 8:16], S1[:, h % 4, :], GONE).then_inc(SEM["rep2_ok"], 1)

            def select(pair, b):
                need(dve, "tops_ok", pair, b + 1)
                v.tensor_reduce(lc[:, :], tops[:, :, :], AX.X, ALU.add).then_inc(SEM["lc_ok"], 1)
                need(dve, "lc_ok", pair, b + 1)
                if b == 0:
                    need(dve, "P_ok", pair - 1)
                else:
                    need(dve, "P_ok", pair, 4)
                v.reciprocal(rc[:, :], lc[:, :]).then_inc(SEM["rc_ok"], 1)
                for c in range(4):
                    h = 4 * c
                    need(dve, "rep2_ok", pair, b * NH + h + 4)
                    need(dve, "E_ok", pair, 4 * b + c + 1)
                    v.scalar_tensor_tensor(E_[:, h:h + 4, :], Sb[:, h:h + 4, :], GONE / 2, E_[:, h:h + 4, :],
                                           ALU.is_lt, ALU.mult).then_inc(SEM["sel_ok"], 1)

            def body(i, front, topk, back):
                k, j = i - 1, i - 2
                if back:
                    need(dve, "v_b", j)
                    need(dve, "pe_o2", j - 1)
                    v.tensor_copy(diagonal(vbdc, 0, LC, 0, [[4 * 32, 2 * NG], [32 + D, 4], [1, D]]),
                                  vcB[:, :, :].rearrange("p b (g j d) -> p (b g) j d", j=4, d=D)) \
                        .then_inc(SEM["vbdc_ok"], 1)
                if front:
                    need(dve, "x0_in", i)
                    need(dve, "x1_ok", i - 1)
                    stats(0, x0, st0, mv0, i, None)
                if topk:
                    top16(k, 0, 0)
                if front:
                    normalise(0, x0, mv0, rs0, z0, i)
                if topk:
                    top16(k, 0, 1)
                if front:
                    need(dve, "pe_S0", i)
                    v.tensor_reduce(m0[:, :], bank(1, L, 0, 2 * LC).rearrange("p (b k) -> p b k", b=2), AX.X, ALU.max) \
                        .then_inc(SEM["m0_ok"], 1)
                    need(dve, "m0_ok", i)
                    v.tensor_scalar(nm0[:, :], m0[:, :], -SC0, None, ALU.mult).then_inc(SEM["nm0_ok"], 1)
                    need(dve, "P0_ok", i)
                    v.reciprocal(r0[:, :], l0[:, :]).then_inc(SEM["r0_ok"], 1)
                    need(dve, "r0_ok", i)
                    for b in range(2):
                        v.tensor_scalar(P0n[:, b, :], P0[:, b, :], r0[:, b:b + 1], None, ALU.mult) \
                            .then_inc(SEM["P0n_ok"], 1)
                if topk:
                    top16(k, 0, 2)
                if front:
                    lg = bank(0, L, 0, 2 * NE).rearrange("p (b e) -> p b e", b=2)
                    need(dve, "pe_rlt", i)
                    v.tensor_reduce(rm[:, :], lg, AX.X, ALU.max).then_inc(SEM["rm_ok"], 1)
                    need(dve, "rm_ok", i)
                    v.tensor_tensor(re[:, :, :], lg, rm[:, :, None].to_broadcast([L, 2, NE]), ALU.subtract) \
                        .then_inc(SEM["re_ok"], 1)
                    need(dve, "rx_ok", i)
                    v.tensor_reduce(rs[:, :], rx[:, :, :], AX.X, ALU.add).then_inc(SEM["rs_ok"], 1)
                    need(dve, "rs_ok", i)
                    v.reciprocal(rr[:, :], rs[:, :]).then_inc(SEM["rr_ok"], 1)
                    need(dve, "rr_ok", i)
                    v.memset(pr[:, :, NE:NE + 1], 1.0)
                    v.tensor_tensor(pr[:, :, 0:NE], rx[:, :, :], rr[:, :, None].to_broadcast([L, 2, NE]), ALU.mult) \
                        .then_inc(SEM["pr_ok"], 1)
                if topk:
                    top16(k, 0, 3)
                if front:
                    for n, (t_in, t_out) in enumerate(((zb, t0), (t0, t1), (t1, t2))):
                        for b in range(2):
                            need(dve, "zb_ok" if n == 0 else f"t{n - 1}_ok", i, b + 1)
                            v.scalar_tensor_tensor(t_out[:, b, :], bank(3 * b, L, C * n, C * n + C), pr[:, b, n:n + 1],
                                                   t_in[:, b, :], ALU.mult, ALU.add).then_inc(SEM[f"t{n}_ok"], 1)
                    need(dve, "t2_ok", i)
                    need(dve, "pe_thT", i)
                    v.scalar_tensor_tensor(dl[:, :, :], two(bank(1, L, 0, TP)), 1.0, t2[:, :, :], ALU.add, ALU.mult) \
                        .then_inc(SEM["dl_ok"], 1)
                    need(dve, "dl_ok", i)
                    v.tensor_tensor(x1[:, :, :], dl[:, :, :], x0[:, :, :], ALU.add).then_inc(SEM["x1_ok"], 1)
                    stats(1, x1, st1, mv1, i, "x1_ok")
                if topk:
                    select(k, 0)
                if front:
                    normalise(1, x1, mv1, rs1, z1, i)
                if back:
                    need(dve, "x_b", j)
                    need(dve, "pe_y2t", j)
                    v.tensor_tensor(x3[:, :, :], two(bank(5, L, 0, TP)), xB[:, :, :], ALU.add).then_inc(SEM["x3_ok"], 1)
                    stats(3, x3, st3, mv3, j, "x3_ok")
                if topk:
                    top16(k, 1, 0)
                if back:
                    normalise(3, x3, mv3, rs3, z3, j)
                if topk:
                    top16(k, 1, 1)
                if back:
                    for c in range(HID // C):
                        need(dve, "sa_ok", j, c + 1)
                        v.scalar_tensor_tensor(u[:, c, :], bank(M1_BANK[c], C, TP, 2 * TP), col("b_m1", HID // C + c),
                                               sa[:, c, :], ALU.add, ALU.mult).then_inc(SEM["u_ok"], 1)
                if front:
                    for b in range(2):
                        sc = ps[:, 1024 * (1 - b):1024 * (1 - b) + 1024].rearrange("p (h k) -> p h k", k=WIN)
                        need(dve, "pe_S1", i, b + 1)
                        v.tensor_reduce(m1[:, b, :], sc, AX.X, ALU.max).then_inc(SEM["m1_ok"], 1)
                        need(dve, "m1_ok", i, b + 1)
                        v.tensor_tensor(d1[:, b, :, :], sc, m1[:, b, :, None].to_broadcast([L, NH, WIN]), ALU.subtract) \
                            .then_inc(SEM["d1_ok"], 1)
                if topk:
                    top16(k, 1, 2)
                if front:
                    for b in range(2):
                        need(dve, "E1_ok", i, b + 1)
                        v.tensor_reduce(l1[:, b, :], d1[:, b, :, :], AX.X, ALU.add).then_inc(SEM["l1_ok"], 1)
                        need(dve, "l1_ok", i, b + 1)
                        v.reciprocal(r1[:, b, :], l1[:, b, :]).then_inc(SEM["r1_ok"], 1)
                if topk:
                    top16(k, 1, 3)
                if back:
                    need(dve, "pe_y3t", j)
                    need(dve, "x4_out", j - 1)
                    v.tensor_tensor(x4[:, :, :], two(bank(4, L, 0, TP)), x3[:, :, :], ALU.add).then_inc(SEM["x4_ok"], 1)
                if front:
                    need(dve, "pe_y1t", i)
                    need(dve, "x_m", i - 1)
                    v.tensor_tensor(xA[:, :, :], two(bank(0, L, 0, TP)), x1[:, :, :], ALU.add).then_inc(SEM["xA_ok"], 1)
                    stats(2, xA, st2, mv2, i, "xA_ok")
                    normalise(2, xA, mv2, rs2, z2, i)
                if topk:
                    select(k, 1)

            iterations(dve, body)

        @block.scalar
        def _(act):
            a = nc.scalar
            for dst, src in ((rb[:, 0:1], I["L0_xcond_router_b"].rearrange("(p o) -> p o", o=1)),
                             (Wq0[:, :], I["L0_xcond_Wq"]), (Wk0[:, :], I["L0_xcond_Wk"]), (Wv0[:, :], I["L0_xcond_Wv"]),
                             (rw[:, :, :], I["L0_xcond_router_W"].rearrange("(k p) n -> p k n", p=C)),
                             (wkv[:, :, :], I["L1_xcond_w_kv"].rearrange("p (k n) -> p k n", n=C)),
                             (ew1[:, :, :, :], I["L0_xcond_e_w1"].rearrange("e (k p) n -> p e k n", p=C)),
                             (wso[:, :], I["L1_xcond_w_so"]), (wq[:, :], I["L1_xcond_w_q"]), (wco[:, :], I["L1_xcond_w_co"]),
                             (wm2[:, :, :], I["L1_xcond_w_m2"].rearrange("(k p) n -> p k n", p=C))):
                act.dma_start(dst, src).then_inc(w_small, 16)
            act.dma_start(mixb[NE:NE + 1, :], I["L0_xcond_out_b"].rearrange("(o c) -> o c", o=1)).then_inc(mixb_in, 16)
            act.wait_ge(su_dve, 1)
            a.activation(scond[:, :], cols[:, rows["cond"]:rows["cond"] + NB], ACT.Silu).then_inc(su_act, 1)
            a.mul(gb2h[:, :], col("gate_b2"), 0.5).then_inc(su_act, 1)
            act.wait_ge(su_pe, 3)
            a.mul(ew2o[:, 0:4, :], bank(3).rearrange("p (k n) -> p k n", n=C), 0.5).then_inc(su_act, 1)
            a.mul(ew2o[:, 4:6, :], bank(4, 128, 0, 256).rearrange("p (k n) -> p k n", n=C), 0.5).then_inc(su_act, 1)
            a.copy(mixb[0:NE, :], bank(5, NE, 0, C)).then_inc(su_act, 1)
            act.wait_ge(mixb_in, 16)
            act.wait_ge(su_act, 5)
            act.wait_ge(zero_ok, N_ZERO)
            a.mul(mixh[0:NE + 1, :], mixb[:, :], 0.5).then_inc(su_act, 1)

            def f(name, b):
                return modf[:, MOD[name], b:b + 1]

            def g(name, b):
                return modb[:, MOD[name] - NF, b:b + 1]

            def half(n, b, w=C):
                return bank(n, C, w * b, w * b + w)

            def modulated(n, hT, src, m, pair):
                for b in range(2):
                    a.activation(hT[:, b, :], half(src, b), ACT.Identity, scale=m(f"SC{n}", b), bias=m(f"SH{n}", b)) \
                        .then_inc(SEM[f"h{n}T_ok"], 1)

            def gated(n, yT, src, m, pair):
                for b in range(2):
                    a.activation(yT[:, b, :], half(src, b), ACT.Identity, scale=m(f"G{n}", b), bias=m(f"BG{n}", b)) \
                        .then_inc(SEM[f"y{n}T_ok"], 1)

            def pcT_copy(j, t):
                b, c = t // 4, t % 4
                need(act, "pe_pcT", j, t + 1)
                if b == 0:
                    need(act, "pe_o2", j - 1)
                else:
                    need(act, "pe_o2", j, 1)
                a.copy(pcT[:, 4 * c:4 * c + 4, :], bank(PCT_BANK[t], LC).rearrange("p (h t) -> p h t", h=4)) \
                    .then_inc(SEM["pcT_ok"], 1)

            def exps(k, b):
                for c in range(4):
                    need(act, "sub_ok", k, 4 * b + c + 1)
                    a.activation(E_[:, 4 * c:4 * c + 4, :], E_[:, 4 * c:4 * c + 4, :], ACT.Exp).then_inc(SEM["E_ok"], 1)
                need(act, "tsub_ok", k, b + 1)
                a.activation(tops[:, :, :], tops[:, :, :], ACT.Exp).then_inc(SEM["tops_ok"], 1)

            def body(i, front, topk, back):
                k, j = i - 1, i - 2
                if front:
                    need(act, "pe_z0", i)
                    a.activation(nxT[:, :, :], two(bank(0, C, 0, TP)), ACT.Identity, scale=col("ln_gamma"),
                                 bias=col("ln_beta")).then_inc(SEM["nxT_ok"], 1)
                    a.copy(cT[:, :, :], two(bank(0, C, TP, TP + 2 * LC))).then_inc(SEM["cT_ok"], 1)
                if back:
                    for t in range(3):
                        pcT_copy(j, t)
                if front:
                    need(act, "pe_q0", i)
                    a.copy(q0T[:, :, :], two(bank(1, C, 0, TP))).then_inc(SEM["q0T_ok"], 1)
                    a.copy(k0T[:, :, :], two(bank(1, C, TP, TP + 2 * LC))).then_inc(SEM["k0T_ok"], 1)
                    need(act, "pe_c2", i)
                    need(act, "kbdc_in", i - 1)
                    a.activation(kcT[:, :, :], two(bank(2, C, 0, 2 * LC)), ACT.Identity, bias=col("b_kv", 0)) \
                        .then_inc(SEM["kcT_ok"], 1)
                    a.copy(v0[:, :, :], two(bank(2, LC, 2 * LC, 2 * LC + TP))).then_inc(SEM["v0_ok"], 1)
                    need(act, "pe_vc", i)
                    need(act, "v_m", i - 1)
                    a.copy(vcA[:, :, :], two(bank(3, LC, 0, TP))).then_inc(SEM["vcA_ok"], 1)
                if back:
                    pcT_copy(j, 3)
                if front:
                    need(act, "nm0_ok", i)
                    for b in range(2):
                        a.activation(P0[:, b, :], bank(1, L, LC * b, LC * b + LC), ACT.Exp, scale=SC0,
                                     bias=nm0[:, b:b + 1], accum_out=l0[:, b:b + 1]).then_inc(SEM["P0_ok"], 1)
                if back:
                    for t in range(4, 6):
                        pcT_copy(j, t)
                if front:
                    need(act, "pe_P0T", i)
                    a.copy(P0T[:, :, :], two(bank(0, LC, 0, TP))).then_inc(SEM["P0T_ok"], 1)
                if back:
                    for t in range(6, 8):
                        pcT_copy(j, t)
                if front:
                    need(act, "pe_ev", i)
                    a.copy(evT[:, :, :], two(bank(2, C, 0, TP))).then_inc(SEM["evT_ok"], 1)
                if back:
                    need(act, "pe_o2", j)
                    for b in range(2):
                        a.activation(ocT[:, b, :], half(7, b), ACT.Identity, bias=col("b_kv", 1)) \
                            .then_inc(SEM["ocT_ok"], 1)
                if front:
                    need(act, "modf_ok", i)
                    need(act, "pe_rl", i)
                    for b in range(2):
                        a.activation(rlT[:, b, :], bank(3, NE, L * b, L * b + L), ACT.Identity,
                                     bias=modf[0:NE, MOD["RL"], b:b + 1]).then_inc(SEM["rlT_ok"], 1)
                    need(act, "re_ok", i)
                    a.activation(rx[:, :, :], re[:, :, :], ACT.Exp).then_inc(SEM["rx_ok"], 1)
                if topk:
                    exps(k, 0)
                if front:
                    for e in range(NE):
                        need(act, f"pe_e{e}", i)
                        for c in range(2):
                            for b in range(2):
                                a.activation(hT[:, 2 * e + c, b, :], bank(1 + e, C, TP * c + L * b, TP * c + L * b + L),
                                             ACT.Silu, bias=f(f"EB{2 * e + c}", b)).then_inc(SEM[f"h{e}_ok"], 1)
                    need(act, "pe_g1", i)
                    for b in range(2):
                        a.activation(gs[:, b, :], half(0, b), ACT.Silu, bias=f("GB", b)).then_inc(SEM["gs_ok"], 1)
                if back:
                    need(act, "modb_ok", j)
                    need(act, "pe_y2", j)
                    gated(2, y2T, 4, g, j)
                if front:
                    need(act, "pe_g2", i)
                    a.activation(th[:, :, :], two(bank(2, C, 0, TP)), ACT.Tanh, scale=0.5, bias=gb2h[:, 0:1]) \
                        .then_inc(SEM["th_ok"], 1)
                    need(act, "pe_prT", i)
                    a.copy(prT[0:NE + 1, :, :], two(bank(1, NE + 1, 0, TP))).then_inc(SEM["prT_ok"], 1)
                    for b in range(2):
                        need(act, "pe_y", i, b + 1)
                        a.copy(zb[:, b, :], bank(3 * b, L, NE * C, NE * C + C)).then_inc(SEM["zb_ok"], 1)
                    need(act, "pe_z1", i)
                    modulated(1, h1T, 2, f, i)
                if back:
                    need(act, "pe_z3", j)
                    modulated(3, h3T, 6, g, j)
                if front:
                    need(act, "pe_qk1", i)
                    a.activation(q1T[:, :, :], two(bank(0, C, 0, TP)), ACT.Identity, bias=col("b_qkv", 0)) \
                        .then_inc(SEM["q1T_ok"], 1)
                    need(act, "kbd1_in", i - 1)
                    a.activation(k1T[:, :, :], two(bank(0, C, TP, 2 * TP)), ACT.Identity, bias=col("b_qkv", 1)) \
                        .then_inc(SEM["k1T_ok"], 1)
                    need(act, "pe_v1", i)
                    need(act, "pe_o1", i - 1)
                    for h in range(2):
                        a.copy(diagonal(vbd1, 64 * h, 64, D * h, [[64, 4 * NG], [32 + 2 * D, 2], [1, D]]),
                               bank(1)[64 * h:64 * h + 64, :].rearrange("p (x q c) -> p x q c", q=2, c=2 * D)
                               [:, :, :, D * h:D * h + D]).then_inc(SEM["v1_ok"], 1)
                if back:
                    for c in range(HID // C):
                        need(act, "pe_m1", j, c + 1)
                        a.activation(sa[:, c, :], bank(M1_BANK[c], C, 0, TP), ACT.Silu, bias=col("b_m1", c)) \
                            .then_inc(SEM["sa_ok"], 1)
                if front:
                    for b in range(2):
                        need(act, "d1_ok", i, b + 1)
                        a.activation(d1[:, b, :, :], d1[:, b, :, :], ACT.Exp, scale=SC1).then_inc(SEM["E1_ok"], 1)
                    for b in range(2):
                        need(act, "pe_p1T", i, b + 1)
                        a.copy(p1T[:, b, :, :], ps[:, 1024 * (1 - b):1024 * (1 - b) + 1024]
                               .rearrange("p (k t) -> p k t", t=L)).then_inc(SEM["p1T_ok"], 1)
                if back:
                    need(act, "pe_y3", j)
                    gated(3, y3T, 7, g, j)
                if front:
                    need(act, "pe_o1", i)
                    a.activation(o1T[:, :, :], two(bank(2, C, 0, TP)), ACT.Identity, bias=col("b_qkv", 2)) \
                        .then_inc(SEM["o1T_ok"], 1)
                    need(act, "pe_y1", i)
                    gated(1, y1T, 3, f, i)
                    need(act, "pe_z2", i)
                    modulated(2, h2T, 1, f, i)
                    need(act, "pe_qc", i)
                    a.activation(qcT[:, :, :], two(bank(2, C, 0, TP)), ACT.Identity, bias=col("b_q")) \
                        .then_inc(SEM["qcT_ok"], 1)
                    for t in range(8):
                        b, c = t // 4, t % 4
                        need(act, "pe_Sc", i, t + 1)
                        need(act, "rep1_ok", i - 1, b * NH + 4 * c + 4)
                        need(act, "sub_ok", i - 1, t + 1)
                        a.mul(S[:, b, 4 * c:4 * c + 4, :], bank(SC_BANK[c], L, 0, 4 * LC)
                              .rearrange("p (h k) -> p h k", k=LC), SC1).then_inc(SEM["S_ok"], 1)
                if topk:
                    exps(k, 1)

            iterations(act, body)

        @block.tensor
        def _(pe):
            t_ = nc.tensor

            def mm(o, l, r, start=True, stop=True):
                return t_.matmul(o, l, r, start=start, stop=stop)

            def back_to(o, x):
                return t_.transpose(o, x, ident[0:x.shape[0], 0:x.shape[0]])

            pe.wait_ge(id_ok, 1)
            pe.wait_ge(w_rows, 16 * N_ROW_LOADS)
            back_to(bank(0, C, 0, n_rows), rowt[:, :]).then_inc(su_pe, 1)
            pe.wait_ge(w_big, 16 * N_BIG)
            for n in range(NE * 2):
                r = back_to(bank(1 + n // 4, C, C * (n % 4), C * (n % 4) + C), ew2[:, n, :])
            r.then_inc(su_pe, 1)
            pe.wait_ge(su_dve, 3)
            for n in range(NE * 2):
                mm(bank(3 + n // 4, C, C * (n % 4), C * (n % 4) + C), ew2T[:, n, :], outw[:, :])
            mm(bank(5, NE, 0, C), cols[:, rows["e_b2"]:rows["e_b2"] + NE], outw[:, :]).then_inc(su_pe, 1)
            pe.wait_ge(w_small, 16 * N_SMALL)
            cond = cols[:, rows["cond"]:rows["cond"] + NB]
            for n in range(NE * 2):
                mm(bank(6, C, NB * n, NB * n + NB), ew1[:, n // 2, 2, C * (n % 2):C * (n % 2) + C], cond)
            mm(bank(6, C, NB * 6, NB * 7), gw1[:, 2, :], cond)
            mm(bank(6, NE, NB * 7, NB * 8), rw[:, 2, :], cond).then_inc(su_pe, 1)
            pe.wait_ge(su_act, 1)
            for n in range(9):
                r = mm(bank(7, C, NB * n, NB * n + NB), wada[:, n, :], scond[:, :])
            r.then_inc(su_pe, 1)
            pe.wait_ge(mods_ok, N_MODS)
            pe.wait_ge(su_act, 6)
            pe.wait_ge(zero_ok, N_ZERO)

            def half(n, b, parts=C, w=L, off=0):
                return bank(n, parts, off + w * b, off + w * b + w)

            def flat(x):
                return x.rearrange("p b t -> p (b t)")

            def to_F(name, n, z, pair, free, part=None):
                need(pe, free, pair, part)
                for b in range(2):
                    need(pe, f"z{name}_ok", pair, b + 1)
                    r = back_to(half(n, b), z[:, b, :])
                r.then_inc(SEM[f"pe_z{name}"], 1)

            def to_T(sem, n, y, ready, pair):
                for b in range(2):
                    need(pe, ready, pair, b + 1)
                    r = back_to(half(n, b, L, C), y[:, b, :])
                r.then_inc(SEM[sem], 1)

            def probs_T(j, ts):
                for t in ts:
                    b, c = t // 4, t % 4
                    if t == 0:
                        need(pe, "x4_ok", j - 1)
                    elif t < 3:
                        need(pe, "u_ok", j - 1, t + 2)
                    else:
                        need(pe, "pcT_ok", j, t - 2)
                    need(pe, "P_ok", j, t + 1)
                    for n in range(4):
                        r = back_to(bank(PCT_BANK[t], LC, L * n, L * n + L), P[:, b, 4 * c + n, :])
                    r.then_inc(SEM["pe_pcT"], 1)

            def cross_values(j, b):
                if b == 0:
                    need(pe, "vbdc_ok", j)
                    need(pe, "y3T_ok", j - 1)
                need(pe, "pcT_ok", j, 4 * b + 4)
                for n in range(4):
                    for gq in range(NG):
                        r = mm(ps[32 * gq:32 * gq + 32, 512 * 7 + L * b:512 * 7 + L * b + L],
                               vbdc[:, b * NG + gq, n, :], pcT[:, 4 * gq + n, :], n == 0, n == 3)
                r.then_inc(SEM["pe_o2"], 1)

            def body(i, front, topk, back):
                j = i - 2
                if front:
                    need(pe, "S_ok", i - 1, 6)
                    need(pe, "c0_in", i)
                    for b in range(2):
                        need(pe, "z0_ok", i, b + 1)
                        back_to(half(0, b), z0[:, b, :])
                    for b in range(2):
                        r = back_to(half(0, b, C, LC, TP), c0[:, b, :])
                    r.then_inc(SEM["pe_z0"], 1)
                if back:
                    probs_T(j, range(3))
                if front:
                    need(pe, "S_ok", i - 1, 7)
                    need(pe, "nxT_ok", i)
                    mm(bank(1, C, 0, TP), Wq0[:, :], flat(nxT))
                    need(pe, "cT_ok", i)
                    mm(bank(1, C, TP, TP + 2 * LC), Wk0[:, :], flat(cT)).then_inc(SEM["pe_q0"], 1)
                    need(pe, "S_ok", i - 1, 8)
                    mm(bank(2, C, 0, 2 * LC), wkv[:, 0, :], flat(cT))
                    for b in range(2):
                        r = mm(half(2, b, LC, C, 2 * LC), cT[:, b, :], Wv0[:, :])
                    r.then_inc(SEM["pe_c2"], 1)
                    need(pe, "S_ok", i - 1, 5)
                    for b in range(2):
                        r = mm(half(3, b, LC, C), cT[:, b, :], wkv[:, 1, :])
                    r.then_inc(SEM["pe_vc"], 1)
                if back:
                    probs_T(j, range(3, 4))
                if front:
                    need(pe, "k0T_ok", i)
                    for b in range(2):
                        r = mm(half(1, b, L, LC), q0T[:, b, :], k0T[:, b, :])
                    r.then_inc(SEM["pe_S0"], 1)
                if back:
                    probs_T(j, range(4, 6))
                    cross_values(j, 0)
                if front:
                    for b in range(2):
                        need(pe, "P0n_ok", i, b + 1)
                        r = back_to(half(0, b, LC), P0n[:, b, :])
                    r.then_inc(SEM["pe_P0T"], 1)
                if back:
                    probs_T(j, range(6, 8))
                if front:
                    need(pe, "v0_ok", i)
                    need(pe, "P0T_ok", i)
                    for b in range(2):
                        r = mm(half(2, b), v0[:, b, :], P0T[:, b, :])
                    r.then_inc(SEM["pe_ev"], 1)
                if back:
                    cross_values(j, 1)
                if front:
                    need(pe, "vcA_ok", i)
                    mm(bank(3, NE, 0, TP), rw[:, 0, :], flat(nxT), True, False)
                    need(pe, "evT_ok", i)
                    mm(bank(3, NE, 0, TP), rw[:, 1, :], flat(evT), False, True).then_inc(SEM["pe_rl"], 1)
                    for b in range(2):
                        need(pe, "rlT_ok", i, b + 1, alone=True)
                        r = back_to(half(0, b, L, NE), rlT[:, b, :])
                    r.then_inc(SEM["pe_rlt"], 1)
                    for e in range(NE):
                        if e == 0:
                            need(pe, "P0_ok", i)
                        for c in range(2):
                            for s, x in enumerate((nxT, evT)):
                                r = mm(bank(1 + e, C, TP * c, TP * c + TP), ew1[:, e, s, C * c:C * c + C], flat(x),
                                       s == 0, s == 1)
                        r.then_inc(SEM[f"pe_e{e}"], 1)
                    need(pe, "re_ok", i)
                    for s, x in enumerate((nxT, evT)):
                        r = mm(bank(0, C, 0, TP), gw1[:, s, :], flat(x), s == 0, s == 1)
                    r.then_inc(SEM["pe_g1"], 1)
                if back:
                    need(pe, "ocT_ok", j)
                    need(pe, "pcT_ok", j, 7)
                    mm(bank(4, C, 0, TP), wco[:, :], flat(ocT)).then_inc(SEM["pe_y2"], 1)
                if front:
                    need(pe, "gs_ok", i)
                    need(pe, "h1_ok", i)
                    mm(bank(2, C, 0, TP), gw2[:, :], flat(gs)).then_inc(SEM["pe_g2"], 1)
                    need(pe, "pr_ok", i)
                    for b in range(2):
                        r = back_to(half(1, b, NE + 1), pr[:, b, :])
                    r.then_inc(SEM["pe_prT"], 1)
                    need(pe, "h2_ok", i)
                    need(pe, "prT_ok", i)
                    for b in range(2):
                        for e in range(NE):
                            for c in range(2):
                                mm(bank(3 * b, L, C * e, C * e + C), hT[:, 2 * e + c, b, :], ew2o[:, 2 * e + c, :],
                                   c == 0, c == 1)
                        mm(bank(3 * b, L, C * NE, C * NE + C), prT[:, b, :], mixh[:, :]).then_inc(SEM["pe_y"], 1)
                if back:
                    to_T("pe_y2t", 5, y2T, "y2T_ok", j)
                if front:
                    need(pe, "th_ok", i)
                    for b in range(2):
                        r = back_to(half(1, b, L, C), th[:, b, :])
                    r.then_inc(SEM["pe_thT"], 1)
                    to_F("1", 2, z1, i, "th_ok")
                if back:
                    to_F("3", 6, z3, j, "pcT_ok", 6)
                if front:
                    need(pe, "t2_ok", i, 1)
                    need(pe, "h1T_ok", i)
                    mm(bank(0, C, 0, TP), wqkv[:, 0, :], flat(h1T))
                    mm(bank(0, C, TP, 2 * TP), wqkv[:, 1, :], flat(h1T)).then_inc(SEM["pe_qk1"], 1)
                    need(pe, "dl_ok", i)
                    for b in range(2):
                        for w in range(2):
                            for h in range(2):
                                r = mm(ps[64 * h:64 * h + 64, 512 + C * (2 * b + w):512 + C * (2 * b + w) + C],
                                       h1T[:, b, WIN * w:WIN * w + WIN], wqkv[:, 2, :])
                    r.then_inc(SEM["pe_v1"], 1)
                if back:
                    need(pe, "h3T_ok", j)
                    for c in range(HID // C):
                        n = M1_BANK[c]
                        if n == 4:
                            need(pe, "y2T_ok", j)
                        elif n == 5:
                            need(pe, "x3_ok", j)
                        mm(bank(n, C, 0, TP), wm1[:, C * c:C * c + C], flat(h3T))
                        mm(bank(n, C, TP, 2 * TP), wm1[:, HID + C * c:HID + C * c + C], flat(h3T)) \
                            .then_inc(SEM["pe_m1"], 1)
                if front:
                    need(pe, "q1T_ok", i)
                    need(pe, "kbd1_in", i)
                    for b in range(2):
                        if b == 0:
                            need(pe, "t2_ok", i, 2)
                        else:
                            need(pe, "k1T_ok", i)
                            need(pe, "v1_ok", i)
                        for q in range(2):
                            for w in range(2):
                                n = 2 * (1 - b) + q
                                r = mm(ps[64 * w:64 * w + 64, 512 * n:512 * n + 512],
                                       q1T[:, b, WIN * w:WIN * w + WIN], kbd1[:, b, 8 * q:8 * q + 8, WIN * w:WIN * w + WIN])
                        r.then_inc(SEM["pe_S1"], 1)
                    for b in range(2):
                        need(pe, "d1_ok", i, b + 1)
                        need(pe, "p1_ok", i, b + 1)
                        for n in range(NH // 2):
                            o = 1024 * (1 - b) + L * n
                            r = back_to(ps[:, o:o + L], d1[:, b, 2 * n:2 * n + 2, :].rearrange("p h k -> p (h k)"))
                        r.then_inc(SEM["pe_p1T"], 1)
                if back:
                    need(pe, "u_ok", j)
                    for c in range(HID // C):
                        r = mm(bank(7, C, 0, TP), wm2[:, c, :], u[:, c, :], c == 0, c == HID // C - 1)
                    r.then_inc(SEM["pe_y3"], 1)
                    to_T("pe_y3t", 4, y3T, "y3T_ok", j)
                if front:
                    need(pe, "v1_ok", i)
                    need(pe, "p1T_ok", i)
                    for b in range(2):
                        for w in range(2):
                            for q in range(2):
                                for gq in range(NG):
                                    o = 1024 + L * b + WIN * w
                                    r = mm(ps[32 * gq:32 * gq + 32, o:o + WIN], vbd1[:, (2 * b + w) * NG + gq, q, :],
                                           p1T[:, b, 2 * gq + q, WIN * w:WIN * w + WIN], q == 0, q == 1)
                    r.then_inc(SEM["pe_o1"], 1)
                    need(pe, "o1T_ok", i)
                    mm(bank(3, C, 0, TP), wso[:, :], flat(o1T)).then_inc(SEM["pe_y1"], 1)
                    to_T("pe_y1t", 0, y1T, "y1T_ok", i)
                    to_F("2", 1, z2, i, "p1T_ok")
                    need(pe, "h2T_ok", i)
                    mm(bank(2, C, 0, TP), wq[:, :], flat(h2T)).then_inc(SEM["pe_qc"], 1)
                    need(pe, "kbdc_in", i)
                    need(pe, "qcT_ok", i)
                    for t in range(8):
                        b, c = t // 4, t % 4
                        if b:
                            need(pe, "S_ok", i, c + 1)
                        mm(bank(SC_BANK[c], L, 0, 4 * LC), qcT[:, b, :], kbdc[:, b, 4 * c:4 * c + 4, :]
                           .rearrange("p h k -> p (h k)")).then_inc(SEM["pe_Sc"], 1)

            iterations(pe, body)


def kernel(**inputs):
    import numpy as _np
    import concourse.bacc as _bacc
    from concourse import mybir as _mybir
    from concourse.bass_utils import run_bass_kernel_spmd as _run

    nc = _bacc.Bacc("TRN2", target_bir_lowering=False, num_devices=1)
    arrays, aps = {}, {}
    for name, value in inputs.items():
        a = _np.ascontiguousarray(value)
        arrays[f"in_{name}"] = a
        aps[name] = nc.dram_tensor(f"in_{name}", a.shape, _mybir.dt.from_np(a.dtype), kind="ExternalInput").ap()
    shape = inputs["x"].shape
    out = nc.dram_tensor("out_0", shape, _mybir.dt.float32, kind="ExternalOutput").ap()
    pixart_layers_kernel(nc, aps, out)
    r = _run(nc, [arrays], core_ids=[0])
    return r.results[0]["out_0"]
```

```python
from contextlib import ExitStack

import concourse.bass as bass
from concourse import mybir


def pixart_layers_kernel(nc: bass.Bass, I, out: bass.AP):
    f32 = mybir.dt.float32
    ALU = mybir.AluOpType
    ACT = mybir.ActivationFunctionType
    AX = mybir.AxisListType

    NB, L, C = I["x"].shape
    LC = I["ctx_1024"].shape[1]
    PAIRS = NB // 2
    TP = 2 * L
    NE, _, RH = I["L0_xcond_e_w1"].shape
    NH = 16
    D = C // NH
    WIN, SHIFT, TOPK = 64, 32, 16
    HID = I["L1_xcond_w_m2"].shape[0]
    NG = C // 32
    EPS0, EPS1 = 1e-5, 1e-6
    SC0, SC1 = float(C) ** -0.5, float(D) ** -0.5
    GONE = -1.0e30

    rows = {}
    n_rows = 0
    for name, n in (("ln_gamma", 1), ("ln_beta", 1), ("e_b1", NE * RH // C), ("gate_b1", 1), ("gate_b2", 1),
                    ("b_ada", 9), ("b_qkv", 3), ("b_so", 1), ("b_q", 1), ("b_kv", 2), ("b_co", 1),
                    ("b_m1", 2 * HID // C), ("b_m2", 1), ("cond", NB), ("e_b2", NE)):
        rows[name] = n_rows
        n_rows += n

    MODS = ["EB0", "EB1", "EB2", "EB3", "EB4", "EB5", "GB", "RL", "SC1", "SH1", "G1", "BG1", "SC2", "SH2",
            "G2", "BG2", "SC3", "SH3", "G3", "BG3"]
    MOD = {m: n for n, m in enumerate(MODS)}
    NM, NW, NBK = len(MODS), MOD["G1"], MOD["G2"]

    ctx = ExitStack()
    with ctx:
        def sb(name, *shape):
            return ctx.enter_context(nc.sbuf_tensor(name, list(shape), f32))

        rowt = sb("rowt", n_rows, C)
        cols = sb("cols", C, n_rows)
        ident = sb("ident", 128, 128)
        Wq0, Wk0, Wv0 = sb("Wq0", C, C), sb("Wk0", C, C), sb("Wv0", C, C)
        rw = sb("rw", C, 3, NE)
        rb = sb("rb", NE, 1)
        ew1 = sb("ew1", C, NE, 3, RH)
        ew2o = sb("ew2o", C, NE * 2, C)
        outw = sb("outw", C, C)
        gw1 = sb("gw1", C, 3, C)
        gw2 = sb("gw2", C, C)
        mixb = sb("mixb", NE + 1, C)
        mixh = sb("mixh", C, C)
        wqkv = sb("wqkv", C, 3, C)
        wso, wq, wkv, wco = sb("wso", C, C), sb("wq", C, C), sb("wkv", C, 2, C), sb("wco", C, C)
        wm1 = sb("wm1", C, 2 * HID)
        wm2 = sb("wm2", C, HID // C, C)
        scond = sb("scond", C, NB)
        modT = sb("modT", C, 9, NB)
        modall = sb("modall", C, PAIRS, NM, 2)
        gb2h = sb("gb2h", C, 1)
        mhalf, minus = sb("mhalf", 128, 2), sb("minus", 128, 2)
        modm = sb("modm", C, NW, 2)
        modw = sb("modw", C, NBK - NW, 2)
        modb = sb("modb", C, NM - NBK, 2)
        bso = sb("bso", C, 1)

        x0 = sb("x0", L, 2, C)
        c0 = sb("c0", LC, 2, C)
        st0, mv0, ln0 = sb("st0", L, 2, 6), sb("mv0", L, 2, 2), sb("ln0", L, 4, 2)
        z0 = sb("z0", L, 2, C)
        nxT = sb("nxT", C, 2, L)
        cT = sb("cT", C, 2, LC)
        q0T = sb("q0T", C, 2, L)
        k0T = sb("k0T", C, 2, LC)
        kcT = sb("kcT", C, 2, LC)
        v0 = sb("v0", LC, 2, C)
        vcA, vcM, vcB = sb("vcA", LC, 2, C), sb("vcM", LC, 2, C), sb("vcB", LC, 2, C)
        m0, nm0, l0, r0 = sb("m0", L, 2), sb("nm0", L, 2), sb("l0", L, 2), sb("r0", L, 2)
        P0 = sb("P0", L, 2, LC)
        P0n = sb("P0n", L, 2, LC)
        P0T = sb("P0T", LC, 2, L)
        evT = sb("evT", C, 2, L)
        rlT = sb("rlT", NE, 2, L)
        rm, re, rx = sb("rm", L, 2), sb("re", L, 2, NE), sb("rx", L, 2, NE)
        rs, rr = sb("rs", L, 2), sb("rr", L, 2)
        pr = sb("pr", L, 2, NE + 1)
        prT = sb("prT", C, 2, L)
        hT = sb("hT", C, NE * 2, 2, L)
        gs = sb("gs", C, 2, L)
        th = sb("th", C, 2, L)
        zb = sb("zb", L, 2, C)
        t0, t1, t2, dl = sb("t0", L, 2, C), sb("t1", L, 2, C), sb("t2", L, 2, C), sb("dl", L, 2, C)
        x1 = sb("x1", L, 2, C)
        st1, mv1, ln1 = sb("st1", L, 2, 6), sb("mv1", L, 2, 2), sb("ln1", L, 4, 2)
        z1 = sb("z1", L, 2, C)
        h1T = sb("h1T", C, 2, L)
        q1T = sb("q1T", C, 2, L)
        k1T = sb("k1T", C, 2, L)
        kbd1 = sb("kbd1", C, 2, NH, L)
        vbd1 = sb("vbd1", 128, 2 * 2 * NG, 2, 32)
        m1 = sb("m1", L, 2, NH)
        d1 = sb("d1", L, 2, NH, WIN)
        ones1 = sb("ones1", 128, 2, 32)
        r1 = sb("r1", C, 2, L)
        x1w = sb("x1w", L, 2, C)
        p1T = sb("p1T", 128, 2, NH // 2, L)
        o1T = sb("o1T", C, 2, L)
        y1T = sb("y1T", C, 2, L)
        xA, xM, xB = sb("xA", L, 2, C), sb("xM", L, 2, C), sb("xB", L, 2, C)
        st2, mv2, ln2 = sb("st2", L, 2, 6), sb("mv2", L, 2, 2), sb("ln2", L, 4, 2)
        z2 = sb("z2", L, 2, C)
        h2T = sb("h2T", C, 2, L)
        qcT = sb("qcT", C, 2, L)
        kbdc = sb("kbdc", C, 2, NH, LC)
        S = sb("S", L, 2, NH, LC)
        Sb = sb("Sb", L, NH, LC)
        S1 = sb("S1", L, 4, LC)
        top = sb("top", L, 2, NH, TOPK)
        tops = sb("tops", L, NH, TOPK)
        lc, rc = sb("lc", L, NH), sb("rc", L, NH)
        E_ = sb("E_", L, NH, LC)
        P = sb("P", L, 2, NH, LC)
        ew2 = E_[:, 0:7, :].rearrange("p h k -> p (h k)")[:, 0:6 * C].rearrange("p (k n) -> p k n", n=C)
        ew2T = E_[:, 8:15, :].rearrange("p h k -> p (h k)")[:, 0:6 * C].rearrange("p (k n) -> p k n", n=C)
        wada = P[:, 0, 0:10, :].rearrange("p h k -> p (h k)")[:, 0:9 * C].rearrange("p (k n) -> p k n", n=C)
        vbdc = sb("vbdc", LC, 2 * NG, 4, 32)
        pcT = sb("pcT", LC, NH, L)
        ocT = sb("ocT", C, 2, L)
        y2T = sb("y2T", C, 2, L)
        x3 = sb("x3", L, 2, C)
        st3, mv3, ln3 = sb("st3", L, 2, 6), sb("mv3", L, 2, 2), sb("ln3", L, 4, 2)
        z3 = sb("z3", L, 2, C)
        h3T = sb("h3T", C, 2, L)
        sa = sb("sa", C, HID // C, TP)
        u = sb("u", C, HID // C, TP)
        y3T = sb("y3T", C, 2, L)
        x4 = sb("x4", L, 2, C)

        ps = ctx.enter_context(nc.psum_tensor("ps", [128, 8 * 512], f32))

        def bank(n, parts=128, a=0, b=512):
            return ps[0:parts, 512 * n + a:512 * n + b]

        def two(ap):
            return ap.rearrange("p (b t) -> p b t", b=2)

        def one(name):
            return ctx.enter_context(nc.semaphore(name))

        def sems(names):
            return [ctx.enter_context(nc.semaphore(n)) for n in names.split()]

        def after(pair, per, part=None):
            value = per * pair + (per if part is None else part)
            return max(value, 0) if isinstance(value, int) else value

        x0_in, = sems("x0_in")
        c0_in, v_b, v_m, x_b, x_m = sems("c0_in v_b v_m x_b x_m")
        x4_out, = sems("x4_out")
        kbd1_in, kbdc_in = sems("kbd1_in kbdc_in")
        pe_z0, pe_q0, pe_v0, pe_S0, pe_P0T, pe_ev, pe_rl = sems("pe_z0 pe_q0 pe_v0 pe_S0 pe_P0T pe_ev pe_rl")
        pe_rlt, pe_e0, pe_e1, pe_e2, pe_g1, pe_prT, pe_g2 = sems("pe_rlt pe_e0 pe_e1 pe_e2 pe_g1 pe_prT pe_g2")
        pe_thT, pe_z1, pe_ckv, pe_qk1, pe_v1, pe_o1, pe_y1 = sems("pe_thT pe_z1 pe_ckv pe_qk1 pe_v1 pe_o1 pe_y1")
        pe_y1t, pe_z2, pe_qc, pe_y2, pe_y2t, pe_z3, pe_y3 = sems("pe_y1t pe_z2 pe_qc pe_y2 pe_y2t pe_z3 pe_y3")
        pe_y3t, = sems("pe_y3t")
        pe_y, pe_o2 = sems("pe_y pe_o2")
        pe_Sc, pe_pcT = sems("pe_Sc pe_pcT")
        pe_m1, pe_S1, pe_p1T = sems("pe_m1 pe_S1 pe_p1T")
        nxT_ok, cT_ok, q0T_ok, k0T_ok, kcT_ok, v0_ok, vcA_ok = sems("nxT_ok cT_ok q0T_ok k0T_ok kcT_ok v0_ok vcA_ok")
        P0T_ok, evT_ok, rx_ok, th_ok, prT_ok, q1T_ok, k1T_ok = sems("P0T_ok evT_ok rx_ok th_ok prT_ok q1T_ok k1T_ok")
        qcT_ok, = sems("qcT_ok")
        P0_ok, rlT_ok, gs_ok, zb_ok, h1T_ok, v1_ok, y1T_ok = sems("P0_ok rlT_ok gs_ok zb_ok h1T_ok v1_ok y1T_ok")
        h2T_ok, tops_ok, ocT_ok, y2T_ok, h3T_ok, y3T_ok = sems("h2T_ok tops_ok ocT_ok y2T_ok h3T_ok y3T_ok")
        h0_ok, h1_ok, h2_ok, sa_ok, E1_ok, p1T_ok = sems("h0_ok h1_ok h2_ok sa_ok E1_ok p1T_ok")
        S_ok, E_ok, pcT_ok = sems("S_ok E_ok pcT_ok")
        mv0_ok, m0_ok, nm0_ok, r0_ok, rm_ok, re_ok, rs_ok = sems("mv0_ok m0_ok nm0_ok r0_ok rm_ok re_ok rs_ok")
        rr_ok, pr_ok, dl_ok, x1_ok, mv1_ok, x1w_ok, r1_ok = sems("rr_ok pr_ok dl_ok x1_ok mv1_ok x1w_ok r1_ok")
        o1T_ok, xA_ok, mv2_ok, vbdc_ok, x3_ok, mv3_ok, x4_ok = sems("o1T_ok xA_ok mv2_ok vbdc_ok x3_ok mv3_ok x4_ok")
        st0_ok, st1_ok, st2_ok, st3_ok, z0_ok, z1_ok, z2_ok = sems("st0_ok st1_ok st2_ok st3_ok z0_ok z1_ok z2_ok")
        z3_ok, t0_ok, t1_ok, t2_ok, lc_ok, rc_ok = sems("z3_ok t0_ok t1_ok t2_ok lc_ok rc_ok")
        P0n_ok, = sems("P0n_ok")
        u_ok, m1_ok, d1_ok = sems("u_ok m1_ok d1_ok")
        sel_ok, = sems("sel_ok")
        max1_ok, rep1_ok, max2_ok, rep2_ok = sems("max1_ok rep1_ok max2_ok rep2_ok")
        modm_ok, modw_ok, modb_ok = sems("modm_ok modw_ok modb_ok")
        tsub_ok, = sems("tsub_ok")
        ln0_ok, ln1_ok, ln2_ok, ln3_ok = sems("ln0_ok ln1_ok ln2_ok ln3_ok")
        sub_ok, P_ok = sems("sub_ok P_ok")

        id0, id_ok, zero_ok = one("id0"), one("id_ok"), one("zero_ok")

        passed = one("passed")
        w_rows, w_small, w_big = one("w_rows"), one("w_small"), one("w_big")
        mixb_in = one("mixb_in")
        su_pe, su_act, su_dve = one("su_pe"), one("su_act"), one("su_dve")
        mods_ok, ones0 = one("mods_ok"), one("ones0")

        DEPTH = 4

        def iterations(eng, body):
            for i in range(DEPTH):
                body(i, range(i + 1))
            with eng.Fori(DEPTH, PAIRS) as i:
                body(i, range(DEPTH))
            for i in range(PAIRS, PAIRS + DEPTH - 1):
                body(i, range(i - PAIRS + 1, DEPTH))

        S1_BANK = [3, 4, 5, 3]
        P1T_BANK = [4, 5, 3, 4]
        SC_BANK = [4 + t if t < 2 else 3 + (t - 2) % 3 for t in range(8)]
        PCT_BANK = [6, 7, 6, 7, 7, 6, 7, 6]
        OC_BANK = [6, 7]
        E_BANK = [2, 0, 1]
        Y_BANK = [2, 0]
        M1_BANK = [7, 6, 7, 6]
        N_MODS = NE * 2 + 2 + 12
        N_ZERO = 10
        N_ROW_LOADS, N_SMALL, N_BIG = 15, 11, 7

        def col(name, n=0):
            return cols[:, rows[name] + n:rows[name] + n + 1]

        def diagonal(t, part, parts, off, dims):
            pitch = 1
            for n in list(t.shape)[1:]:
                pitch *= n
            return bass.AP(t, part * pitch + off, [[pitch, parts]] + dims)

        block = ctx.enter_context(nc.Block())

        @block.sync
        def _(sp):
            def row(name, src):
                n = src.shape[0]
                sp.dma_start(rowt[rows[name]:rows[name] + n, :], src).then_inc(w_rows, 16)

            def vec(name, key):
                row(name, I[key].rearrange("(r c) -> r c", c=C))

            def load(i):
                xs = I["x"][bass.ds(2 * i, 2), :, :].rearrange("b t d -> t b d")
                cs = I["ctx_1024"][bass.ds(2 * i, 2), :, :].rearrange("b t d -> t b d")
                sp.wait_ge(x1_ok, after(i - 1, 1))
                sp.wait_ge(z0_ok, after(i - 1, 2))
                sp.wait_ge(pe_z0, after(i - 1, 1))
                sp.dma_start(x0[0:L - SHIFT, :, :], xs[SHIFT:L, :, :]).then_inc(x0_in, 16)
                sp.dma_start(x0[L - SHIFT:L, :, :], xs[0:SHIFT, :, :]).then_inc(x0_in, 16)
                sp.dma_start(c0[:, :, :], cs).then_inc(c0_in, 16)

            vec("ln_gamma", "L0_xcond_ln_gamma")
            vec("ln_beta", "L0_xcond_ln_beta")
            row("e_b1", I["L0_xcond_e_b1"].rearrange("e (r c) -> (e r) c", c=C))
            vec("gate_b1", "L0_xcond_gate_b1")
            vec("gate_b2", "L0_xcond_gate_b2")
            vec("b_ada", "L1_xcond_b_ada")
            vec("b_qkv", "L1_xcond_b_qkv")
            vec("b_so", "L1_xcond_b_so")
            vec("b_q", "L1_xcond_b_q")
            vec("b_kv", "L1_xcond_b_kv")
            vec("b_co", "L1_xcond_b_co")
            vec("b_m1", "L1_xcond_b_m1")
            vec("b_m2", "L1_xcond_b_m2")
            row("cond", I["cond_1024"])
            row("e_b2", I["L0_xcond_e_b2"])
            def spread(dst, src, moved):
                for h in range(NH):
                    sp.dma_start(dst[D * h:D * h + D, :, h, :], src[D * h:D * h + D, :, :]).then_inc(moved, 16)

            def window_keys(w):
                sp.wait_ge(k1T_ok, after(w, 1))
                sp.wait_ge(pe_S1, after(w - 1, 4))
                spread(kbd1, k1T, kbd1_in)

            def cross_keys(w):
                sp.wait_ge(kcT_ok, after(w, 1))
                sp.wait_ge(pe_Sc, after(w - 1, 8))
                spread(kbdc, kcT, kbdc_in)

            def values_to_M(w):
                sp.wait_ge(vcA_ok, after(w, 1))
                sp.wait_ge(v_b, after(w - 1, 16))
                sp.dma_start(vcM[:, :, :], vcA[:, :, :]).then_inc(v_m, 16)

            def values_to_B(k):
                sp.wait_ge(v_m, after(k, 16))
                sp.wait_ge(vbdc_ok, after(k - 1, 1))
                sp.dma_start(vcB[:, :, :], vcM[:, :, :]).then_inc(v_b, 16)

            def x_to_M(w):
                sp.wait_ge(xA_ok, after(w, 1))
                sp.wait_ge(x_b, after(w - 1, 16))
                sp.dma_start(xM[:, :, :], xA[:, :, :]).then_inc(x_m, 16)

            def x_to_B(k):
                sp.wait_ge(x_m, after(k, 16))
                sp.wait_ge(x3_ok, after(k - 1, 1))
                sp.dma_start(xB[:, :, :], xM[:, :, :]).then_inc(x_b, 16)

            def store(j):
                sp.wait_ge(x4_ok, after(j, 1))
                os = out[bass.ds(2 * j, 2), :, :].rearrange("b t d -> t b d")
                sp.dma_start(os[SHIFT:L, :, :], x4[0:L - SHIFT, :, :]).then_inc(x4_out, 16)
                sp.dma_start(os[0:SHIFT, :, :], x4[L - SHIFT:L, :, :]).then_inc(x4_out, 16)

            def body(i, live):
                i1, i2, i3 = i - 1, i - 2, i - 3
                if 2 in live:
                    values_to_B(i2)
                if 0 in live:
                    load(i)
                if 1 in live:
                    window_keys(i1)
                    values_to_M(i1)
                    cross_keys(i1)
                if 3 in live:
                    store(i3)
                if 1 in live:
                    x_to_M(i1)
                    x_to_B(i1)

            iterations(sp, body)
            sp.wait_ge(x4_out, after(PAIRS - 1, 32))

        @block.gpsimd
        def _(pool):
            g = nc.gpsimd
            g.memset(ident[:, :], 0.0).then_inc(id0, 1)
            pool.wait_ge(id0, 1)
            g.affine_select(out=ident[:, :], in_=ident[:, :], compare_op=ALU.not_equal, fill=1.0, base=0,
                            pattern=[[-1, 128]], channel_multiplier=1).then_inc(id_ok, 1)
            for dst, src in ((ew2[:, :, :], I["L0_xcond_e_w2"].rearrange("e (k p) n -> p (e k) n", p=C)),
                             (outw[:, :], I["L0_xcond_out_w"]),
                             (gw1[:, :, :], I["L0_xcond_gate_w1"].rearrange("(k p) n -> p k n", p=C)),
                             (gw2[:, :], I["L0_xcond_gate_w2"]),
                             (wada[:, :, :], I["L1_xcond_w_ada"].rearrange("p (k n) -> p k n", n=C)),
                             (wqkv[:, :, :], I["L1_xcond_w_qkv"].rearrange("p (k n) -> p k n", n=C)),
                             (wm1[:, :], I["L1_xcond_w_m1"])):
                pool.dma_start(dst, src).then_inc(w_big, 16)
            g.memset(mhalf[:, :], -0.5).then_inc(zero_ok, 1)
            g.memset(minus[:, :], -1.0).then_inc(zero_ok, 1)
            g.memset(mixh[:, :], 0.0).then_inc(zero_ok, 1)
            g.memset(prT[:, :, :], 0.0).then_inc(zero_ok, 1)
            g.memset(vbd1[:, :, :, :], 0.0).then_inc(zero_ok, 1)
            g.memset(vbdc[:, :, :, :], 0.0).then_inc(zero_ok, 1)
            g.memset(kbdc[:, :, :, :], 0.0).then_inc(zero_ok, 1)
            pool.wait_ge(mods_ok, N_MODS)

            def normalise(mv_ok, ln_ok, z_ok, x, mv, ln, z, eps, pair):
                pool.wait_ge(mv_ok, after(pair, 1))
                pool.sem_inc(passed, 1)
                g.tensor_scalar(ln[:, 0, :], mv[:, :, 1], eps, None, ALU.add).then_inc(ln_ok, 1)
                g.tensor_tensor(ln[:, 1, :], mv[:, :, 0], minus[0:L, :], ALU.mult).then_inc(ln_ok, 1)
                pool.wait_ge(ln_ok, after(pair, 4, 1))
                g.tensor_tensor(ln[:, 2, :], ln[:, 0, :], mhalf[0:L, :], ALU.pow).then_inc(ln_ok, 1)
                pool.wait_ge(ln_ok, after(pair, 4, 3))
                g.tensor_tensor(ln[:, 3, :], ln[:, 1, :], ln[:, 2, :], ALU.mult).then_inc(ln_ok, 1)
                pool.wait_ge(ln_ok, after(pair, 4))
                pool.sem_inc(passed, 1)
                for b in range(2):
                    g.tensor_scalar(z[:, b, :], x[:, b, :], ln[:, 2, b:b + 1], ln[:, 3, b:b + 1], ALU.mult, ALU.add) \
                        .then_inc(z_ok, 1)

            def prototypes_norm(i):
                pool.wait_ge(r0_ok, after(i, 1))
                g.tensor_tensor(P0n[:, :, :], P0[:, :, :], r0[:, :, None].to_broadcast([L, 2, LC]), ALU.mult) \
                    .then_inc(P0n_ok, 1)

            def keep_x1(i):
                pool.wait_ge(x1_ok, after(i, 1))
                pool.wait_ge(xA_ok, after(i - 1, 1))
                pool.sem_inc(passed, 1)
                g.tensor_copy(x1w[:, :, :], x1[:, :, :]).then_inc(x1w_ok, 1)

            def shift(pair, b, c):
                h = 4 * c
                pool.wait_ge(max1_ok, after(pair, 2 * NH, b * NH + h + 4))
                if b == 0:
                    pool.wait_ge(P_ok, after(pair - 1, 8, 4 + c + 1))
                else:
                    pool.wait_ge(P_ok, after(pair, 8, c + 1))
                g.tensor_tensor(E_[:, h:h + 4, :], S[:, b, h:h + 4, :],
                                top[:, b, h:h + 4, 0:1].to_broadcast([L, 4, LC]), ALU.subtract) \
                    .then_inc(sub_ok, 1)

            def shift_top(pair, b):
                pool.wait_ge(max2_ok, after(pair, 2 * NH, b * NH + NH))
                if b == 0:
                    pool.wait_ge(lc_ok, after(pair - 1, 2))
                else:
                    pool.wait_ge(lc_ok, after(pair, 2, 1))
                g.tensor_tensor(tops[:, :, :], top[:, b, :, :], top[:, b, :, 0:1].to_broadcast([L, NH, TOPK]),
                                ALU.subtract).then_inc(tsub_ok, 1)

            def norm_top(pair, b, c):
                h = 4 * c
                pool.wait_ge(rc_ok, after(pair, 2, b + 1))
                pool.wait_ge(sel_ok, after(pair, 8, 4 * b + c + 1))
                pool.wait_ge(pe_pcT, after(pair - 1, 8, 4 * b + c + 1))
                g.tensor_tensor(P[:, b, h:h + 4, :], E_[:, h:h + 4, :],
                                rc[:, h:h + 4, None].to_broadcast([L, 4, LC]), ALU.mult).then_inc(P_ok, 1)

            def columns(dst, copied, a, b, pair):
                g.tensor_copy(dst[:, :, :], modall[:, bass.ds(pair, 1), a:b, :].rearrange("p o m b -> p (o m) b")) \
                    .then_inc(copied, 1)

            def body(i, live):
                i1, i2, i3 = i - 1, i - 2, i - 3
                if 0 in live:
                    pool.wait_ge(h1T_ok, after(i - 1, 2))
                    columns(modm, modm_ok, 0, NW, i)
                if 2 in live:
                    pool.wait_ge(y3T_ok, after(i2 - 1, 2))
                    columns(modb, modb_ok, NBK, NM, i2)
                    shift(i2, 1, 1)
                    shift(i2, 1, 2)
                    norm_top(i2, 0, 3)
                    shift(i2, 1, 3)
                    shift_top(i2, 1)
                    norm_top(i2, 1, 0)
                    norm_top(i2, 1, 1)
                    norm_top(i2, 1, 2)
                if 1 in live:
                    keep_x1(i1)
                if 2 in live:
                    norm_top(i2, 1, 3)
                if 0 in live:
                    pool.wait_ge(pe_z0, after(i - 1, 1))
                    normalise(mv0_ok, ln0_ok, z0_ok, x0, mv0, ln0, z0, EPS0, i)
                if 2 in live:
                    pool.wait_ge(pe_z3, after(i2 - 1, 1))
                    normalise(mv3_ok, ln3_ok, z3_ok, x3, mv3, ln3, z3, EPS1, i2)
                if 1 in live:
                    pool.wait_ge(pe_z2, after(i1 - 1, 1))
                    normalise(mv2_ok, ln2_ok, z2_ok, xA, mv2, ln2, z2, EPS1, i1)
                if 0 in live:
                    prototypes_norm(i)
                if 1 in live:
                    shift(i1, 0, 0)
                    shift(i1, 0, 1)
                    shift(i1, 0, 2)
                    shift(i1, 0, 3)
                    shift_top(i1, 0)
                    norm_top(i1, 0, 0)
                    norm_top(i1, 0, 1)
                if 0 in live:
                    pool.wait_ge(h2T_ok, after(i - 1, 2))
                    columns(modw, modw_ok, NW, NBK, i)
                    pool.wait_ge(pe_z1, after(i - 1, 1))
                    normalise(mv1_ok, ln1_ok, z1_ok, x1, mv1, ln1, z1, EPS1, i)
                if 1 in live:
                    norm_top(i1, 0, 2)
                    shift(i1, 1, 0)

            iterations(pool, body)

        @block.vector
        def _(dve):
            v = nc.vector
            v.memset(modall[:, :, :, :], 0.0).then_inc(zero_ok, 1)
            v.memset(kbd1[:, :, :, :], 0.0).then_inc(zero_ok, 1)
            v.memset(ones1[:, :, :], 0.0).then_inc(ones0, 1)
            dve.wait_ge(ones0, 1)
            for h in range(2):
                r = v.memset(diagonal(ones1, 64 * h, 64, D * h, [[32 + 2 * D, 2], [1, D]]), 1.0)
            r.then_inc(zero_ok, 1)
            dve.wait_ge(su_pe, 1)
            v.tensor_copy(cols[:, :], bank(0, C, 0, n_rows)).then_inc(su_dve, 1)
            dve.wait_ge(su_pe, 2)
            v.tensor_copy(ew2T[:, 0:4, :], bank(1).rearrange("p (k n) -> p k n", n=C)).then_inc(su_dve, 1)
            v.tensor_copy(ew2T[:, 4:6, :], bank(2, 128, 0, 256).rearrange("p (k n) -> p k n", n=C)).then_inc(su_dve, 1)
            dve.wait_ge(su_pe, 4)
            dve.wait_ge(su_dve, 1)
            dve.wait_ge(zero_ok, N_ZERO)
            pairs = lambda ap: ap.rearrange("p (i b) -> p i b", b=2)

            def put(name, src, *a, parts=C):
                v.tensor_scalar(modall[0:parts, :, MOD[name], :], pairs(src), *a).then_inc(mods_ok, 1)

            for n in range(NE * 2):
                put(f"EB{n}", bank(6, C, NB * n, NB * n + NB), col("e_b1", n), None, ALU.add)
            put("GB", bank(6, C, NB * 6, NB * 7), col("gate_b1"), None, ALU.add)
            dve.wait_ge(w_small, 16 * N_SMALL)
            put("RL", bank(6, NE, NB * 7, NB * 8), rb[:, 0:1], None, ALU.add, parts=NE)
            dve.wait_ge(su_pe, 5)
            v.tensor_tensor(modT[:, :, :], bank(7, C, 0, 9 * NB).rearrange("p (k b) -> p k b", b=NB),
                            cols[:, rows["b_ada"]:rows["b_ada"] + 9, None].to_broadcast([C, 9, NB]), ALU.add) \
                .then_inc(su_dve, 1)
            dve.wait_ge(su_dve, 4)
            v.tensor_tensor(bso[:, :], bank(0, C, 0, 1), col("b_so"), ALU.add).then_inc(su_dve, 1)
            dve.wait_ge(su_dve, 5)
            for n, b in ((1, bso[:, 0:1]), (2, col("b_co")), (3, col("b_m2"))):
                t = 3 * (n - 1)
                put(f"SH{n}", modT[:, t, :], 0.0, None, ALU.add)
                put(f"SC{n}", modT[:, t + 1, :], 1.0, None, ALU.add)
                put(f"G{n}", modT[:, t + 2, :], 0.0, None, ALU.add)
                put(f"BG{n}", modT[:, t + 2, :], b, None, ALU.mult)

            def stats(x_ok, st_ok, mv_ok, x, st, mv, pair):
                for b in range(2):
                    if x_ok is not None:
                        dve.wait_ge(x_ok, after(pair, 1))
                    v.bn_stats(st[:, b, :], x[:, b, :]).then_inc(st_ok, 1)
                dve.wait_ge(st_ok, after(pair, 2))
                dve.sem_inc(passed, 1)
                for b in range(2):
                    r = v.bn_aggr(mv[:, b, :], st[:, b, :])
                r.then_inc(mv_ok, 1)

            def top16(pair, b, c):
                hs = range(4 * c, 4 * c + 4)
                dve.wait_ge(S_ok, after(pair, 8, 4 * b + c + 1))
                dve.sem_inc(passed, 1)
                for h in hs:
                    v.max(top[:, b, h, 0:8], S[:, b, h, :]).then_inc(max1_ok, 1)
                for h in hs:
                    dve.wait_ge(max1_ok, after(pair, 2 * NH, b * NH + h + 1))
                    dve.sem_inc(passed, 1)
                    v.match_replace(S1[:, h % 4, :], top[:, b, h, 0:8], S[:, b, h, :], GONE).then_inc(rep1_ok, 1)
                for h in hs:
                    dve.wait_ge(rep1_ok, after(pair, 2 * NH, b * NH + h + 1))
                    dve.sem_inc(passed, 1)
                    v.max(top[:, b, h, 8:16], S1[:, h % 4, :]).then_inc(max2_ok, 1)
                for h in hs:
                    dve.wait_ge(max2_ok, after(pair, 2 * NH, b * NH + h + 1))
                    dve.sem_inc(passed, 1)
                    v.match_replace(Sb[:, h, :], top[:, b, h, 8:16], S1[:, h % 4, :], GONE).then_inc(rep2_ok, 1)

            def select(pair, b, c):
                h = 4 * c
                dve.wait_ge(rep2_ok, after(pair, 2 * NH, b * NH + h + 4))
                dve.wait_ge(E_ok, after(pair, 8, 4 * b + c + 1))
                v.scalar_tensor_tensor(E_[:, h:h + 4, :], Sb[:, h:h + 4, :], GONE / 2, E_[:, h:h + 4, :],
                                       ALU.is_lt, ALU.mult).then_inc(sel_ok, 1)

            def softmax_sum(pair, b):
                dve.wait_ge(tops_ok, after(pair, 2, b + 1))
                v.tensor_reduce(lc[:, :], tops[:, :, :], AX.X, ALU.add).then_inc(lc_ok, 1)
                dve.wait_ge(lc_ok, after(pair, 2, b + 1))
                if b == 0:
                    dve.wait_ge(P_ok, after(pair - 1, 8))
                else:
                    dve.wait_ge(P_ok, after(pair, 8, 4))
                v.reciprocal(rc[:, :], lc[:, :]).then_inc(rc_ok, 1)

            def experts(i, b):
                def add(n, t_in, t_out):
                    return v.scalar_tensor_tensor(t_out[:, b, :], bank(Y_BANK[b], L, C * n, C * n + C),
                                                  pr[:, b, n:n + 1], t_in[:, b, :], ALU.mult, ALU.add)

                dve.wait_ge(zb_ok, after(i, 2, b + 1))
                add(0, zb, t0).then_inc(t0_ok, 1)
                dve.wait_ge(t0_ok, after(i, 2, b + 1))
                add(1, t0, t1).then_inc(t1_ok, 1)
                dve.wait_ge(t1_ok, after(i, 2, b + 1))
                add(2, t1, t2).then_inc(t2_ok, 1)

            def residual(i):
                dve.wait_ge(t2_ok, after(i, 2))
                dve.wait_ge(pe_thT, after(i, 1))
                v.scalar_tensor_tensor(dl[:, :, :], two(bank(1, L, 0, TP)), 1.0, t2[:, :, :], ALU.add, ALU.mult) \
                    .then_inc(dl_ok, 1)
                dve.wait_ge(dl_ok, after(i, 1))
                dve.wait_ge(z1_ok, after(i - 1, 2))
                dve.wait_ge(x1w_ok, after(i - 1, 1))
                v.tensor_tensor(x1[:, :, :], dl[:, :, :], x0[:, :, :], ALU.add).then_inc(x1_ok, 1)

            def prototypes_max(i):
                dve.wait_ge(pe_S0, after(i, 1))
                v.tensor_reduce(m0[:, :], two(bank(0, L, 0, 2 * LC)), AX.X, ALU.max).then_inc(m0_ok, 1)
                dve.wait_ge(m0_ok, after(i, 1))
                v.tensor_scalar(nm0[:, :], m0[:, :], -SC0, None, ALU.mult).then_inc(nm0_ok, 1)

            def prototypes_sum(i):
                dve.wait_ge(P0_ok, after(i, 2))
                v.reciprocal(r0[:, :], l0[:, :]).then_inc(r0_ok, 1)

            def router_max(i):
                lg = bank(1, L, 0, 2 * NE).rearrange("p (b e) -> p b e", b=2)
                dve.wait_ge(pe_rlt, after(i, 1))
                v.tensor_reduce(rm[:, :], lg, AX.X, ALU.max).then_inc(rm_ok, 1)
                dve.wait_ge(rm_ok, after(i, 1))
                v.tensor_tensor(re[:, :, :], lg, rm[:, :, None].to_broadcast([L, 2, NE]), ALU.subtract) \
                    .then_inc(re_ok, 1)

            def router_norm(i):
                dve.wait_ge(rx_ok, after(i, 1))
                v.tensor_reduce(rs[:, :], rx[:, :, :], AX.X, ALU.add).then_inc(rs_ok, 1)
                dve.wait_ge(rs_ok, after(i, 1))
                v.reciprocal(rr[:, :], rs[:, :]).then_inc(rr_ok, 1)
                dve.wait_ge(rr_ok, after(i, 1))
                v.memset(pr[:, :, NE:NE + 1], 1.0)
                v.tensor_tensor(pr[:, :, 0:NE], rx[:, :, :], rr[:, :, None].to_broadcast([L, 2, NE]), ALU.mult) \
                    .then_inc(pr_ok, 1)

            def window_shift(w, t):
                b, q = t // 2, t % 2
                sc = bank(S1_BANK[t]).rearrange("p (h k) -> p h k", k=WIN)
                dve.wait_ge(pe_S1, after(w, 4, t + 1))
                v.tensor_reduce(m1[:, b, 8 * q:8 * q + 8], sc, AX.X, ALU.max).then_inc(m1_ok, 1)
                dve.wait_ge(m1_ok, after(w, 4, t + 1))
                v.tensor_tensor(d1[:, b, 8 * q:8 * q + 8, :], sc, m1[:, b, 8 * q:8 * q + 8, None]
                                .to_broadcast([L, 8, WIN]), ALU.subtract).then_inc(d1_ok, 1)

            def window_norm(w):
                dve.wait_ge(pe_o1, after(w, 1))
                v.reciprocal(r1[:, :, :], two(bank(5, C, TP, 2 * TP))).then_inc(r1_ok, 1)
                dve.wait_ge(r1_ok, after(w, 1))
                v.tensor_tensor(o1T[:, :, :], two(bank(5, C, 0, TP)), r1[:, :, :], ALU.mult).then_inc(o1T_ok, 1)

            def swiglu(j, c):
                dve.wait_ge(sa_ok, after(j, 4, c + 1))
                v.scalar_tensor_tensor(u[:, c, :], bank(M1_BANK[c], C, TP, 2 * TP), col("b_m1", HID // C + c),
                                       sa[:, c, :], ALU.add, ALU.mult).then_inc(u_ok, 1)

            def cross_values(j):
                dve.wait_ge(v_b, after(j, 16))
                dve.wait_ge(pe_o2, after(j - 1, 2))
                v.tensor_copy(diagonal(vbdc, 0, LC, 0, [[4 * 32, 2 * NG], [32 + D, 4], [1, D]]),
                              vcB[:, :, :].rearrange("p b (g j d) -> p (b g) j d", j=4, d=D)) \
                    .then_inc(vbdc_ok, 1)

            def x_after_window(w):
                dve.wait_ge(pe_y1t, after(w, 1))
                dve.wait_ge(x_m, after(w - 1, 16))
                dve.wait_ge(z2_ok, after(w - 1, 2))
                dve.wait_ge(x1w_ok, after(w, 1))
                v.tensor_tensor(xA[:, :, :], two(bank(4, L, 0, TP)), x1w[:, :, :], ALU.add).then_inc(xA_ok, 1)

            def x_after_cross(j):
                dve.wait_ge(x_b, after(j, 16))
                dve.wait_ge(pe_y2t, after(j, 1))
                dve.wait_ge(z3_ok, after(j - 1, 2))
                v.tensor_tensor(x3[:, :, :], two(bank(7, L, 0, TP)), xB[:, :, :], ALU.add).then_inc(x3_ok, 1)

            def x_after_swiglu(j):
                dve.wait_ge(pe_y3t, after(j, 1))
                dve.wait_ge(x4_out, after(j - 1, 32))
                v.tensor_tensor(x4[:, :, :], two(bank(6, L, 0, TP)), x3[:, :, :], ALU.add).then_inc(x4_ok, 1)

            def body(i, live):
                i1, i2, i3 = i - 1, i - 2, i - 3
                if 1 in live:
                    experts(i1, 1)
                    residual(i1)
                    stats(x1_ok, st1_ok, mv1_ok, x1, st1, mv1, i1)
                if 2 in live:
                    select(i2, 0, 2)
                    top16(i2, 1, 1)
                    select(i2, 0, 3)
                    top16(i2, 1, 2)
                if 3 in live:
                    x_after_swiglu(i3)
                if 2 in live:
                    top16(i2, 1, 3)
                if 0 in live:
                    dve.wait_ge(x0_in, after(i, 32))
                    stats(None, st0_ok, mv0_ok, x0, st0, mv0, i)
                if 2 in live:
                    cross_values(i2)
                    select(i2, 1, 0)
                    softmax_sum(i2, 1)
                    select(i2, 1, 1)
                    select(i2, 1, 2)
                    select(i2, 1, 3)
                if 1 in live:
                    window_shift(i1, 0)
                    window_shift(i1, 1)
                    window_shift(i1, 2)
                    window_shift(i1, 3)
                if 2 in live:
                    x_after_cross(i2)
                    stats(x3_ok, st3_ok, mv3_ok, x3, st3, mv3, i2)
                if 1 in live:
                    window_norm(i1)
                if 0 in live:
                    prototypes_max(i)
                if 1 in live:
                    x_after_window(i1)
                    stats(xA_ok, st2_ok, mv2_ok, xA, st2, mv2, i1)
                if 2 in live:
                    swiglu(i2, 0)
                    swiglu(i2, 1)
                    swiglu(i2, 2)
                    swiglu(i2, 3)
                if 1 in live:
                    top16(i1, 0, 0)
                if 0 in live:
                    prototypes_sum(i)
                if 1 in live:
                    top16(i1, 0, 1)
                    top16(i1, 0, 2)
                if 0 in live:
                    router_max(i)
                if 1 in live:
                    select(i1, 0, 0)
                if 0 in live:
                    router_norm(i)
                if 1 in live:
                    top16(i1, 0, 3)
                    select(i1, 0, 1)
                    top16(i1, 1, 0)
                    softmax_sum(i1, 0)
                if 0 in live:
                    experts(i, 0)

            iterations(dve, body)

        @block.scalar
        def _(act):
            a = nc.scalar
            for dst, src in ((rb[:, 0:1], I["L0_xcond_router_b"].rearrange("(p o) -> p o", o=1)),
                             (Wq0[:, :], I["L0_xcond_Wq"]), (Wk0[:, :], I["L0_xcond_Wk"]), (Wv0[:, :], I["L0_xcond_Wv"]),
                             (rw[:, :, :], I["L0_xcond_router_W"].rearrange("(k p) n -> p k n", p=C)),
                             (wkv[:, :, :], I["L1_xcond_w_kv"].rearrange("p (k n) -> p k n", n=C)),
                             (ew1[:, :, :, :], I["L0_xcond_e_w1"].rearrange("e (k p) n -> p e k n", p=C)),
                             (wso[:, :], I["L1_xcond_w_so"]), (wq[:, :], I["L1_xcond_w_q"]), (wco[:, :], I["L1_xcond_w_co"]),
                             (wm2[:, :, :], I["L1_xcond_w_m2"].rearrange("(k p) n -> p k n", p=C))):
                act.dma_start(dst, src).then_inc(w_small, 16)
            act.dma_start(mixb[NE:NE + 1, :], I["L0_xcond_out_b"].rearrange("(o c) -> o c", o=1)).then_inc(mixb_in, 16)
            act.wait_ge(su_dve, 1)
            a.activation(scond[:, :], cols[:, rows["cond"]:rows["cond"] + NB], ACT.Silu).then_inc(su_act, 1)
            a.mul(gb2h[:, :], col("gate_b2"), 0.5).then_inc(su_act, 1)
            act.wait_ge(su_pe, 3)
            a.mul(ew2o[:, 0:4, :], bank(3).rearrange("p (k n) -> p k n", n=C), 0.5).then_inc(su_act, 1)
            a.mul(ew2o[:, 4:6, :], bank(4, 128, 0, 256).rearrange("p (k n) -> p k n", n=C), 0.5).then_inc(su_act, 1)
            a.copy(mixb[0:NE, :], bank(5, NE, 0, C)).then_inc(su_act, 1)
            act.wait_ge(mixb_in, 16)
            act.wait_ge(su_act, 5)
            act.wait_ge(zero_ok, N_ZERO)
            a.mul(mixh[0:NE + 1, :], mixb[:, :], 0.5).then_inc(su_act, 1)

            def of_mix(name, b):
                return modm[:, MOD[name], b:b + 1]

            def of_window(name, b):
                return modw[:, MOD[name] - NW, b:b + 1]

            def of_back(name, b):
                return modb[:, MOD[name] - NBK, b:b + 1]

            def half(n, b, w=C):
                return bank(n, C, w * b, w * b + w)

            def modulated(n, hT_ok, hT, src, m):
                for b in range(2):
                    a.activation(hT[:, b, :], half(src, b), ACT.Identity, scale=m(f"SC{n}", b), bias=m(f"SH{n}", b)) \
                        .then_inc(hT_ok, 1)

            def gated(n, yT_ok, yT, src, m):
                for b in range(2):
                    a.activation(yT[:, b, :], half(src, b), ACT.Identity, scale=m(f"G{n}", b), bias=m(f"BG{n}", b)) \
                        .then_inc(yT_ok, 1)

            def pcT_copy(j, t):
                b, c = t // 4, t % 4
                act.wait_ge(pe_pcT, after(j, 8, t + 1))
                if b == 0:
                    act.wait_ge(pe_o2, after(j - 1, 2))
                else:
                    act.wait_ge(pe_o2, after(j, 2, 1))
                a.copy(pcT[:, 4 * c:4 * c + 4, :], bank(PCT_BANK[t], LC).rearrange("p (h t) -> p h t", h=4)) \
                    .then_inc(pcT_ok, 1)

            def exps(k, b, c):
                act.wait_ge(sub_ok, after(k, 8, 4 * b + c + 1))
                a.activation(E_[:, 4 * c:4 * c + 4, :], E_[:, 4 * c:4 * c + 4, :], ACT.Exp).then_inc(E_ok, 1)

            def exps_top(k, b):
                act.wait_ge(tsub_ok, after(k, 2, b + 1))
                a.activation(tops[:, :, :], tops[:, :, :], ACT.Exp).then_inc(tops_ok, 1)

            def oc_copy(j, b):
                act.wait_ge(pe_o2, after(j, 2, b + 1))
                a.activation(ocT[:, b, :], bank(OC_BANK[b], C, 0, L), ACT.Identity, bias=col("b_kv", 1)) \
                    .then_inc(ocT_ok, 1)

            def expert_hidden(e, h_ok):
                for c in range(2):
                    for b in range(2):
                        a.activation(hT[:, 2 * e + c, b, :], bank(E_BANK[e], C, TP * c + L * b, TP * c + L * b + L),
                                     ACT.Silu, bias=of_mix(f"EB{2 * e + c}", b)).then_inc(h_ok, 1)

            def p1T_copy(w, t):
                b, q = t // 2, t % 2
                act.wait_ge(pe_p1T, after(w, 4, t + 1))
                a.copy(p1T[:, b, 4 * q:4 * q + 4, :], bank(P1T_BANK[t]).rearrange("p (k t) -> p k t", t=L)) \
                    .then_inc(p1T_ok, 1)

            def z_copy(i, b):
                act.wait_ge(pe_y, after(i, 2, b + 1))
                a.copy(zb[:, b, :], bank(Y_BANK[b], L, NE * C, NE * C + C)).then_inc(zb_ok, 1)

            def silu_a(j, c):
                act.wait_ge(pe_m1, after(j, 4, c + 1))
                a.activation(sa[:, c, :], bank(M1_BANK[c], C, 0, TP), ACT.Silu, bias=col("b_m1", c)) \
                    .then_inc(sa_ok, 1)

            def scores_copy(w, t):
                b, c = t // 4, t % 4
                act.wait_ge(pe_Sc, after(w, 8, t + 1))
                act.wait_ge(rep1_ok, after(w - 1, 2 * NH, b * NH + 4 * c + 4))
                act.wait_ge(sub_ok, after(w - 1, 8, t + 1))
                a.mul(S[:, b, 4 * c:4 * c + 4, :], bank(SC_BANK[t], L, 0, 4 * LC)
                      .rearrange("p (h k) -> p h k", k=LC), SC1).then_inc(S_ok, 1)

            def window_keys(w):
                act.wait_ge(pe_qk1, after(w, 1))
                act.wait_ge(kbd1_in, after(w - 1, 16 * NH))
                a.activation(k1T[:, :, :], two(bank(4, C, TP, 2 * TP)), ACT.Identity, bias=col("b_qkv", 1)) \
                    .then_inc(k1T_ok, 1)

            def window_queries(w):
                act.wait_ge(pe_qk1, after(w, 1))
                act.wait_ge(pe_S1, after(w - 1, 4))
                a.activation(q1T[:, :, :], two(bank(4, C, 0, TP)), ACT.Identity, bias=col("b_qkv", 0)) \
                    .then_inc(q1T_ok, 1)

            def cross_keys(w):
                act.wait_ge(pe_ckv, after(w, 1))
                act.wait_ge(kbdc_in, after(w - 1, 16 * NH))
                a.activation(kcT[:, :, :], two(bank(3, C, 0, 2 * LC)), ACT.Identity, bias=col("b_kv", 0)) \
                    .then_inc(kcT_ok, 1)

            def cross_values(w):
                act.wait_ge(pe_ckv, after(w, 1))
                act.wait_ge(v_m, after(w - 1, 16))
                a.copy(vcA[:, :, :], two(bank(3, LC, 2 * LC, 2 * LC + TP))).then_inc(vcA_ok, 1)

            def window_values(w):
                act.wait_ge(pe_v1, after(w, 1))
                act.wait_ge(pe_o1, after(w - 1, 1))
                for h in range(2):
                    a.copy(diagonal(vbd1, 64 * h, 64, D * h, [[64, 4 * NG], [32 + 2 * D, 2], [1, D]]),
                           bank(5)[64 * h:64 * h + 64, :].rearrange("p (x q c) -> p x q c", q=2, c=2 * D)
                           [:, :, :, D * h:D * h + D]).then_inc(v1_ok, 1)

            def nx_copy(i):
                act.wait_ge(pe_z0, after(i, 1))
                act.wait_ge(pe_g1, after(i - 1, 1))
                a.activation(nxT[:, :, :], two(bank(0, C, 0, TP)), ACT.Identity, scale=col("ln_gamma"),
                             bias=col("ln_beta")).then_inc(nxT_ok, 1)

            def context_copy(i):
                act.wait_ge(pe_z0, after(i, 1))
                act.wait_ge(pe_ckv, after(i - 1, 1))
                a.copy(cT[:, :, :], two(bank(0, C, TP, TP + 2 * LC))).then_inc(cT_ok, 1)

            def qk0_copy(i):
                act.wait_ge(pe_q0, after(i, 1))
                a.copy(q0T[:, :, :], two(bank(1, C, 0, TP))).then_inc(q0T_ok, 1)
                a.copy(k0T[:, :, :], two(bank(1, C, TP, TP + 2 * LC))).then_inc(k0T_ok, 1)

            def v0_copy(i):
                act.wait_ge(pe_v0, after(i, 1))
                a.copy(v0[:, :, :], two(bank(2, LC, 0, TP))).then_inc(v0_ok, 1)

            def prototypes_exp(i):
                act.wait_ge(nm0_ok, after(i, 1))
                for b in range(2):
                    a.activation(P0[:, b, :], bank(0, L, LC * b, LC * b + LC), ACT.Exp, scale=SC0,
                                 bias=nm0[:, b:b + 1], accum_out=l0[:, b:b + 1]).then_inc(P0_ok, 1)

            def P0T_copy(i):
                act.wait_ge(pe_P0T, after(i, 1))
                a.copy(P0T[:, :, :], two(bank(1, LC, 0, TP))).then_inc(P0T_ok, 1)

            def evidence_copy(i):
                act.wait_ge(pe_ev, after(i, 1))
                a.copy(evT[:, :, :], two(bank(2, C, 0, TP))).then_inc(evT_ok, 1)

            def router_copy(i):
                act.wait_ge(modm_ok, after(i, 1))
                act.wait_ge(pe_rl, after(i, 1))
                for b in range(2):
                    a.activation(rlT[:, b, :], bank(0, NE, L * b, L * b + L), ACT.Identity,
                                 bias=modm[0:NE, MOD["RL"], b:b + 1]).then_inc(rlT_ok, 1)

            def router_exp(i):
                act.wait_ge(re_ok, after(i, 1))
                a.activation(rx[:, :, :], re[:, :, :], ACT.Exp).then_inc(rx_ok, 1)

            def gate_hidden(i):
                act.wait_ge(pe_g1, after(i, 1))
                for b in range(2):
                    a.activation(gs[:, b, :], half(2, b), ACT.Silu, bias=of_mix("GB", b)).then_inc(gs_ok, 1)

            def shares_copy(i):
                act.wait_ge(pe_prT, after(i, 1))
                a.copy(prT[0:NE + 1, :, :], two(bank(1, NE + 1, 0, TP))).then_inc(prT_ok, 1)

            def gate_tanh(i):
                act.wait_ge(pe_g2, after(i, 1))
                a.activation(th[:, :, :], two(bank(0, C, 0, TP)), ACT.Tanh, scale=0.5, bias=gb2h[:, 0:1]) \
                    .then_inc(th_ok, 1)

            def window_exp(w, t):
                b, q = t // 2, t % 2
                act.wait_ge(d1_ok, after(w, 4, t + 1))
                a.activation(d1[:, b, 8 * q:8 * q + 8, :], d1[:, b, 8 * q:8 * q + 8, :], ACT.Exp, scale=SC1) \
                    .then_inc(E1_ok, 1)

            def queries_copy(w):
                act.wait_ge(pe_qc, after(w, 1))
                a.activation(qcT[:, :, :], two(bank(3, C, 0, TP)), ACT.Identity, bias=col("b_q")) \
                    .then_inc(qcT_ok, 1)

            def body(i, live):
                i1, i2, i3 = i - 1, i - 2, i - 3
                if 1 in live:
                    cross_keys(i1)
                    act.wait_ge(pe_z1, after(i1, 1))
                    act.wait_ge(pe_v1, after(i1 - 1, 1))
                    modulated(1, h1T_ok, h1T, 2, of_mix)
                    window_keys(i1)
                if 2 in live:
                    exps(i2, 1, 0)
                if 1 in live:
                    window_queries(i1)
                if 2 in live:
                    pcT_copy(i2, 0)
                    pcT_copy(i2, 1)
                    exps(i2, 1, 1)
                    pcT_copy(i2, 2)
                    exps(i2, 1, 2)
                    pcT_copy(i2, 3)
                if 1 in live:
                    cross_values(i1)
                if 2 in live:
                    exps_top(i2, 1)
                    exps(i2, 1, 3)
                    oc_copy(i2, 0)
                    pcT_copy(i2, 4)
                    pcT_copy(i2, 5)
                    pcT_copy(i2, 6)
                if 1 in live:
                    window_values(i1)
                if 2 in live:
                    pcT_copy(i2, 7)
                if 1 in live:
                    window_exp(i1, 0)
                    window_exp(i1, 1)
                if 2 in live:
                    oc_copy(i2, 1)
                if 1 in live:
                    window_exp(i1, 2)
                    p1T_copy(i1, 0)
                    p1T_copy(i1, 1)
                    window_exp(i1, 3)
                if 2 in live:
                    act.wait_ge(modb_ok, after(i2, 1))
                    act.wait_ge(pe_y2, after(i2, 1))
                    gated(2, y2T_ok, y2T, 6, of_back)
                if 1 in live:
                    p1T_copy(i1, 2)
                    p1T_copy(i1, 3)
                if 0 in live:
                    nx_copy(i)
                    context_copy(i)
                    qk0_copy(i)
                if 1 in live:
                    act.wait_ge(modw_ok, after(i1, 1))
                    act.wait_ge(pe_y1, after(i1, 1))
                    gated(1, y1T_ok, y1T, 3, of_window)
                if 2 in live:
                    act.wait_ge(modb_ok, after(i2, 1))
                    act.wait_ge(pe_z3, after(i2, 1))
                    modulated(3, h3T_ok, h3T, 6, of_back)
                    silu_a(i2, 0)
                    silu_a(i2, 1)
                if 1 in live:
                    act.wait_ge(modw_ok, after(i1, 1))
                    act.wait_ge(pe_z2, after(i1, 1))
                    modulated(2, h2T_ok, h2T, 5, of_window)
                if 2 in live:
                    silu_a(i2, 2)
                if 1 in live:
                    queries_copy(i1)
                if 2 in live:
                    silu_a(i2, 3)
                if 1 in live:
                    scores_copy(i1, 0)
                if 0 in live:
                    prototypes_exp(i)
                if 1 in live:
                    scores_copy(i1, 1)
                if 2 in live:
                    act.wait_ge(pe_y3, after(i2, 1))
                    gated(3, y3T_ok, y3T, 7, of_back)
                if 1 in live:
                    scores_copy(i1, 2)
                if 0 in live:
                    v0_copy(i)
                    P0T_copy(i)
                if 1 in live:
                    scores_copy(i1, 3)
                if 0 in live:
                    evidence_copy(i)
                if 1 in live:
                    scores_copy(i1, 4)
                    exps(i1, 0, 0)
                    scores_copy(i1, 5)
                if 0 in live:
                    router_copy(i)
                if 1 in live:
                    exps(i1, 0, 1)
                if 0 in live:
                    router_exp(i)
                    act.wait_ge(pe_e0, after(i, 1))
                    expert_hidden(0, h0_ok)
                    act.wait_ge(pe_e1, after(i, 1))
                    expert_hidden(1, h1_ok)
                    act.wait_ge(pe_e2, after(i, 1))
                    expert_hidden(2, h2_ok)
                    gate_hidden(i)
                    shares_copy(i)
                    gate_tanh(i)
                if 1 in live:
                    exps_top(i1, 0)
                if 0 in live:
                    z_copy(i, 0)
                    z_copy(i, 1)
                if 1 in live:
                    scores_copy(i1, 6)
                    exps(i1, 0, 2)
                    exps(i1, 0, 3)
                    scores_copy(i1, 7)

            iterations(act, body)

        @block.tensor
        def _(pe):
            t_ = nc.tensor

            def mm(o, l, r, start=True, stop=True):
                return t_.matmul(o, l, r, start=start, stop=stop)

            def back_to(o, x):
                return t_.transpose(o, x, ident[0:x.shape[0], 0:x.shape[0]])

            pe.wait_ge(id_ok, 1)
            pe.wait_ge(w_rows, 16 * N_ROW_LOADS)
            back_to(bank(0, C, 0, n_rows), rowt[:, :]).then_inc(su_pe, 1)
            pe.wait_ge(w_big, 16 * N_BIG)
            for n in range(NE * 2):
                r = back_to(bank(1 + n // 4, C, C * (n % 4), C * (n % 4) + C), ew2[:, n, :])
            r.then_inc(su_pe, 1)
            pe.wait_ge(su_dve, 3)
            for n in range(NE * 2):
                mm(bank(3 + n // 4, C, C * (n % 4), C * (n % 4) + C), ew2T[:, n, :], outw[:, :])
            mm(bank(5, NE, 0, C), cols[:, rows["e_b2"]:rows["e_b2"] + NE], outw[:, :]).then_inc(su_pe, 1)
            pe.wait_ge(w_small, 16 * N_SMALL)
            cond = cols[:, rows["cond"]:rows["cond"] + NB]
            for n in range(NE * 2):
                mm(bank(6, C, NB * n, NB * n + NB), ew1[:, n // 2, 2, C * (n % 2):C * (n % 2) + C], cond)
            mm(bank(6, C, NB * 6, NB * 7), gw1[:, 2, :], cond)
            mm(bank(6, NE, NB * 7, NB * 8), rw[:, 2, :], cond).then_inc(su_pe, 1)
            pe.wait_ge(su_act, 1)
            mm(bank(0, C, 0, 1), wso[:, :], col("b_qkv", 2))
            for n in range(9):
                r = mm(bank(7, C, NB * n, NB * n + NB), wada[:, n, :], scond[:, :])
            r.then_inc(su_pe, 1)
            pe.wait_ge(mods_ok, N_MODS)
            pe.wait_ge(su_act, 6)
            pe.wait_ge(zero_ok, N_ZERO)

            def half(n, b, parts=C, w=L, off=0):
                return bank(n, parts, off + w * b, off + w * b + w)

            def flat(x):
                return x.rearrange("p b t -> p (b t)")

            def turned(n, y, y_ok, pair):
                for b in range(2):
                    pe.wait_ge(y_ok, after(pair, 2, b + 1))
                    r = back_to(half(n, b), y[:, b, :])
                return r

            def probs_T(j, t):
                b, c = t // 4, t % 4
                if t == 0:
                    pe.wait_ge(x4_ok, after(j - 1, 1))
                elif t == 1:
                    pe.wait_ge(y3T_ok, after(j - 1, 2))
                elif t == 5:
                    pe.wait_ge(ocT_ok, after(j, 2, 1))
                else:
                    pe.wait_ge(pcT_ok, after(j, 8, t if t == 4 else t - 1))
                pe.wait_ge(P_ok, after(j, 8, t + 1))
                for n in range(4):
                    r = back_to(bank(PCT_BANK[t], LC, L * n, L * n + L), P[:, b, 4 * c + n, :])
                r.then_inc(pe_pcT, 1)

            def cross_values(j, b):
                if b == 0:
                    pe.wait_ge(vbdc_ok, after(j, 1))
                pe.wait_ge(pcT_ok, after(j, 8, 4 * b + 4))
                for n in range(4):
                    for gq in range(NG):
                        r = mm(ps[32 * gq:32 * gq + 32, 512 * OC_BANK[b]:512 * OC_BANK[b] + L],
                               vbdc[:, b * NG + gq, n, :], pcT[:, 4 * gq + n, :], n == 0, n == 3)
                r.then_inc(pe_o2, 1)

            def expert_in(e):
                for c in range(2):
                    for s, x in enumerate((nxT, evT)):
                        r = mm(bank(E_BANK[e], C, TP * c, TP * c + TP), ew1[:, e, s, C * c:C * c + C], flat(x),
                               s == 0, s == 1)
                return r

            def experts_out(i, b):
                pe.wait_ge(h0_ok, after(i, 4))
                pe.wait_ge(h1_ok, after(i, 4))
                pe.wait_ge(h2_ok, after(i, 4))
                pe.wait_ge(prT_ok, after(i, 1))
                if b == 0:
                    pe.wait_ge(gs_ok, after(i, 2))
                else:
                    pe.wait_ge(th_ok, after(i, 1))
                for e in range(NE):
                    for c in range(2):
                        mm(bank(Y_BANK[b], L, C * e, C * e + C), hT[:, 2 * e + c, b, :], ew2o[:, 2 * e + c, :],
                           c == 0, c == 1)
                mm(bank(Y_BANK[b], L, C * NE, C * NE + C), prT[:, b, :], mixh[:, :]).then_inc(pe_y, 1)

            def window_scores(w, t):
                pe.wait_ge(q1T_ok, after(w, 1))
                pe.wait_ge(kbd1_in, after(w, 16 * NH))
                b, q = t // 2, t % 2
                if t == 0:
                    pe.wait_ge(vcA_ok, after(w, 1))
                elif t == 2:
                    pe.wait_ge(v1_ok, after(w, 2))
                elif t == 3:
                    pe.wait_ge(d1_ok, after(w, 4, 1))
                for h in range(2):
                    n = S1_BANK[t]
                    r = mm(ps[64 * h:64 * h + 64, 512 * n:512 * n + 512], q1T[:, b, WIN * h:WIN * h + WIN],
                           kbd1[:, b, 8 * q:8 * q + 8, WIN * h:WIN * h + WIN])
                r.then_inc(pe_S1, 1)

            def window_T(w, t):
                b, q = t // 2, t % 2
                if t < 3:
                    pe.wait_ge(d1_ok, after(w, 4, t + 2))
                else:
                    pe.wait_ge(p1T_ok, after(w, 4, 1))
                pe.wait_ge(E1_ok, after(w, 4, t + 1))
                for n in range(4):
                    h = 8 * q + 2 * n
                    r = back_to(bank(P1T_BANK[t], 128, L * n, L * n + L),
                                d1[:, b, h:h + 2, :].rearrange("p h k -> p (h k)"))
                r.then_inc(pe_p1T, 1)

            def window_values(w):
                pe.wait_ge(v1_ok, after(w, 2))
                pe.wait_ge(p1T_ok, after(w, 4))
                for off in (0, TP):
                    for b in range(2):
                        for h in range(2):
                            for q in range(2):
                                for gq in range(NG):
                                    o = 512 * 5 + off + L * b + WIN * h
                                    lhsT = ones1[:, q, :] if off else vbd1[:, (2 * b + h) * NG + gq, q, :]
                                    r = mm(ps[32 * gq:32 * gq + 32, o:o + WIN], lhsT,
                                           p1T[:, b, 2 * gq + q, WIN * h:WIN * h + WIN], q == 0, q == 1)
                r.then_inc(pe_o1, 1)

            def swiglu_in(c):
                n = M1_BANK[c]
                mm(bank(n, C, 0, TP), wm1[:, C * c:C * c + C], flat(h3T))
                mm(bank(n, C, TP, 2 * TP), wm1[:, HID + C * c:HID + C * c + C], flat(h3T)).then_inc(pe_m1, 1)

            def cross_scores(w, t):
                b, c = t // 4, t % 4
                if t == 0:
                    pe.wait_ge(xA_ok, after(w, 1))
                elif t == 1:
                    pe.wait_ge(h2T_ok, after(w, 2))
                elif t > 2:
                    pe.wait_ge(S_ok, after(w, 8, t - 2))
                if t == 0:
                    pe.wait_ge(kbdc_in, after(w, 16 * NH))
                    pe.wait_ge(qcT_ok, after(w, 1))
                mm(bank(SC_BANK[t], L, 0, 4 * LC), qcT[:, b, :], kbdc[:, b, 4 * c:4 * c + 4, :]
                   .rearrange("p h k -> p (h k)")).then_inc(pe_Sc, 1)

            def window_qk(w):
                pe.wait_ge(S_ok, after(w - 1, 8, 7))
                pe.wait_ge(h1T_ok, after(w, 2))
                mm(bank(4, C, 0, TP), wqkv[:, 0, :], flat(h1T))
                mm(bank(4, C, TP, 2 * TP), wqkv[:, 1, :], flat(h1T)).then_inc(pe_qk1, 1)

            def cross_kv(w):
                pe.wait_ge(S_ok, after(w - 1, 8, 6))
                pe.wait_ge(cT_ok, after(w, 1))
                mm(bank(3, C, 0, 2 * LC), wkv[:, 0, :], flat(cT))
                for b in range(2):
                    r = mm(half(3, b, LC, C, 2 * LC), cT[:, b, :], wkv[:, 1, :])
                r.then_inc(pe_ckv, 1)

            def window_v(w):
                pe.wait_ge(S_ok, after(w - 1, 8))
                pe.wait_ge(h1T_ok, after(w, 2))
                for b in range(2):
                    for q in range(2):
                        for h in range(2):
                            o = 512 * 5 + C * (2 * b + q)
                            r = mm(ps[64 * h:64 * h + 64, o:o + C], h1T[:, b, WIN * q:WIN * q + WIN], wqkv[:, 2, :])
                r.then_inc(pe_v1, 1)

            def inputs_T(i):
                pe.wait_ge(t2_ok, after(i - 1, 2))
                pe.wait_ge(c0_in, after(i, 16))
                for b in range(2):
                    back_to(half(0, b, C, LC, TP), c0[:, b, :])
                turned(0, z0, z0_ok, i).then_inc(pe_z0, 1)

            def prototypes_qk(i):
                pe.wait_ge(dl_ok, after(i - 1, 1))
                pe.wait_ge(nxT_ok, after(i, 1))
                mm(bank(1, C, 0, TP), Wq0[:, :], flat(nxT))
                pe.wait_ge(cT_ok, after(i, 1))
                mm(bank(1, C, TP, TP + 2 * LC), Wk0[:, :], flat(cT)).then_inc(pe_q0, 1)

            def prototypes_v(i):
                pe.wait_ge(h1T_ok, after(i - 1, 2))
                pe.wait_ge(cT_ok, after(i, 1))
                for b in range(2):
                    r = mm(half(2, b, LC), cT[:, b, :], Wv0[:, :])
                r.then_inc(pe_v0, 1)

            def prototypes_scores(i):
                pe.wait_ge(cT_ok, after(i, 1))
                pe.wait_ge(nxT_ok, after(i, 1))
                pe.wait_ge(k0T_ok, after(i, 1))
                for b in range(2):
                    r = mm(half(0, b, L, LC), q0T[:, b, :], k0T[:, b, :])
                r.then_inc(pe_S0, 1)

            def prototypes_T(i):
                pe.wait_ge(P0n_ok, after(i, 1))
                for b in range(2):
                    r = back_to(half(1, b, LC), P0n[:, b, :])
                r.then_inc(pe_P0T, 1)

            def evidence(i):
                pe.wait_ge(v0_ok, after(i, 1))
                pe.wait_ge(P0T_ok, after(i, 1))
                for b in range(2):
                    r = mm(half(2, b), v0[:, b, :], P0T[:, b, :])
                r.then_inc(pe_ev, 1)

            def router(i):
                pe.wait_ge(P0_ok, after(i, 2))
                mm(bank(0, NE, 0, TP), rw[:, 0, :], flat(nxT), True, False)
                pe.wait_ge(evT_ok, after(i, 1))
                mm(bank(0, NE, 0, TP), rw[:, 1, :], flat(evT), False, True).then_inc(pe_rl, 1)

            def router_T(i):
                pe.wait_ge(P0T_ok, after(i, 1))
                for b in range(2):
                    pe.wait_ge(rlT_ok, after(i, 2, b + 1))
                    pe.sem_inc(passed, 1)
                    r = back_to(half(1, b, L, NE), rlT[:, b, :])
                r.then_inc(pe_rlt, 1)

            def gate_in(i):
                pe.wait_ge(h0_ok, after(i, 4))
                for s, x in enumerate((nxT, evT)):
                    r = mm(bank(2, C, 0, TP), gw1[:, s, :], flat(x), s == 0, s == 1)
                r.then_inc(pe_g1, 1)

            def shares_T(i):
                pe.wait_ge(h2_ok, after(i, 4))
                pe.wait_ge(pr_ok, after(i, 1))
                for b in range(2):
                    r = back_to(half(1, b, NE + 1), pr[:, b, :])
                r.then_inc(pe_prT, 1)

            def gate_out(i):
                pe.wait_ge(h1_ok, after(i, 4))
                pe.wait_ge(gs_ok, after(i, 2))
                mm(bank(0, C, 0, TP), gw2[:, :], flat(gs)).then_inc(pe_g2, 1)

            def gate_T(i):
                pe.wait_ge(th_ok, after(i, 1))
                for b in range(2):
                    r = back_to(half(1, b, L, C), th[:, b, :])
                r.then_inc(pe_thT, 1)

            def body(i, live):
                i1, i2, i3 = i - 1, i - 2, i - 3
                if 2 in live:
                    cross_scores(i2, 7)
                if 1 in live:
                    pe.wait_ge(t2_ok, after(i1, 2, 1))
                    turned(2, z1, z1_ok, i1).then_inc(pe_z1, 1)
                    window_qk(i1)
                if 2 in live:
                    probs_T(i2, 0)
                    probs_T(i2, 1)
                    probs_T(i2, 2)
                    probs_T(i2, 3)
                if 1 in live:
                    window_v(i1)
                if 2 in live:
                    cross_values(i2, 0)
                    probs_T(i2, 4)
                    probs_T(i2, 5)
                    probs_T(i2, 6)
                if 1 in live:
                    window_scores(i1, 0)
                    window_scores(i1, 1)
                if 2 in live:
                    probs_T(i2, 7)
                if 1 in live:
                    window_scores(i1, 2)
                if 2 in live:
                    cross_values(i2, 1)
                if 1 in live:
                    window_scores(i1, 3)
                    window_T(i1, 0)
                    window_T(i1, 1)
                if 2 in live:
                    pe.wait_ge(ocT_ok, after(i2, 2))
                    pe.wait_ge(pcT_ok, after(i2, 8))
                    mm(bank(6, C, 0, TP), wco[:, :], flat(ocT)).then_inc(pe_y2, 1)
                if 0 in live:
                    inputs_T(i)
                if 1 in live:
                    window_T(i1, 2)
                    window_T(i1, 3)
                if 2 in live:
                    turned(7, y2T, y2T_ok, i2).then_inc(pe_y2t, 1)
                if 1 in live:
                    window_values(i1)
                if 0 in live:
                    prototypes_qk(i)
                if 2 in live:
                    pe.wait_ge(y2T_ok, after(i2, 2))
                    turned(6, z3, z3_ok, i2).then_inc(pe_z3, 1)
                if 1 in live:
                    pe.wait_ge(o1T_ok, after(i1, 1))
                    mm(bank(3, C, 0, TP), wso[:, :], flat(o1T)).then_inc(pe_y1, 1)
                if 0 in live:
                    prototypes_scores(i)
                if 1 in live:
                    turned(4, y1T, y1T_ok, i1).then_inc(pe_y1t, 1)
                if 2 in live:
                    pe.wait_ge(x3_ok, after(i2, 1))
                    pe.wait_ge(h3T_ok, after(i2, 2))
                    swiglu_in(0)
                if 0 in live:
                    prototypes_v(i)
                if 2 in live:
                    pe.wait_ge(h3T_ok, after(i2, 2))
                    swiglu_in(1)
                    pe.wait_ge(u_ok, after(i2, 4, 1))
                    swiglu_in(2)
                if 1 in live:
                    pe.wait_ge(o1T_ok, after(i1, 1))
                    turned(5, z2, z2_ok, i1).then_inc(pe_z2, 1)
                if 2 in live:
                    pe.wait_ge(u_ok, after(i2, 4, 2))
                    swiglu_in(3)
                if 1 in live:
                    pe.wait_ge(y1T_ok, after(i1, 2))
                    pe.wait_ge(h2T_ok, after(i1, 2))
                    mm(bank(3, C, 0, TP), wq[:, :], flat(h2T)).then_inc(pe_qc, 1)
                    cross_scores(i1, 0)
                if 2 in live:
                    pe.wait_ge(u_ok, after(i2, 4))
                    for c in range(HID // C):
                        r = mm(bank(7, C, 0, TP), wm2[:, c, :], u[:, c, :], c == 0, c == HID // C - 1)
                    r.then_inc(pe_y3, 1)
                if 1 in live:
                    cross_scores(i1, 1)
                    cross_scores(i1, 2)
                    cross_scores(i1, 3)
                    cross_scores(i1, 4)
                if 0 in live:
                    prototypes_T(i)
                if 1 in live:
                    cross_scores(i1, 5)
                if 0 in live:
                    evidence(i)
                if 2 in live:
                    turned(6, y3T, y3T_ok, i2).then_inc(pe_y3t, 1)
                if 0 in live:
                    router(i)
                    pe.wait_ge(evT_ok, after(i, 1))
                    expert_in(0).then_inc(pe_e0, 1)
                    router_T(i)
                    pe.wait_ge(rlT_ok, after(i, 2))
                    expert_in(1).then_inc(pe_e1, 1)
                    pe.wait_ge(re_ok, after(i, 1))
                    expert_in(2).then_inc(pe_e2, 1)
                    gate_in(i)
                    cross_kv(i)
                    shares_T(i)
                    gate_out(i)
                    experts_out(i, 0)
                    experts_out(i, 1)
                if 1 in live:
                    cross_scores(i1, 6)
                if 0 in live:
                    gate_T(i)

            iterations(pe, body)


def kernel(**inputs):
    import numpy as _np
    import concourse.bacc as _bacc
    from concourse import mybir as _mybir
    from concourse.bass_utils import run_bass_kernel_spmd as _run

    nc = _bacc.Bacc("TRN2", target_bir_lowering=False, num_devices=1)
    arrays, aps = {}, {}
    for name, value in inputs.items():
        a = _np.ascontiguousarray(value)
        arrays[f"in_{name}"] = a
        aps[name] = nc.dram_tensor(f"in_{name}", a.shape, _mybir.dt.from_np(a.dtype), kind="ExternalInput").ap()
    shape = inputs["x"].shape
    out = nc.dram_tensor("out_0", shape, _mybir.dt.float32, kind="ExternalOutput").ap()
    pixart_layers_kernel(nc, aps, out)
    r = _run(nc, [arrays], core_ids=[0])
    return r.results[0]["out_0"]
```

```python
from contextlib import ExitStack

import concourse.bass as bass
from concourse import mybir


def pixart_layers_kernel(nc: bass.Bass, I, out: bass.AP):
    f32 = mybir.dt.float32
    ALU = mybir.AluOpType
    ACT = mybir.ActivationFunctionType
    AX = mybir.AxisListType

    NB, L, C = I["x"].shape
    LC = I["ctx_1024"].shape[1]
    PAIRS = NB // 2
    TP = 2 * L
    NE, _, RH = I["L0_xcond_e_w1"].shape
    NH = 16
    D = C // NH
    WIN, SHIFT, TOPK = 64, 32, 16
    HID = I["L1_xcond_w_m2"].shape[0]
    NG = C // 32
    EPS0, EPS1 = 1e-5, 1e-6
    SC0, SC1 = float(C) ** -0.5, float(D) ** -0.5
    GONE = -1.0e30

    rows = {}
    n_rows = 0
    for name, n in (("e_b1", NE * RH // C), ("gate_b1", 1), ("gate_b2", 1),
                    ("b_ada", 9), ("b_qkv", 3), ("b_so", 1), ("b_q", 1), ("b_kv", 2), ("b_co", 1),
                    ("b_m1", 2 * HID // C), ("b_m2", 1), ("cond", NB), ("e_b2", NE)):
        rows[name] = n_rows
        n_rows += n

    MODS = ["EB0", "EB1", "EB2", "EB3", "EB4", "EB5", "GB", "RL", "SC1", "SH1", "G1", "BG1", "SC2", "SH2",
            "G2", "BG2", "SC3", "SH3", "G3", "BG3"]
    MOD = {m: n for n, m in enumerate(MODS)}
    NM, NW, NBK = len(MODS), MOD["G1"], MOD["G2"]

    ctx = ExitStack()
    with ctx:
        def sb(name, *shape):
            return ctx.enter_context(nc.sbuf_tensor(name, list(shape), f32))

        rowt = sb("rowt", n_rows, C)
        lncol = sb("lncol", C, 2)
        cols = sb("cols", C, n_rows)
        ident = sb("ident", 128, 128)
        Wq0, Wk0, Wv0 = sb("Wq0", C, C), sb("Wk0", C, C), sb("Wv0", C, C)
        rw = sb("rw", C, 3, NE)
        rb = sb("rb", NE, 1)
        ew1 = sb("ew1", C, NE, 3, RH)
        ew2o = sb("ew2o", C, NE * 2, C)
        outw = sb("outw", C, C)
        gw1 = sb("gw1", C, 3, C)
        gw2 = sb("gw2", C, C)
        mixb = sb("mixb", NE + 1, C)
        mixh = sb("mixh", C, C)
        wqkv = sb("wqkv", C, 3, C)
        wso, wq, wkv, wco = sb("wso", C, C), sb("wq", C, C), sb("wkv", C, 2, C), sb("wco", C, C)
        wm1 = sb("wm1", C, 2 * HID)
        wm2 = sb("wm2", C, HID // C, C)
        scond = sb("scond", C, NB)
        modT = sb("modT", C, 9, NB)
        modall = sb("modall", C, PAIRS, NM, 2)
        gb2h = sb("gb2h", C, 1)
        mhalf, minus = sb("mhalf", 128, 2), sb("minus", 128, 2)
        modm = sb("modm", C, NW, 2)
        modw = sb("modw", C, NBK - NW, 2)
        modb = sb("modb", C, NM - NBK, 2)
        bso = sb("bso", C, 1)

        x0 = sb("x0", L, 2, C)
        c0 = sb("c0", LC, 2, C)
        st0, mv0, ln0 = sb("st0", L, 2, 6), sb("mv0", L, 2, 2), sb("ln0", L, 4, 2)
        z0 = sb("z0", L, 2, C)
        nxT = sb("nxT", C, 2, L)
        cT = sb("cT", C, 2, LC)
        q0T = sb("q0T", C, 2, L)
        k0T = sb("k0T", C, 2, LC)
        kcT = sb("kcT", C, 2, LC)
        v0 = sb("v0", LC, 2, C)
        vcA, vcM, vcB = sb("vcA", LC, 2, C), sb("vcM", LC, 2, C), sb("vcB", LC, 2, C)
        m0, nm0, l0, r0 = sb("m0", L, 2), sb("nm0", L, 2), sb("l0", L, 2), sb("r0", L, 2)
        P0 = sb("P0", L, 2, LC)
        P0n = sb("P0n", L, 2, LC)
        P0T = sb("P0T", LC, 2, L)
        evT = sb("evT", C, 2, L)
        rlT = sb("rlT", NE, 2, L)
        rm, re, rx = sb("rm", L, 2), sb("re", L, 2, NE), sb("rx", L, 2, NE)
        rs, rr = sb("rs", L, 2), sb("rr", L, 2)
        pr = sb("pr", L, 2, NE + 1)
        prT = sb("prT", C, 2, L)
        hT = sb("hT", C, NE * 2, 2, L)
        gs = sb("gs", C, 2, L)
        th = sb("th", C, 2, L)
        zb = sb("zb", L, 2, C)
        t0, t1, t2, dl = sb("t0", L, 2, C), sb("t1", L, 2, C), sb("t2", L, 2, C), sb("dl", L, 2, C)
        x1 = sb("x1", L, 2, C)
        st1, mv1, ln1 = sb("st1", L, 2, 6), sb("mv1", L, 2, 2), sb("ln1", L, 4, 2)
        z1 = sb("z1", L, 2, C)
        h1T = sb("h1T", C, 2, L)
        q1T = sb("q1T", C, 2, L)
        k1T = sb("k1T", C, 2, L)
        kbd1 = sb("kbd1", C, 2, NH, L)
        vbd1 = sb("vbd1", 128, 2 * 2 * NG, 2, 32)
        m1 = sb("m1", L, 2, NH)
        d1 = sb("d1", L, 2, NH, WIN)
        ones1 = sb("ones1", 128, 2, 32)
        r1 = sb("r1", C, 2, L)
        x1w = sb("x1w", L, 2, C)
        p1T = sb("p1T", 128, 2, NH // 2, L)
        o1T = sb("o1T", C, 2, L)
        y1T = sb("y1T", C, 2, L)
        xA, xM, xB = sb("xA", L, 2, C), sb("xM", L, 2, C), sb("xB", L, 2, C)
        st2, mv2, ln2 = sb("st2", L, 2, 6), sb("mv2", L, 2, 2), sb("ln2", L, 4, 2)
        z2 = sb("z2", L, 2, C)
        h2T = sb("h2T", C, 2, L)
        qcT = sb("qcT", C, 2, L)
        kbdc = sb("kbdc", C, 2, NH, LC)
        S = sb("S", L, 2, NH, LC)
        Sb = sb("Sb", L, NH, LC)
        S1 = sb("S1", L, 4, LC)
        top = sb("top", L, 2, NH, TOPK)
        tops = sb("tops", L, NH, TOPK)
        lc, rc = sb("lc", L, NH), sb("rc", L, NH)
        E_ = sb("E_", L, NH, LC)
        P = sb("P", L, 2, NH, LC)
        ew2 = E_[:, 0:7, :].rearrange("p h k -> p (h k)")[:, 0:6 * C].rearrange("p (k n) -> p k n", n=C)
        ew2T = E_[:, 8:15, :].rearrange("p h k -> p (h k)")[:, 0:6 * C].rearrange("p (k n) -> p k n", n=C)
        wada = P[:, 0, 0:10, :].rearrange("p h k -> p (h k)")[:, 0:9 * C].rearrange("p (k n) -> p k n", n=C)
        vbdc = sb("vbdc", LC, 2 * NG, 4, 32)
        pcT = sb("pcT", LC, NH, L)
        ocT = sb("ocT", C, 2, L)
        y2T = sb("y2T", C, 2, L)
        x3 = sb("x3", L, 2, C)
        st3, mv3, ln3 = sb("st3", L, 2, 6), sb("mv3", L, 2, 2), sb("ln3", L, 4, 2)
        z3 = sb("z3", L, 2, C)
        h3T = sb("h3T", C, 2, L)
        sa = sb("sa", C, HID // C, TP)
        u = sb("u", C, HID // C, TP)
        y3T = sb("y3T", C, 2, L)
        x4 = sb("x4", L, 2, C)

        ps = ctx.enter_context(nc.psum_tensor("ps", [128, 8 * 512], f32))

        def bank(n, parts=128, a=0, b=512):
            return ps[0:parts, 512 * n + a:512 * n + b]

        def two(ap):
            return ap.rearrange("p (b t) -> p b t", b=2)

        def one(name):
            return ctx.enter_context(nc.semaphore(name))

        def sems(names):
            return [ctx.enter_context(nc.semaphore(n)) for n in names.split()]

        def after(pair, per, part=None):
            value = per * pair + (per if part is None else part)
            return max(value, 0) if isinstance(value, int) else value

        x0_in, = sems("x0_in")
        c0_in, v_b, v_m, x_b, x_m = sems("c0_in v_b v_m x_b x_m")
        x4_out, = sems("x4_out")
        kbd1_in, kbdc_in = sems("kbd1_in kbdc_in")
        pe_z0, pe_q0, pe_v0, pe_S0, pe_P0T, pe_ev, pe_rl = sems("pe_z0 pe_q0 pe_v0 pe_S0 pe_P0T pe_ev pe_rl")
        pe_rlt, pe_e0, pe_e1, pe_e2, pe_g1, pe_prT, pe_g2 = sems("pe_rlt pe_e0 pe_e1 pe_e2 pe_g1 pe_prT pe_g2")
        pe_thT, pe_z1, pe_ckv, pe_qk1, pe_v1, pe_o1, pe_y1 = sems("pe_thT pe_z1 pe_ckv pe_qk1 pe_v1 pe_o1 pe_y1")
        pe_y1t, pe_z2, pe_qc, pe_y2, pe_y2t, pe_z3, pe_y3 = sems("pe_y1t pe_z2 pe_qc pe_y2 pe_y2t pe_z3 pe_y3")
        pe_y3t, = sems("pe_y3t")
        pe_y, pe_o2 = sems("pe_y pe_o2")
        pe_Sc, pe_pcT = sems("pe_Sc pe_pcT")
        pe_m1, pe_S1, pe_p1T = sems("pe_m1 pe_S1 pe_p1T")
        nxT_ok, cT_ok, q0T_ok, k0T_ok, kcT_ok, v0_ok, vcA_ok = sems("nxT_ok cT_ok q0T_ok k0T_ok kcT_ok v0_ok vcA_ok")
        P0T_ok, evT_ok, rx_ok, th_ok, prT_ok, q1T_ok, k1T_ok = sems("P0T_ok evT_ok rx_ok th_ok prT_ok q1T_ok k1T_ok")
        qcT_ok, = sems("qcT_ok")
        P0_ok, rlT_ok, gs_ok, zb_ok, h1T_ok, v1_ok, y1T_ok = sems("P0_ok rlT_ok gs_ok zb_ok h1T_ok v1_ok y1T_ok")
        h2T_ok, tops_ok, ocT_ok, y2T_ok, h3T_ok, y3T_ok = sems("h2T_ok tops_ok ocT_ok y2T_ok h3T_ok y3T_ok")
        h0_ok, h1_ok, h2_ok, sa_ok, ub_ok, E1_ok, p1T_ok = sems("h0_ok h1_ok h2_ok sa_ok ub_ok E1_ok p1T_ok")
        S_ok, E_ok, pcT_ok = sems("S_ok E_ok pcT_ok")
        mv0_ok, m0_ok, nm0_ok, r0_ok, rm_ok, re_ok, rs_ok = sems("mv0_ok m0_ok nm0_ok r0_ok rm_ok re_ok rs_ok")
        rr_ok, pr_ok, dl_ok, x1_ok, mv1_ok, x1w_ok, r1_ok = sems("rr_ok pr_ok dl_ok x1_ok mv1_ok x1w_ok r1_ok")
        o1T_ok, xA_ok, mv2_ok, vbdc_ok, x3_ok, mv3_ok, x4_ok = sems("o1T_ok xA_ok mv2_ok vbdc_ok x3_ok mv3_ok x4_ok")
        st0_ok, st1_ok, st2_ok, st3_ok, z0_ok, z1_ok, z2_ok = sems("st0_ok st1_ok st2_ok st3_ok z0_ok z1_ok z2_ok")
        z3_ok, t0_ok, t1_ok, t2_ok, lc_ok, rc_ok = sems("z3_ok t0_ok t1_ok t2_ok lc_ok rc_ok")
        P0n_ok, = sems("P0n_ok")
        u_ok, m1_ok, d1_ok = sems("u_ok m1_ok d1_ok")
        sel_ok, = sems("sel_ok")
        max1_ok, rep1_ok, max2_ok, rep2_ok = sems("max1_ok rep1_ok max2_ok rep2_ok")
        modm_ok, modw_ok, modb_ok = sems("modm_ok modw_ok modb_ok")
        tsub_ok, = sems("tsub_ok")
        ln0_ok, ln1_ok, ln2_ok, ln3_ok = sems("ln0_ok ln1_ok ln2_ok ln3_ok")
        sub_ok, P_ok = sems("sub_ok P_ok")

        id0, id_ok, zero_ok = one("id0"), one("id_ok"), one("zero_ok")

        passed = one("passed")

        w_rows, w_ln, w_qkv0, w_fold = one("w_rows"), one("w_ln"), one("w_qkv0"), one("w_fold")
        w_small, w_big = one("w_small"), one("w_big")
        mixb_in = one("mixb_in")
        su_pe, su_act, su_dve = one("su_pe"), one("su_act"), one("su_dve")
        mods_ok, ones0, half_ok = one("mods_ok"), one("ones0"), one("half_ok")

        DEPTH = 4

        def iterations(eng, body):
            for i in range(DEPTH):
                body(i, range(i + 1))
            with eng.Fori(DEPTH, PAIRS) as i:
                body(i, range(DEPTH))
            for i in range(PAIRS, PAIRS + DEPTH - 1):
                body(i, range(i - PAIRS + 1, DEPTH))

        S1_BANK = [3, 4, 5, 3]
        P1T_BANK = [4, 5, 3, 4]
        SC_BANK = [4 + t if t < 2 else 3 + (t - 2) % 3 for t in range(8)]
        PCT_BANK = [6, 7, 6, 7, 7, 6, 7, 6]
        OC_BANK = [6, 7]
        E_BANK = [2, 0, 1]
        Y_BANK = [2, 0]
        M1_BANK = [7, 6, 7, 6]
        N_MODS = NE * 2 + 2 + 12
        N_ZERO = 8
        N_ROW_LOADS, N_SMALL, N_BIG = 13, 8, 5

        def col(name, n=0):
            return cols[:, rows[name] + n:rows[name] + n + 1]

        def diagonal(t, part, parts, off, dims):
            pitch = 1
            for n in list(t.shape)[1:]:
                pitch *= n
            return bass.AP(t, part * pitch + off, [[pitch, parts]] + dims)

        block = ctx.enter_context(nc.Block())

        @block.sync
        def _(sp):
            def row(name, src):
                n = src.shape[0]
                sp.dma_start(rowt[rows[name]:rows[name] + n, :], src).then_inc(w_rows, 16)

            def vec(name, key):
                row(name, I[key].rearrange("(r c) -> r c", c=C))

            def load(i):
                xs = I["x"][bass.ds(2 * i, 2), :, :].rearrange("b t d -> t b d")
                cs = I["ctx_1024"][bass.ds(2 * i, 2), :, :].rearrange("b t d -> t b d")
                sp.wait_ge(x1_ok, after(i - 1, 1))
                sp.wait_ge(z0_ok, after(i - 1, 2))
                sp.wait_ge(pe_z0, after(i - 1, 1))
                sp.dma_start(x0[0:L - SHIFT, :, :], xs[SHIFT:L, :, :]).then_inc(x0_in, 16)
                sp.dma_start(x0[L - SHIFT:L, :, :], xs[0:SHIFT, :, :]).then_inc(x0_in, 16)
                sp.dma_start(c0[:, :, :], cs).then_inc(c0_in, 16)

            def ln_columns():
                for n, key in enumerate(("ln_gamma", "ln_beta")):
                    sp.dma_start(lncol[:, n:n + 1], I["L0_xcond_" + key].rearrange("(p o) -> p o", o=1)) \
                        .then_inc(w_ln, 16)

            def bias_rows():
                row("e_b1", I["L0_xcond_e_b1"].rearrange("e (r c) -> (e r) c", c=C))
                vec("gate_b1", "L0_xcond_gate_b1")
                vec("gate_b2", "L0_xcond_gate_b2")
                vec("b_ada", "L1_xcond_b_ada")
                vec("b_qkv", "L1_xcond_b_qkv")
                vec("b_so", "L1_xcond_b_so")
                vec("b_q", "L1_xcond_b_q")
                vec("b_kv", "L1_xcond_b_kv")
                vec("b_co", "L1_xcond_b_co")
                vec("b_m1", "L1_xcond_b_m1")
                vec("b_m2", "L1_xcond_b_m2")
                row("cond", I["cond_1024"])
                row("e_b2", I["L0_xcond_e_b2"])

            def spread(dst, src, moved):
                for h in range(NH):
                    sp.dma_start(dst[D * h:D * h + D, :, h, :], src[D * h:D * h + D, :, :]).then_inc(moved, 16)

            def window_keys(w):
                sp.wait_ge(k1T_ok, after(w, 1))
                sp.wait_ge(pe_S1, after(w - 1, 4))
                spread(kbd1, k1T, kbd1_in)

            def cross_keys(w):
                sp.wait_ge(kcT_ok, after(w, 1))
                sp.wait_ge(pe_Sc, after(w - 1, 8))
                spread(kbdc, kcT, kbdc_in)

            def values_to_M(w):
                sp.wait_ge(vcA_ok, after(w, 1))
                sp.wait_ge(v_b, after(w - 1, 16))
                sp.dma_start(vcM[:, :, :], vcA[:, :, :]).then_inc(v_m, 16)

            def values_to_B(k):
                sp.wait_ge(v_m, after(k, 16))
                sp.wait_ge(vbdc_ok, after(k - 1, 1))
                sp.dma_start(vcB[:, :, :], vcM[:, :, :]).then_inc(v_b, 16)

            def x_to_M(w):
                sp.wait_ge(xA_ok, after(w, 1))
                sp.wait_ge(x_b, after(w - 1, 16))
                sp.dma_start(xM[:, :, :], xA[:, :, :]).then_inc(x_m, 16)

            def x_to_B(k):
                sp.wait_ge(x_m, after(k, 16))
                sp.wait_ge(x3_ok, after(k - 1, 1))
                sp.dma_start(xB[:, :, :], xM[:, :, :]).then_inc(x_b, 16)

            def store(j):
                sp.wait_ge(x4_ok, after(j, 1))
                os = out[bass.ds(2 * j, 2), :, :].rearrange("b t d -> t b d")
                sp.dma_start(os[SHIFT:L, :, :], x4[0:L - SHIFT, :, :]).then_inc(x4_out, 16)
                sp.dma_start(os[0:SHIFT, :, :], x4[L - SHIFT:L, :, :]).then_inc(x4_out, 16)

            def body(i, live):
                i1, i2, i3 = i - 1, i - 2, i - 3
                if 3 in live:
                    x_to_B(i3)
                if 2 in live:
                    values_to_M(i2)
                if 0 in live:
                    load(i)
                    if live == range(1):
                        ln_columns()
                        bias_rows()
                if 2 in live:
                    values_to_B(i2)
                if 1 in live:
                    window_keys(i1)
                if 2 in live:
                    x_to_M(i2)
                if 1 in live:
                    cross_keys(i1)
                if 3 in live:
                    store(i3)

            iterations(sp, body)
            sp.wait_ge(x4_out, after(PAIRS - 1, 32))

        @block.gpsimd
        def _(pool):
            g = nc.gpsimd
            g.memset(ident[:, :], 0.0).then_inc(id0, 1)
            pool.wait_ge(id0, 1)
            g.affine_select(out=ident[:, :], in_=ident[:, :], compare_op=ALU.not_equal, fill=1.0, base=0,
                            pattern=[[-1, 128]], channel_multiplier=1).then_inc(id_ok, 1)
            for dst, src in ((ew2[:, :, :], I["L0_xcond_e_w2"].rearrange("e (k p) n -> p (e k) n", p=C)),
                             (outw[:, :], I["L0_xcond_out_w"])):
                pool.dma_start(dst, src).then_inc(w_fold, 16)
            for dst, src in ((gw1[:, :, :], I["L0_xcond_gate_w1"].rearrange("(k p) n -> p k n", p=C)),
                             (gw2[:, :], I["L0_xcond_gate_w2"]),
                             (wada[:, :, :], I["L1_xcond_w_ada"].rearrange("p (k n) -> p k n", n=C)),
                             (wqkv[:, :, :], I["L1_xcond_w_qkv"].rearrange("p (k n) -> p k n", n=C)),
                             (wm1[:, :], I["L1_xcond_w_m1"])):
                pool.dma_start(dst, src).then_inc(w_big, 16)
            g.memset(mhalf[:, :], -0.5).then_inc(half_ok, 1)
            g.memset(minus[:, :], -1.0).then_inc(half_ok, 1)
            pool.wait_ge(half_ok, 2)

            def zeros():
                g.memset(mixh[:, :], 0.0).then_inc(zero_ok, 1)
                g.memset(prT[:, :, :], 0.0).then_inc(zero_ok, 1)
                g.memset(vbd1[:, :, :, :], 0.0).then_inc(zero_ok, 1)
                g.memset(vbdc[:, :, :, :], 0.0).then_inc(zero_ok, 1)
                g.memset(kbdc[:, :, :, :], 0.0).then_inc(zero_ok, 1)

            def normalise(mv_ok, ln_ok, z_ok, x, mv, ln, z, eps, pair):
                pool.wait_ge(mv_ok, after(pair, 1))
                pool.sem_inc(passed, 1)
                g.tensor_scalar(ln[:, 0, :], mv[:, :, 1], eps, None, ALU.add).then_inc(ln_ok, 1)
                g.tensor_tensor(ln[:, 1, :], mv[:, :, 0], minus[0:L, :], ALU.mult).then_inc(ln_ok, 1)
                pool.wait_ge(ln_ok, after(pair, 4, 1))
                g.tensor_tensor(ln[:, 2, :], ln[:, 0, :], mhalf[0:L, :], ALU.pow).then_inc(ln_ok, 1)
                pool.wait_ge(ln_ok, after(pair, 4, 3))
                g.tensor_tensor(ln[:, 3, :], ln[:, 1, :], ln[:, 2, :], ALU.mult).then_inc(ln_ok, 1)
                pool.wait_ge(ln_ok, after(pair, 4))
                pool.sem_inc(passed, 1)
                for b in range(2):
                    g.tensor_scalar(z[:, b, :], x[:, b, :], ln[:, 2, b:b + 1], ln[:, 3, b:b + 1], ALU.mult, ALU.add) \
                        .then_inc(z_ok, 1)

            def prototypes_norm(i):
                pool.wait_ge(r0_ok, after(i, 1))
                g.tensor_tensor(P0n[:, :, :], P0[:, :, :], r0[:, :, None].to_broadcast([L, 2, LC]), ALU.mult) \
                    .then_inc(P0n_ok, 1)

            def keep_x1(i):
                pool.wait_ge(x1_ok, after(i, 1))
                pool.wait_ge(xA_ok, after(i - 1, 1))
                pool.sem_inc(passed, 1)
                g.tensor_copy(x1w[:, :, :], x1[:, :, :]).then_inc(x1w_ok, 1)

            def swiglu(j, c):
                pool.wait_ge(sa_ok, after(j, 4, c + 1))
                pool.wait_ge(ub_ok, after(j, 4, c + 1))
                g.tensor_tensor(u[:, c, :], u[:, c, :], sa[:, c, :], ALU.mult).then_inc(u_ok, 1)

            def shift(pair, b, c):
                h = 4 * c
                pool.wait_ge(max1_ok, after(pair, 2 * NH, b * NH + h + 4))
                if b == 0:
                    pool.wait_ge(P_ok, after(pair - 1, 8, 4 + c + 1))
                else:
                    pool.wait_ge(P_ok, after(pair, 8, c + 1))
                g.tensor_tensor(E_[:, h:h + 4, :], S[:, b, h:h + 4, :],
                                top[:, b, h:h + 4, 0:1].to_broadcast([L, 4, LC]), ALU.subtract) \
                    .then_inc(sub_ok, 1)

            def shift_top(pair, b):
                pool.wait_ge(max2_ok, after(pair, 2 * NH, b * NH + NH))
                if b == 0:
                    pool.wait_ge(lc_ok, after(pair - 1, 2))
                else:
                    pool.wait_ge(lc_ok, after(pair, 2, 1))
                g.tensor_tensor(tops[:, :, :], top[:, b, :, :], top[:, b, :, 0:1].to_broadcast([L, NH, TOPK]),
                                ALU.subtract).then_inc(tsub_ok, 1)

            def norm_top(pair, b, c):
                h = 4 * c
                pool.wait_ge(rc_ok, after(pair, 2, b + 1))
                pool.wait_ge(sel_ok, after(pair, 8, 4 * b + c + 1))
                pool.wait_ge(pe_pcT, after(pair - 1, 8, 4 * b + c + 1))
                g.tensor_tensor(P[:, b, h:h + 4, :], E_[:, h:h + 4, :],
                                rc[:, h:h + 4, None].to_broadcast([L, 4, LC]), ALU.mult).then_inc(P_ok, 1)

            def columns(dst, copied, a, b, pair):
                g.tensor_copy(dst[:, :, :], modall[:, bass.ds(pair, 1), a:b, :].rearrange("p o m b -> p (o m) b")) \
                    .then_inc(copied, 1)

            def body(i, live):
                i1, i2, i3 = i - 1, i - 2, i - 3
                if 1 in live:
                    prototypes_norm(i1)
                if 2 in live:
                    keep_x1(i2)
                if 3 in live:
                    norm_top(i3, 0, 0)
                if 1 in live:
                    if live == range(2):
                        pool.wait_ge(mods_ok, N_MODS)
                    pool.wait_ge(h1T_ok, after(i1 - 1, 2))
                    columns(modm, modm_ok, 0, NW, i1)
                if 3 in live:
                    shift(i3, 1, 0)
                if 2 in live:
                    pool.wait_ge(h2T_ok, after(i2 - 1, 2))
                    columns(modw, modw_ok, NW, NBK, i2)
                if 3 in live:
                    norm_top(i3, 0, 1)
                    norm_top(i3, 0, 2)
                    shift(i3, 1, 1)
                    shift(i3, 1, 2)
                    norm_top(i3, 0, 3)
                    shift(i3, 1, 3)
                    shift_top(i3, 1)
                if 2 in live:
                    pool.wait_ge(pe_z2, after(i2 - 1, 1))
                    normalise(mv2_ok, ln2_ok, z2_ok, xA, mv2, ln2, z2, EPS1, i2)
                if 3 in live:
                    norm_top(i3, 1, 0)
                    norm_top(i3, 1, 1)
                    norm_top(i3, 1, 2)
                    norm_top(i3, 1, 3)
                if 1 in live:
                    pool.wait_ge(pe_z1, after(i1 - 1, 1))
                    normalise(mv1_ok, ln1_ok, z1_ok, x1, mv1, ln1, z1, EPS1, i1)
                if 2 in live:
                    shift(i2, 0, 0)
                if 3 in live:
                    pool.wait_ge(y3T_ok, after(i3 - 1, 2))
                    columns(modb, modb_ok, NBK, NM, i3)
                if 2 in live:
                    shift(i2, 0, 1)
                if 0 in live:
                    pool.wait_ge(pe_z0, after(i - 1, 1))
                    normalise(mv0_ok, ln0_ok, z0_ok, x0, mv0, ln0, z0, EPS0, i)
                    if live == range(1):
                        zeros()
                if 3 in live:
                    pool.wait_ge(pe_z3, after(i3 - 1, 1))
                    normalise(mv3_ok, ln3_ok, z3_ok, x3, mv3, ln3, z3, EPS1, i3)
                    swiglu(i3, 0)
                    swiglu(i3, 1)
                if 2 in live:
                    shift_top(i2, 0)
                if 3 in live:
                    swiglu(i3, 2)
                    swiglu(i3, 3)
                if 2 in live:
                    shift(i2, 0, 2)
                    shift(i2, 0, 3)

            iterations(pool, body)

        @block.vector
        def _(dve):
            v = nc.vector
            v.memset(modall[:, :, :, :], 0.0).then_inc(zero_ok, 1)
            v.memset(ones1[:, :, :], 0.0).then_inc(ones0, 1)
            dve.wait_ge(ones0, 1)
            for h in range(2):
                r = v.memset(diagonal(ones1, 64 * h, 64, D * h, [[32 + 2 * D, 2], [1, D]]), 1.0)
            r.then_inc(zero_ok, 1)
            dve.wait_ge(su_pe, 1)
            v.tensor_copy(ew2T[:, 0:4, :], bank(4).rearrange("p (k n) -> p k n", n=C)).then_inc(su_dve, 1)
            v.tensor_copy(ew2T[:, 4:6, :], bank(5, 128, 0, 256).rearrange("p (k n) -> p k n", n=C)).then_inc(su_dve, 1)

            def pairs(ap):
                return ap.rearrange("p (i b) -> p i b", b=2)

            def put(name, src, *a, parts=C):
                v.tensor_scalar(modall[0:parts, :, MOD[name], :], pairs(src), *a).then_inc(mods_ok, 1)

            def conditions():
                dve.wait_ge(su_pe, 3)
                v.tensor_copy(cols[:, :], bank(3, C, 0, n_rows)).then_inc(su_dve, 1)
                v.memset(kbd1[:, :, :, :], 0.0).then_inc(zero_ok, 1)
                dve.wait_ge(su_pe, 4)
                dve.wait_ge(su_dve, 3)
                dve.wait_ge(zero_ok, 1)
                for n in range(NE * 2):
                    put(f"EB{n}", bank(5, C, NB * n, NB * n + NB), col("e_b1", n), None, ALU.add)
                put("GB", bank(5, C, NB * 6, NB * 7), col("gate_b1"), None, ALU.add)
                dve.wait_ge(w_small, 16 * N_SMALL)
                put("RL", bank(5, NE, NB * 7, NB * 8), rb[:, 0:1], None, ALU.add, parts=NE)
                dve.wait_ge(su_pe, 5)
                v.tensor_tensor(modT[:, :, :], bank(4, C, 0, 9 * NB).rearrange("p (k b) -> p k b", b=NB),
                                cols[:, rows["b_ada"]:rows["b_ada"] + 9, None].to_broadcast([C, 9, NB]), ALU.add) \
                    .then_inc(su_dve, 1)
                v.tensor_tensor(bso[:, :], bank(4, C, 511, 512), col("b_so"), ALU.add).then_inc(su_dve, 1)
                dve.wait_ge(su_dve, 5)
                for n, b in ((1, bso[:, 0:1]), (2, col("b_co")), (3, col("b_m2"))):
                    t = 3 * (n - 1)
                    put(f"SH{n}", modT[:, t, :], 0.0, None, ALU.add)
                    put(f"SC{n}", modT[:, t + 1, :], 1.0, None, ALU.add)
                    put(f"G{n}", modT[:, t + 2, :], 0.0, None, ALU.add)
                    put(f"BG{n}", modT[:, t + 2, :], b, None, ALU.mult)

            def stats(x_ok, st_ok, mv_ok, x, st, mv, pair):
                for b in range(2):
                    if x_ok is not None:
                        dve.wait_ge(x_ok, after(pair, 1))
                    v.bn_stats(st[:, b, :], x[:, b, :]).then_inc(st_ok, 1)
                dve.wait_ge(st_ok, after(pair, 2))
                dve.sem_inc(passed, 1)
                for b in range(2):
                    r = v.bn_aggr(mv[:, b, :], st[:, b, :])
                r.then_inc(mv_ok, 1)

            def top16(pair, b, c):
                hs = range(4 * c, 4 * c + 4)
                dve.wait_ge(S_ok, after(pair, 8, 4 * b + c + 1))
                dve.sem_inc(passed, 1)
                for h in hs:
                    v.max(top[:, b, h, 0:8], S[:, b, h, :]).then_inc(max1_ok, 1)
                for h in hs:
                    dve.wait_ge(max1_ok, after(pair, 2 * NH, b * NH + h + 1))
                    dve.sem_inc(passed, 1)
                    v.match_replace(S1[:, h % 4, :], top[:, b, h, 0:8], S[:, b, h, :], GONE).then_inc(rep1_ok, 1)
                for h in hs:
                    dve.wait_ge(rep1_ok, after(pair, 2 * NH, b * NH + h + 1))
                    dve.sem_inc(passed, 1)
                    v.max(top[:, b, h, 8:16], S1[:, h % 4, :]).then_inc(max2_ok, 1)
                for h in hs:
                    dve.wait_ge(max2_ok, after(pair, 2 * NH, b * NH + h + 1))
                    dve.sem_inc(passed, 1)
                    v.match_replace(Sb[:, h, :], top[:, b, h, 8:16], S1[:, h % 4, :], GONE).then_inc(rep2_ok, 1)

            def select(pair, b, c):
                h = 4 * c
                dve.wait_ge(rep2_ok, after(pair, 2 * NH, b * NH + h + 4))
                dve.wait_ge(E_ok, after(pair, 8, 4 * b + c + 1))
                v.scalar_tensor_tensor(E_[:, h:h + 4, :], Sb[:, h:h + 4, :], GONE / 2, E_[:, h:h + 4, :],
                                       ALU.is_lt, ALU.mult).then_inc(sel_ok, 1)

            def softmax_sum(pair, b):
                dve.wait_ge(tops_ok, after(pair, 2, b + 1))
                v.tensor_reduce(lc[:, :], tops[:, :, :], AX.X, ALU.add).then_inc(lc_ok, 1)
                dve.wait_ge(lc_ok, after(pair, 2, b + 1))
                if b == 0:
                    dve.wait_ge(P_ok, after(pair - 1, 8))
                else:
                    dve.wait_ge(P_ok, after(pair, 8, 4))
                v.reciprocal(rc[:, :], lc[:, :]).then_inc(rc_ok, 1)

            def experts(i, b):
                def add(n, t_in, t_out):
                    return v.scalar_tensor_tensor(t_out[:, b, :], bank(Y_BANK[b], L, C * n, C * n + C),
                                                  pr[:, b, n:n + 1], t_in[:, b, :], ALU.mult, ALU.add)

                dve.wait_ge(zb_ok, after(i, 2, b + 1))
                add(0, zb, t0).then_inc(t0_ok, 1)
                dve.wait_ge(t0_ok, after(i, 2, b + 1))
                add(1, t0, t1).then_inc(t1_ok, 1)
                dve.wait_ge(t1_ok, after(i, 2, b + 1))
                add(2, t1, t2).then_inc(t2_ok, 1)

            def residual(i):
                dve.wait_ge(t2_ok, after(i, 2))
                dve.wait_ge(pe_thT, after(i, 1))
                v.scalar_tensor_tensor(dl[:, :, :], two(bank(1, L, 0, TP)), 1.0, t2[:, :, :], ALU.add, ALU.mult) \
                    .then_inc(dl_ok, 1)
                dve.wait_ge(dl_ok, after(i, 1))
                dve.wait_ge(z1_ok, after(i - 1, 2))
                dve.wait_ge(x1w_ok, after(i - 1, 1))
                v.tensor_tensor(x1[:, :, :], dl[:, :, :], x0[:, :, :], ALU.add).then_inc(x1_ok, 1)

            def prototypes_max(i):
                dve.wait_ge(pe_S0, after(i, 1))
                v.tensor_reduce(m0[:, :], two(bank(0, L, 0, 2 * LC)), AX.X, ALU.max).then_inc(m0_ok, 1)
                dve.wait_ge(m0_ok, after(i, 1))
                v.tensor_scalar(nm0[:, :], m0[:, :], -SC0, None, ALU.mult).then_inc(nm0_ok, 1)

            def prototypes_sum(i):
                dve.wait_ge(P0_ok, after(i, 2))
                v.reciprocal(r0[:, :], l0[:, :]).then_inc(r0_ok, 1)

            def router_max(i):
                lg = bank(1, L, 0, 2 * NE).rearrange("p (b e) -> p b e", b=2)
                dve.wait_ge(pe_rlt, after(i, 1))
                v.tensor_reduce(rm[:, :], lg, AX.X, ALU.max).then_inc(rm_ok, 1)
                dve.wait_ge(rm_ok, after(i, 1))
                v.tensor_tensor(re[:, :, :], lg, rm[:, :, None].to_broadcast([L, 2, NE]), ALU.subtract) \
                    .then_inc(re_ok, 1)

            def router_norm(i):
                dve.wait_ge(rx_ok, after(i, 1))
                v.tensor_reduce(rs[:, :], rx[:, :, :], AX.X, ALU.add).then_inc(rs_ok, 1)
                dve.wait_ge(rs_ok, after(i, 1))
                v.reciprocal(rr[:, :], rs[:, :]).then_inc(rr_ok, 1)
                dve.wait_ge(rr_ok, after(i, 1))
                v.memset(pr[:, :, NE:NE + 1], 1.0)
                v.tensor_tensor(pr[:, :, 0:NE], rx[:, :, :], rr[:, :, None].to_broadcast([L, 2, NE]), ALU.mult) \
                    .then_inc(pr_ok, 1)

            def window_shift(w, t):
                b, q = t // 2, t % 2
                sc = bank(S1_BANK[t]).rearrange("p (h k) -> p h k", k=WIN)
                dve.wait_ge(pe_S1, after(w, 4, t + 1))
                v.tensor_reduce(m1[:, b, 8 * q:8 * q + 8], sc, AX.X, ALU.max).then_inc(m1_ok, 1)
                dve.wait_ge(m1_ok, after(w, 4, t + 1))
                v.tensor_tensor(d1[:, b, 8 * q:8 * q + 8, :], sc, m1[:, b, 8 * q:8 * q + 8, None]
                                .to_broadcast([L, 8, WIN]), ALU.subtract).then_inc(d1_ok, 1)

            def window_norm(w):
                dve.wait_ge(pe_o1, after(w, 1))
                v.reciprocal(r1[:, :, :], two(bank(5, C, TP, 2 * TP))).then_inc(r1_ok, 1)
                dve.wait_ge(r1_ok, after(w, 1))
                v.tensor_tensor(o1T[:, :, :], two(bank(5, C, 0, TP)), r1[:, :, :], ALU.mult).then_inc(o1T_ok, 1)

            def cross_values(j):
                dve.wait_ge(v_b, after(j, 16))
                dve.wait_ge(pe_o2, after(j - 1, 2))
                v.tensor_copy(diagonal(vbdc, 0, LC, 0, [[4 * 32, 2 * NG], [32 + D, 4], [1, D]]),
                              vcB[:, :, :].rearrange("p b (g j d) -> p (b g) j d", j=4, d=D)) \
                    .then_inc(vbdc_ok, 1)

            def x_after_window(w):
                dve.wait_ge(pe_y1t, after(w, 1))
                dve.wait_ge(x_m, after(w - 1, 16))
                dve.wait_ge(z2_ok, after(w - 1, 2))
                dve.wait_ge(x1w_ok, after(w, 1))
                v.tensor_tensor(xA[:, :, :], two(bank(4, L, 0, TP)), x1w[:, :, :], ALU.add).then_inc(xA_ok, 1)

            def x_after_cross(j):
                dve.wait_ge(x_b, after(j, 16))
                dve.wait_ge(pe_y2t, after(j, 1))
                dve.wait_ge(z3_ok, after(j - 1, 2))
                v.tensor_tensor(x3[:, :, :], two(bank(7, L, 0, TP)), xB[:, :, :], ALU.add).then_inc(x3_ok, 1)

            def x_after_swiglu(j):
                dve.wait_ge(pe_y3t, after(j, 1))
                dve.wait_ge(x4_out, after(j - 1, 32))
                v.tensor_tensor(x4[:, :, :], two(bank(6, L, 0, TP)), x3[:, :, :], ALU.add).then_inc(x4_ok, 1)

            def body(i, live):
                i1, i2, i3 = i - 1, i - 2, i - 3
                if 2 in live:
                    window_shift(i2, 2)
                    window_shift(i2, 3)
                if 3 in live:
                    select(i3, 0, 2)
                    top16(i3, 1, 1)
                if 1 in live:
                    if live == range(2):
                        conditions()
                    router_max(i1)
                if 3 in live:
                    select(i3, 0, 3)
                if 1 in live:
                    router_norm(i1)
                if 3 in live:
                    top16(i3, 1, 2)
                if 2 in live:
                    window_norm(i2)
                if 3 in live:
                    top16(i3, 1, 3)
                if 2 in live:
                    x_after_window(i2)
                if 3 in live:
                    cross_values(i3)
                if 2 in live:
                    stats(xA_ok, st2_ok, mv2_ok, xA, st2, mv2, i2)
                if 3 in live:
                    select(i3, 1, 0)
                    select(i3, 1, 1)
                    softmax_sum(i3, 1)
                if 1 in live:
                    experts(i1, 0)
                if 3 in live:
                    select(i3, 1, 2)
                if 1 in live:
                    experts(i1, 1)
                if 3 in live:
                    select(i3, 1, 3)
                if 1 in live:
                    residual(i1)
                    stats(x1_ok, st1_ok, mv1_ok, x1, st1, mv1, i1)
                if 2 in live:
                    top16(i2, 0, 0)
                if 0 in live:
                    dve.wait_ge(x0_in, after(i, 32))
                    stats(None, st0_ok, mv0_ok, x0, st0, mv0, i)
                if 2 in live:
                    top16(i2, 0, 1)
                if 3 in live:
                    x_after_cross(i3)
                    stats(x3_ok, st3_ok, mv3_ok, x3, st3, mv3, i3)
                if 2 in live:
                    top16(i2, 0, 2)
                    select(i2, 0, 0)
                    top16(i2, 0, 3)
                    select(i2, 0, 1)
                    top16(i2, 1, 0)
                if 0 in live:
                    prototypes_max(i)
                if 1 in live:
                    window_shift(i1, 0)
                if 0 in live:
                    prototypes_sum(i)
                if 2 in live:
                    softmax_sum(i2, 0)
                if 1 in live:
                    window_shift(i1, 1)
                if 3 in live:
                    x_after_swiglu(i3)

            iterations(dve, body)

        @block.scalar
        def _(act):
            a = nc.scalar
            for dst, src in ((Wq0[:, :], I["L0_xcond_Wq"]), (Wk0[:, :], I["L0_xcond_Wk"]),
                             (Wv0[:, :], I["L0_xcond_Wv"])):
                act.dma_start(dst, src).then_inc(w_qkv0, 16)
            for dst, src in ((rb[:, 0:1], I["L0_xcond_router_b"].rearrange("(p o) -> p o", o=1)),
                             (rw[:, :, :], I["L0_xcond_router_W"].rearrange("(k p) n -> p k n", p=C)),
                             (ew1[:, :, :, :], I["L0_xcond_e_w1"].rearrange("e (k p) n -> p e k n", p=C)),
                             (wso[:, :], I["L1_xcond_w_so"]),
                             (wkv[:, :, :], I["L1_xcond_w_kv"].rearrange("p (k n) -> p k n", n=C)),
                             (wq[:, :], I["L1_xcond_w_q"]), (wco[:, :], I["L1_xcond_w_co"]),
                             (wm2[:, :, :], I["L1_xcond_w_m2"].rearrange("(k p) n -> p k n", p=C))):
                act.dma_start(dst, src).then_inc(w_small, 16)
            act.dma_start(mixb[NE:NE + 1, :], I["L0_xcond_out_b"].rearrange("(o c) -> o c", o=1)).then_inc(mixb_in, 16)
            act.wait_ge(su_pe, 2)
            a.mul(ew2o[:, 0:4, :], bank(7).rearrange("p (k n) -> p k n", n=C), 0.5).then_inc(su_act, 1)
            a.mul(ew2o[:, 4:6, :], bank(6, 128, 0, 256).rearrange("p (k n) -> p k n", n=C), 0.5).then_inc(su_act, 1)

            def conditions():
                act.wait_ge(su_dve, 3)
                a.activation(scond[:, :], cols[:, rows["cond"]:rows["cond"] + NB], ACT.Silu).then_inc(su_act, 1)
                a.mul(gb2h[:, :], col("gate_b2"), 0.5).then_inc(su_act, 1)
                act.wait_ge(su_pe, 4)
                a.copy(mixb[0:NE, :], bank(3, NE, 2 * C, 3 * C)).then_inc(su_act, 1)
                act.wait_ge(mixb_in, 16)
                act.wait_ge(su_act, 5)
                act.wait_ge(zero_ok, N_ZERO)
                a.mul(mixh[0:NE + 1, :], mixb[:, :], 0.5).then_inc(su_act, 1)

            def of_mix(name, b):
                return modm[:, MOD[name], b:b + 1]

            def of_window(name, b):
                return modw[:, MOD[name] - NW, b:b + 1]

            def of_back(name, b):
                return modb[:, MOD[name] - NBK, b:b + 1]

            def half(n, b, w=C):
                return bank(n, C, w * b, w * b + w)

            def modulated(n, hT_ok, hT, src, m):
                for b in range(2):
                    a.activation(hT[:, b, :], half(src, b), ACT.Identity, scale=m(f"SC{n}", b), bias=m(f"SH{n}", b)) \
                        .then_inc(hT_ok, 1)

            def gated(n, yT_ok, yT, src, m):
                for b in range(2):
                    a.activation(yT[:, b, :], half(src, b), ACT.Identity, scale=m(f"G{n}", b), bias=m(f"BG{n}", b)) \
                        .then_inc(yT_ok, 1)

            def pcT_copy(j, t):
                b, c = t // 4, t % 4
                act.wait_ge(pe_pcT, after(j, 8, t + 1))
                if b == 0:
                    act.wait_ge(pe_o2, after(j - 1, 2))
                else:
                    act.wait_ge(pe_o2, after(j, 2, 1))
                a.copy(pcT[:, 4 * c:4 * c + 4, :], bank(PCT_BANK[t], LC).rearrange("p (h t) -> p h t", h=4)) \
                    .then_inc(pcT_ok, 1)

            def exps(k, b, c):
                act.wait_ge(sub_ok, after(k, 8, 4 * b + c + 1))
                a.activation(E_[:, 4 * c:4 * c + 4, :], E_[:, 4 * c:4 * c + 4, :], ACT.Exp).then_inc(E_ok, 1)

            def exps_top(k, b):
                act.wait_ge(tsub_ok, after(k, 2, b + 1))
                a.activation(tops[:, :, :], tops[:, :, :], ACT.Exp).then_inc(tops_ok, 1)

            def oc_copy(j, b):
                act.wait_ge(pe_o2, after(j, 2, b + 1))
                a.activation(ocT[:, b, :], bank(OC_BANK[b], C, 0, L), ACT.Identity, bias=col("b_kv", 1)) \
                    .then_inc(ocT_ok, 1)

            def expert_hidden(e, h_ok):
                for c in range(2):
                    for b in range(2):
                        a.activation(hT[:, 2 * e + c, b, :], bank(E_BANK[e], C, TP * c + L * b, TP * c + L * b + L),
                                     ACT.Silu, bias=of_mix(f"EB{2 * e + c}", b)).then_inc(h_ok, 1)

            def p1T_copy(w, t):
                b, q = t // 2, t % 2
                act.wait_ge(pe_p1T, after(w, 4, t + 1))
                a.copy(p1T[:, b, 4 * q:4 * q + 4, :], bank(P1T_BANK[t]).rearrange("p (k t) -> p k t", t=L)) \
                    .then_inc(p1T_ok, 1)

            def z_copy(i, b):
                act.wait_ge(pe_y, after(i, 2, b + 1))
                a.copy(zb[:, b, :], bank(Y_BANK[b], L, NE * C, NE * C + C)).then_inc(zb_ok, 1)

            def silu_a(j, c):
                act.wait_ge(pe_m1, after(j, 4, c + 1))
                a.activation(sa[:, c, :], bank(M1_BANK[c], C, 0, TP), ACT.Silu, bias=col("b_m1", c)) \
                    .then_inc(sa_ok, 1)

            def linear_b(j, c):
                act.wait_ge(pe_m1, after(j, 4, c + 1))
                act.wait_ge(pe_y3, after(j - 1, 1))
                a.activation(u[:, c, :], bank(M1_BANK[c], C, TP, 2 * TP), ACT.Identity, bias=col("b_m1", HID // C + c)) \
                    .then_inc(ub_ok, 1)

            def scores_copy(w, t):
                b, c = t // 4, t % 4
                act.wait_ge(pe_Sc, after(w, 8, t + 1))
                act.wait_ge(rep1_ok, after(w - 1, 2 * NH, b * NH + 4 * c + 4))
                act.wait_ge(sub_ok, after(w - 1, 8, t + 1))
                a.mul(S[:, b, 4 * c:4 * c + 4, :], bank(SC_BANK[t], L, 0, 4 * LC)
                      .rearrange("p (h k) -> p h k", k=LC), SC1).then_inc(S_ok, 1)

            def window_keys(w):
                act.wait_ge(pe_qk1, after(w, 1))
                act.wait_ge(kbd1_in, after(w - 1, 16 * NH))
                a.activation(k1T[:, :, :], two(bank(1, C, TP, 2 * TP)), ACT.Identity, bias=col("b_qkv", 1)) \
                    .then_inc(k1T_ok, 1)

            def window_queries(w):
                act.wait_ge(pe_qk1, after(w, 1))
                act.wait_ge(pe_S1, after(w - 1, 4))
                a.activation(q1T[:, :, :], two(bank(1, C, 0, TP)), ACT.Identity, bias=col("b_qkv", 0)) \
                    .then_inc(q1T_ok, 1)

            def cross_keys(w):
                act.wait_ge(pe_ckv, after(w, 1))
                act.wait_ge(kbdc_in, after(w - 1, 16 * NH))
                a.activation(kcT[:, :, :], two(bank(3, C, 0, 2 * LC)), ACT.Identity, bias=col("b_kv", 0)) \
                    .then_inc(kcT_ok, 1)

            def cross_values(w):
                act.wait_ge(pe_ckv, after(w, 1))
                act.wait_ge(v_m, after(w - 1, 16))
                a.copy(vcA[:, :, :], two(bank(3, LC, 2 * LC, 2 * LC + TP))).then_inc(vcA_ok, 1)

            def window_values(w):
                act.wait_ge(pe_v1, after(w, 1))
                act.wait_ge(pe_o1, after(w - 1, 1))
                for h in range(2):
                    a.copy(diagonal(vbd1, 64 * h, 64, D * h, [[64, 4 * NG], [32 + 2 * D, 2], [1, D]]),
                           bank(5)[64 * h:64 * h + 64, :].rearrange("p (x q c) -> p x q c", q=2, c=2 * D)
                           [:, :, :, D * h:D * h + D]).then_inc(v1_ok, 1)

            def nx_copy(i):
                act.wait_ge(pe_z0, after(i, 1))
                act.wait_ge(pe_g1, after(i - 1, 1))
                a.activation(nxT[:, :, :], two(bank(0, C, 0, TP)), ACT.Identity, scale=lncol[:, 0:1],
                             bias=lncol[:, 1:2]).then_inc(nxT_ok, 1)

            def context_copy(i):
                act.wait_ge(pe_z0, after(i, 1))
                act.wait_ge(pe_ckv, after(i - 1, 1))
                a.copy(cT[:, :, :], two(bank(0, C, TP, TP + 2 * LC))).then_inc(cT_ok, 1)

            def qk0_copy(i):
                act.wait_ge(pe_q0, after(i, 1))
                a.copy(q0T[:, :, :], two(bank(1, C, 0, TP))).then_inc(q0T_ok, 1)
                a.copy(k0T[:, :, :], two(bank(1, C, TP, TP + 2 * LC))).then_inc(k0T_ok, 1)

            def v0_copy(i):
                act.wait_ge(pe_v0, after(i, 1))
                a.copy(v0[:, :, :], two(bank(2, LC, 0, TP))).then_inc(v0_ok, 1)

            def prototypes_exp(i):
                act.wait_ge(nm0_ok, after(i, 1))
                for b in range(2):
                    a.activation(P0[:, b, :], bank(0, L, LC * b, LC * b + LC), ACT.Exp, scale=SC0,
                                 bias=nm0[:, b:b + 1], accum_out=l0[:, b:b + 1]).then_inc(P0_ok, 1)

            def P0T_copy(i):
                act.wait_ge(pe_P0T, after(i, 1))
                a.copy(P0T[:, :, :], two(bank(1, LC, 0, TP))).then_inc(P0T_ok, 1)

            def evidence_copy(i):
                act.wait_ge(pe_ev, after(i, 1))
                a.copy(evT[:, :, :], two(bank(2, C, 0, TP))).then_inc(evT_ok, 1)

            def router_copy(i):
                act.wait_ge(modm_ok, after(i, 1))
                act.wait_ge(pe_rl, after(i, 1))
                for b in range(2):
                    a.activation(rlT[:, b, :], bank(0, NE, L * b, L * b + L), ACT.Identity,
                                 bias=modm[0:NE, MOD["RL"], b:b + 1]).then_inc(rlT_ok, 1)

            def router_exp(i):
                act.wait_ge(re_ok, after(i, 1))
                a.activation(rx[:, :, :], re[:, :, :], ACT.Exp).then_inc(rx_ok, 1)

            def gate_hidden(i):
                act.wait_ge(pe_g1, after(i, 1))
                for b in range(2):
                    a.activation(gs[:, b, :], half(2, b), ACT.Silu, bias=of_mix("GB", b)).then_inc(gs_ok, 1)

            def shares_copy(i):
                act.wait_ge(pe_prT, after(i, 1))
                a.copy(prT[0:NE + 1, :, :], two(bank(1, NE + 1, 0, TP))).then_inc(prT_ok, 1)

            def gate_tanh(i):
                act.wait_ge(pe_g2, after(i, 1))
                a.activation(th[:, :, :], two(bank(0, C, 0, TP)), ACT.Tanh, scale=0.5, bias=gb2h[:, 0:1]) \
                    .then_inc(th_ok, 1)

            def window_exp(w, t):
                b, q = t // 2, t % 2
                act.wait_ge(d1_ok, after(w, 4, t + 1))
                a.activation(d1[:, b, 8 * q:8 * q + 8, :], d1[:, b, 8 * q:8 * q + 8, :], ACT.Exp, scale=SC1) \
                    .then_inc(E1_ok, 1)

            def queries_copy(w):
                act.wait_ge(pe_qc, after(w, 1))
                a.activation(qcT[:, :, :], two(bank(3, C, 0, TP)), ACT.Identity, bias=col("b_q")) \
                    .then_inc(qcT_ok, 1)

            def body(i, live):
                i1, i2, i3 = i - 1, i - 2, i - 3
                if 1 in live:
                    P0T_copy(i1)
                if 2 in live:
                    window_exp(i2, 0)
                    window_exp(i2, 1)
                if 3 in live:
                    exps(i3, 0, 3)
                if 1 in live:
                    evidence_copy(i1)
                if 2 in live:
                    window_exp(i2, 2)
                    p1T_copy(i2, 0)
                    window_exp(i2, 3)
                    p1T_copy(i2, 1)
                    p1T_copy(i2, 2)
                if 1 in live:
                    if live == range(2):
                        conditions()
                    router_copy(i1)
                if 3 in live:
                    pcT_copy(i3, 0)
                if 2 in live:
                    p1T_copy(i2, 3)
                if 3 in live:
                    exps(i3, 1, 0)
                if 1 in live:
                    router_exp(i1)
                if 3 in live:
                    exps(i3, 1, 1)
                if 1 in live:
                    act.wait_ge(pe_e0, after(i1, 1))
                    expert_hidden(0, h0_ok)
                    act.wait_ge(pe_e1, after(i1, 1))
                    expert_hidden(1, h1_ok)
                    act.wait_ge(pe_e2, after(i1, 1))
                    expert_hidden(2, h2_ok)
                if 2 in live:
                    act.wait_ge(modw_ok, after(i2, 1))
                    act.wait_ge(pe_y1, after(i2, 1))
                    gated(1, y1T_ok, y1T, 3, of_window)
                if 1 in live:
                    gate_hidden(i1)
                if 3 in live:
                    pcT_copy(i3, 1)
                if 1 in live:
                    shares_copy(i1)
                if 3 in live:
                    pcT_copy(i3, 2)
                if 1 in live:
                    gate_tanh(i1)
                if 3 in live:
                    exps_top(i3, 1)
                if 1 in live:
                    z_copy(i1, 0)
                if 3 in live:
                    pcT_copy(i3, 3)
                    exps(i3, 1, 2)
                if 1 in live:
                    z_copy(i1, 1)
                if 3 in live:
                    exps(i3, 1, 3)
                    oc_copy(i3, 0)
                if 2 in live:
                    act.wait_ge(modw_ok, after(i2, 1))
                    act.wait_ge(pe_z2, after(i2, 1))
                    modulated(2, h2T_ok, h2T, 5, of_window)
                    queries_copy(i2)
                if 3 in live:
                    pcT_copy(i3, 4)
                    pcT_copy(i3, 5)
                if 2 in live:
                    scores_copy(i2, 0)
                if 3 in live:
                    pcT_copy(i3, 6)
                    pcT_copy(i3, 7)
                if 1 in live:
                    act.wait_ge(pe_z1, after(i1, 1))
                    act.wait_ge(pe_v1, after(i1 - 1, 1))
                    modulated(1, h1T_ok, h1T, 2, of_mix)
                if 2 in live:
                    scores_copy(i2, 1)
                if 3 in live:
                    oc_copy(i3, 1)
                if 2 in live:
                    scores_copy(i2, 2)
                if 1 in live:
                    window_keys(i1)
                if 3 in live:
                    act.wait_ge(modb_ok, after(i3, 1))
                    act.wait_ge(pe_y2, after(i3, 1))
                    gated(2, y2T_ok, y2T, 6, of_back)
                if 2 in live:
                    scores_copy(i2, 3)
                    exps(i2, 0, 0)
                    scores_copy(i2, 4)
                if 1 in live:
                    window_queries(i1)
                if 2 in live:
                    scores_copy(i2, 5)
                    scores_copy(i2, 6)
                    exps(i2, 0, 1)
                if 0 in live:
                    if live == range(1):
                        act.wait_ge(w_ln, 32)
                    nx_copy(i)
                if 2 in live:
                    scores_copy(i2, 7)
                if 0 in live:
                    context_copy(i)
                if 3 in live:
                    act.wait_ge(modb_ok, after(i3, 1))
                    act.wait_ge(pe_z3, after(i3, 1))
                    modulated(3, h3T_ok, h3T, 6, of_back)
                if 1 in live:
                    cross_keys(i1)
                    cross_values(i1)
                if 3 in live:
                    silu_a(i3, 0)
                    linear_b(i3, 0)
                    silu_a(i3, 1)
                    linear_b(i3, 1)
                if 0 in live:
                    qk0_copy(i)
                if 1 in live:
                    window_values(i1)
                if 3 in live:
                    linear_b(i3, 2)
                    silu_a(i3, 2)
                    linear_b(i3, 3)
                    silu_a(i3, 3)
                if 0 in live:
                    prototypes_exp(i)
                if 2 in live:
                    exps_top(i2, 0)
                if 0 in live:
                    v0_copy(i)
                if 3 in live:
                    act.wait_ge(pe_y3, after(i3, 1))
                    gated(3, y3T_ok, y3T, 7, of_back)
                if 2 in live:
                    exps(i2, 0, 2)

            iterations(act, body)

        @block.tensor
        def _(pe):
            t_ = nc.tensor

            def mm(o, l, r, start=True, stop=True):
                return t_.matmul(o, l, r, start=start, stop=stop)

            def back_to(o, x):
                return t_.transpose(o, x, ident[0:x.shape[0], 0:x.shape[0]])

            pe.wait_ge(id_ok, 1)
            pe.wait_ge(w_fold, 32)
            for n in range(NE * 2):
                r = back_to(bank(4 + n // 4, C, C * (n % 4), C * (n % 4) + C), ew2[:, n, :])
            r.then_inc(su_pe, 1)
            pe.wait_ge(su_dve, 2)
            for n in range(NE * 2):
                r = mm(bank(7 - n // 4, C, C * (n % 4), C * (n % 4) + C), ew2T[:, n, :], outw[:, :])
            r.then_inc(su_pe, 1)

            def bias_columns():
                pe.wait_ge(w_rows, 16 * N_ROW_LOADS)
                back_to(bank(3, C, 0, n_rows), rowt[:, :]).then_inc(su_pe, 1)

            def conditions():
                pe.wait_ge(w_small, 16 * N_SMALL)
                pe.wait_ge(w_big, 16 * N_BIG)
                pe.wait_ge(su_dve, 3)
                cond = cols[:, rows["cond"]:rows["cond"] + NB]
                for n in range(NE * 2):
                    mm(bank(5, C, NB * n, NB * n + NB), ew1[:, n // 2, 2, C * (n % 2):C * (n % 2) + C], cond)
                mm(bank(5, C, NB * 6, NB * 7), gw1[:, 2, :], cond)
                mm(bank(5, NE, NB * 7, NB * 8), rw[:, 2, :], cond)
                mm(bank(3, NE, 2 * C, 3 * C), cols[:, rows["e_b2"]:rows["e_b2"] + NE], outw[:, :]).then_inc(su_pe, 1)
                mm(bank(4, C, 511, 512), wso[:, :], col("b_qkv", 2))
                pe.wait_ge(su_act, 3)
                for n in range(9):
                    r = mm(bank(4, C, NB * n, NB * n + NB), wada[:, n, :], scond[:, :])
                r.then_inc(su_pe, 1)
                pe.wait_ge(mods_ok, N_MODS)
                pe.wait_ge(su_act, 6)
                pe.wait_ge(zero_ok, N_ZERO)

            def half(n, b, parts=C, w=L, off=0):
                return bank(n, parts, off + w * b, off + w * b + w)

            def flat(x):
                return x.rearrange("p b t -> p (b t)")

            def turned(n, y, y_ok, pair):
                for b in range(2):
                    pe.wait_ge(y_ok, after(pair, 2, b + 1))
                    r = back_to(half(n, b), y[:, b, :])
                return r

            def probs_T(j, t):
                b, c = t // 4, t % 4
                if t == 0:
                    pe.wait_ge(x4_ok, after(j - 1, 1))
                elif t == 1:
                    pe.wait_ge(y3T_ok, after(j - 1, 2))
                elif t == 5:
                    pe.wait_ge(ocT_ok, after(j, 2, 1))
                else:
                    pe.wait_ge(pcT_ok, after(j, 8, t if t == 4 else t - 1))
                pe.wait_ge(P_ok, after(j, 8, t + 1))
                for n in range(4):
                    r = back_to(bank(PCT_BANK[t], LC, L * n, L * n + L), P[:, b, 4 * c + n, :])
                r.then_inc(pe_pcT, 1)

            def cross_values(j, b):
                if b == 0:
                    pe.wait_ge(vbdc_ok, after(j, 1))
                pe.wait_ge(pcT_ok, after(j, 8, 4 * b + 4))
                for n in range(4):
                    for gq in range(NG):
                        r = mm(ps[32 * gq:32 * gq + 32, 512 * OC_BANK[b]:512 * OC_BANK[b] + L],
                               vbdc[:, b * NG + gq, n, :], pcT[:, 4 * gq + n, :], n == 0, n == 3)
                r.then_inc(pe_o2, 1)

            def expert_in(e):
                for c in range(2):
                    for s, x in enumerate((nxT, evT)):
                        r = mm(bank(E_BANK[e], C, TP * c, TP * c + TP), ew1[:, e, s, C * c:C * c + C], flat(x),
                               s == 0, s == 1)
                return r

            def experts_out(i, b):
                pe.wait_ge(h0_ok, after(i, 4))
                pe.wait_ge(h1_ok, after(i, 4))
                pe.wait_ge(h2_ok, after(i, 4))
                pe.wait_ge(prT_ok, after(i, 1))
                if b == 0:
                    pe.wait_ge(gs_ok, after(i, 2))
                else:
                    pe.wait_ge(th_ok, after(i, 1))
                for e in range(NE):
                    for c in range(2):
                        mm(bank(Y_BANK[b], L, C * e, C * e + C), hT[:, 2 * e + c, b, :], ew2o[:, 2 * e + c, :],
                           c == 0, c == 1)
                mm(bank(Y_BANK[b], L, C * NE, C * NE + C), prT[:, b, :], mixh[:, :]).then_inc(pe_y, 1)

            def window_scores(w, t):
                pe.wait_ge(q1T_ok, after(w, 1))
                pe.wait_ge(kbd1_in, after(w, 16 * NH))
                b, q = t // 2, t % 2
                if t == 0:
                    pe.wait_ge(vcA_ok, after(w, 1))
                elif t == 1:
                    pe.wait_ge(S_ok, after(w - 1, 8, 7))
                elif t == 2:
                    pe.wait_ge(v1_ok, after(w, 2))
                elif t == 3:
                    pe.wait_ge(d1_ok, after(w, 4, 1))
                for h in range(2):
                    n = S1_BANK[t]
                    r = mm(ps[64 * h:64 * h + 64, 512 * n:512 * n + 512], q1T[:, b, WIN * h:WIN * h + WIN],
                           kbd1[:, b, 8 * q:8 * q + 8, WIN * h:WIN * h + WIN])
                r.then_inc(pe_S1, 1)

            def window_T(w, t):
                b, q = t // 2, t % 2
                if t < 3:
                    pe.wait_ge(d1_ok, after(w, 4, t + 2))
                else:
                    pe.wait_ge(p1T_ok, after(w, 4, 1))
                pe.wait_ge(E1_ok, after(w, 4, t + 1))
                for n in range(4):
                    h = 8 * q + 2 * n
                    r = back_to(bank(P1T_BANK[t], 128, L * n, L * n + L),
                                d1[:, b, h:h + 2, :].rearrange("p h k -> p (h k)"))
                r.then_inc(pe_p1T, 1)

            def window_values(w):
                pe.wait_ge(v1_ok, after(w, 2))
                pe.wait_ge(p1T_ok, after(w, 4))
                for off in (0, TP):
                    for b in range(2):
                        for h in range(2):
                            for q in range(2):
                                for gq in range(NG):
                                    o = 512 * 5 + off + L * b + WIN * h
                                    lhsT = ones1[:, q, :] if off else vbd1[:, (2 * b + h) * NG + gq, q, :]
                                    r = mm(ps[32 * gq:32 * gq + 32, o:o + WIN], lhsT,
                                           p1T[:, b, 2 * gq + q, WIN * h:WIN * h + WIN], q == 0, q == 1)
                r.then_inc(pe_o1, 1)

            def swiglu_in(c):
                n = M1_BANK[c]
                mm(bank(n, C, 0, TP), wm1[:, C * c:C * c + C], flat(h3T))
                mm(bank(n, C, TP, 2 * TP), wm1[:, HID + C * c:HID + C * c + C], flat(h3T)).then_inc(pe_m1, 1)

            def cross_scores(w, t):
                b, c = t // 4, t % 4
                if t == 0:
                    pe.wait_ge(xA_ok, after(w, 1))
                elif t == 1:
                    pe.wait_ge(h2T_ok, after(w, 2))
                elif t > 2:
                    pe.wait_ge(S_ok, after(w, 8, t - 2))
                if t == 0:
                    pe.wait_ge(kbdc_in, after(w, 16 * NH))
                    pe.wait_ge(qcT_ok, after(w, 1))
                mm(bank(SC_BANK[t], L, 0, 4 * LC), qcT[:, b, :], kbdc[:, b, 4 * c:4 * c + 4, :]
                   .rearrange("p h k -> p (h k)")).then_inc(pe_Sc, 1)

            def window_qk(w):
                pe.wait_ge(dl_ok, after(w, 1))
                pe.wait_ge(h1T_ok, after(w, 2))
                mm(bank(1, C, 0, TP), wqkv[:, 0, :], flat(h1T))
                mm(bank(1, C, TP, 2 * TP), wqkv[:, 1, :], flat(h1T)).then_inc(pe_qk1, 1)

            def cross_kv(w):
                pe.wait_ge(S_ok, after(w - 1, 8, 6))
                pe.wait_ge(cT_ok, after(w, 1))
                mm(bank(3, C, 0, 2 * LC), wkv[:, 0, :], flat(cT))
                for b in range(2):
                    r = mm(half(3, b, LC, C, 2 * LC), cT[:, b, :], wkv[:, 1, :])
                r.then_inc(pe_ckv, 1)

            def window_v(w):
                pe.wait_ge(S_ok, after(w - 1, 8))
                pe.wait_ge(h1T_ok, after(w, 2))
                for b in range(2):
                    for q in range(2):
                        for h in range(2):
                            o = 512 * 5 + C * (2 * b + q)
                            r = mm(ps[64 * h:64 * h + 64, o:o + C], h1T[:, b, WIN * q:WIN * q + WIN], wqkv[:, 2, :])
                r.then_inc(pe_v1, 1)

            def inputs_T(i):
                pe.wait_ge(t2_ok, after(i - 1, 2))
                pe.wait_ge(c0_in, after(i, 16))
                for b in range(2):
                    back_to(half(0, b, C, LC, TP), c0[:, b, :])
                turned(0, z0, z0_ok, i).then_inc(pe_z0, 1)

            def prototypes_qk(i):
                pe.wait_ge(k1T_ok, after(i - 1, 1))
                pe.wait_ge(q1T_ok, after(i - 1, 1))
                pe.wait_ge(nxT_ok, after(i, 1))
                mm(bank(1, C, 0, TP), Wq0[:, :], flat(nxT))
                pe.wait_ge(cT_ok, after(i, 1))
                mm(bank(1, C, TP, TP + 2 * LC), Wk0[:, :], flat(cT)).then_inc(pe_q0, 1)

            def prototypes_v(i):
                pe.wait_ge(h1T_ok, after(i - 1, 2))
                pe.wait_ge(cT_ok, after(i, 1))
                for b in range(2):
                    r = mm(half(2, b, LC), cT[:, b, :], Wv0[:, :])
                r.then_inc(pe_v0, 1)

            def prototypes_scores(i):
                pe.wait_ge(cT_ok, after(i, 1))
                pe.wait_ge(nxT_ok, after(i, 1))
                pe.wait_ge(k0T_ok, after(i, 1))
                for b in range(2):
                    r = mm(half(0, b, L, LC), q0T[:, b, :], k0T[:, b, :])
                r.then_inc(pe_S0, 1)

            def prototypes_T(i):
                pe.wait_ge(P0n_ok, after(i, 1))
                for b in range(2):
                    r = back_to(half(1, b, LC), P0n[:, b, :])
                r.then_inc(pe_P0T, 1)

            def evidence(i):
                pe.wait_ge(v0_ok, after(i, 1))
                pe.wait_ge(P0T_ok, after(i, 1))
                for b in range(2):
                    r = mm(half(2, b), v0[:, b, :], P0T[:, b, :])
                r.then_inc(pe_ev, 1)

            def router(i):
                pe.wait_ge(P0_ok, after(i, 2))
                mm(bank(0, NE, 0, TP), rw[:, 0, :], flat(nxT), True, False)
                pe.wait_ge(evT_ok, after(i, 1))
                mm(bank(0, NE, 0, TP), rw[:, 1, :], flat(evT), False, True).then_inc(pe_rl, 1)

            def router_T(i):
                pe.wait_ge(P0T_ok, after(i, 1))
                for b in range(2):
                    pe.wait_ge(rlT_ok, after(i, 2, b + 1))
                    pe.sem_inc(passed, 1)
                    r = back_to(half(1, b, L, NE), rlT[:, b, :])
                r.then_inc(pe_rlt, 1)

            def gate_in(i):
                pe.wait_ge(h0_ok, after(i, 4))
                for s, x in enumerate((nxT, evT)):
                    r = mm(bank(2, C, 0, TP), gw1[:, s, :], flat(x), s == 0, s == 1)
                r.then_inc(pe_g1, 1)

            def shares_T(i):
                pe.wait_ge(h2_ok, after(i, 4))
                pe.wait_ge(pr_ok, after(i, 1))
                for b in range(2):
                    r = back_to(half(1, b, NE + 1), pr[:, b, :])
                r.then_inc(pe_prT, 1)

            def gate_out(i):
                pe.wait_ge(h1_ok, after(i, 4))
                pe.wait_ge(gs_ok, after(i, 2))
                mm(bank(0, C, 0, TP), gw2[:, :], flat(gs)).then_inc(pe_g2, 1)

            def gate_T(i):
                pe.wait_ge(th_ok, after(i, 1))
                for b in range(2):
                    r = back_to(half(1, b, L, C), th[:, b, :])
                r.then_inc(pe_thT, 1)

            def body(i, live):
                i1, i2, i3 = i - 1, i - 2, i - 3
                if 2 in live:
                    window_scores(i2, 3)
                if 1 in live:
                    evidence(i1)
                if 2 in live:
                    window_T(i2, 0)
                if 3 in live:
                    probs_T(i3, 0)
                if 2 in live:
                    window_T(i2, 1)
                if 1 in live:
                    if live == range(2):
                        conditions()
                    router(i1)
                if 2 in live:
                    window_T(i2, 2)
                    window_T(i2, 3)
                if 1 in live:
                    pe.wait_ge(evT_ok, after(i1, 1))
                    expert_in(0).then_inc(pe_e0, 1)
                    router_T(i1)
                if 2 in live:
                    window_values(i2)
                if 1 in live:
                    pe.wait_ge(rlT_ok, after(i1, 2))
                    expert_in(1).then_inc(pe_e1, 1)
                    pe.wait_ge(re_ok, after(i1, 1))
                    expert_in(2).then_inc(pe_e2, 1)
                    gate_in(i1)
                if 2 in live:
                    pe.wait_ge(o1T_ok, after(i2, 1))
                    mm(bank(3, C, 0, TP), wso[:, :], flat(o1T)).then_inc(pe_y1, 1)
                if 3 in live:
                    probs_T(i3, 1)
                    probs_T(i3, 2)
                if 1 in live:
                    shares_T(i1)
                if 2 in live:
                    turned(4, y1T, y1T_ok, i2).then_inc(pe_y1t, 1)
                if 1 in live:
                    gate_out(i1)
                if 3 in live:
                    probs_T(i3, 3)
                if 1 in live:
                    experts_out(i1, 0)
                    experts_out(i1, 1)
                if 3 in live:
                    cross_values(i3, 0)
                if 2 in live:
                    pe.wait_ge(o1T_ok, after(i2, 1))
                    turned(5, z2, z2_ok, i2).then_inc(pe_z2, 1)
                if 1 in live:
                    gate_T(i1)
                if 3 in live:
                    probs_T(i3, 4)
                if 2 in live:
                    pe.wait_ge(y1T_ok, after(i2, 2))
                    pe.wait_ge(h2T_ok, after(i2, 2))
                    mm(bank(3, C, 0, TP), wq[:, :], flat(h2T)).then_inc(pe_qc, 1)
                if 3 in live:
                    probs_T(i3, 5)
                if 2 in live:
                    cross_scores(i2, 0)
                if 3 in live:
                    probs_T(i3, 6)
                if 2 in live:
                    cross_scores(i2, 1)
                if 3 in live:
                    probs_T(i3, 7)
                if 2 in live:
                    cross_scores(i2, 2)
                if 1 in live:
                    pe.wait_ge(t2_ok, after(i1, 2, 1))
                    turned(2, z1, z1_ok, i1).then_inc(pe_z1, 1)
                if 3 in live:
                    cross_values(i3, 1)
                if 1 in live:
                    window_qk(i1)
                if 3 in live:
                    pe.wait_ge(ocT_ok, after(i3, 2))
                    pe.wait_ge(pcT_ok, after(i3, 8))
                    mm(bank(6, C, 0, TP), wco[:, :], flat(ocT)).then_inc(pe_y2, 1)
                if 2 in live:
                    cross_scores(i2, 3)
                    cross_scores(i2, 4)
                if 3 in live:
                    turned(7, y2T, y2T_ok, i3).then_inc(pe_y2t, 1)
                if 2 in live:
                    cross_scores(i2, 5)
                    cross_scores(i2, 6)
                if 0 in live:
                    inputs_T(i)
                if 2 in live:
                    cross_scores(i2, 7)
                if 1 in live:
                    cross_kv(i1)
                if 3 in live:
                    pe.wait_ge(y2T_ok, after(i3, 2))
                    turned(6, z3, z3_ok, i3).then_inc(pe_z3, 1)
                if 1 in live:
                    window_v(i1)
                if 0 in live:
                    if live == range(1):
                        pe.wait_ge(w_qkv0, 48)
                    prototypes_qk(i)
                if 3 in live:
                    pe.wait_ge(x3_ok, after(i3, 1))
                    pe.wait_ge(h3T_ok, after(i3, 2))
                    swiglu_in(0)
                    pe.wait_ge(h3T_ok, after(i3, 2))
                    swiglu_in(1)
                if 0 in live:
                    prototypes_v(i)
                if 3 in live:
                    pe.wait_ge(sa_ok, after(i3, 4, 1))
                    pe.wait_ge(ub_ok, after(i3, 4, 1))
                    swiglu_in(2)
                    pe.wait_ge(sa_ok, after(i3, 4, 2))
                    pe.wait_ge(ub_ok, after(i3, 4, 2))
                    swiglu_in(3)
                if 0 in live:
                    prototypes_scores(i)
                if 1 in live:
                    window_scores(i1, 0)
                    window_scores(i1, 1)
                if 3 in live:
                    pe.wait_ge(u_ok, after(i3, 4))
                    for c in range(HID // C):
                        r = mm(bank(7, C, 0, TP), wm2[:, c, :], u[:, c, :], c == 0, c == HID // C - 1)
                    r.then_inc(pe_y3, 1)
                if 1 in live:
                    window_scores(i1, 2)
                if 0 in live:
                    if live == range(1):
                        bias_columns()
                    prototypes_T(i)
                if 3 in live:
                    turned(6, y3T, y3T_ok, i3).then_inc(pe_y3t, 1)

            iterations(pe, body)


def kernel(**inputs):
    import numpy as _np
    import concourse.bacc as _bacc
    from concourse import mybir as _mybir
    from concourse.bass_utils import run_bass_kernel_spmd as _run

    nc = _bacc.Bacc("TRN2", target_bir_lowering=False, num_devices=1)
    arrays, aps = {}, {}
    for name, value in inputs.items():
        a = _np.ascontiguousarray(value)
        arrays[f"in_{name}"] = a
        aps[name] = nc.dram_tensor(f"in_{name}", a.shape, _mybir.dt.from_np(a.dtype), kind="ExternalInput").ap()
    shape = inputs["x"].shape
    out = nc.dram_tensor("out_0", shape, _mybir.dt.float32, kind="ExternalOutput").ap()
    pixart_layers_kernel(nc, aps, out)
    r = _run(nc, [arrays], core_ids=[0])
    return r.results[0]["out_0"]
```
